# Optimizing a Trainium2 kernel written in Bass

```python
import numpy as np
import jax
import jax.numpy as jnp

def _softmax(x, axis=-1):
    return jax.nn.softmax(x, axis=axis)

def _gelu(x):
    return jax.nn.gelu(x, approximate=True)

def _silu(x):
    return jax.nn.silu(x)

def _sigmoid(x):
    return jax.nn.sigmoid(x)

def _layernorm(x, axis=-1, eps=1e-05):
    m = jnp.mean(x, axis=axis, keepdims=True)
    v = jnp.var(x, axis=axis, keepdims=True)
    return (x - m) / jnp.sqrt(v + eps)

def _scatter_add(tgt, idx, src, axis=0):
    return tgt.at[idx].add(src)

def _segment_sum(src, seg, n):
    return jax.ops.segment_sum(src, seg, n)
kernel_name = 'mk_gnn_resnorm_d4_gnn_r32_22ccdc'

def setup_inputs(seed: int=0):
    np.random.seed(seed)
    _w = jnp.asarray

    def _rec_inputs():
        import jax
        import jax.numpy as jnp
        _gk = jax.random.key(seed)
        x = -0.0002928 + 1 * jax.random.normal(jax.random.fold_in(_gk, 1), (512, 256), jnp.float32)
        _s = jax.random.randint(jax.random.fold_in(_gk, 2), (4096,), 0, 512, jnp.int32)
        _d = jax.random.randint(jax.random.fold_in(_gk, 3), (4096,), 0, 512, jnp.int32)
        _loop = jnp.arange(512, dtype=jnp.int32)
        src = jnp.concatenate([_s, _d, _loop])
        dst = jnp.concatenate([_d, _s, _loop])
        _o = jnp.argsort(dst, stable=True)
        src = src[_o]
        dst = dst[_o]
        edge_type_8 = jax.random.randint(jax.random.fold_in(_gk, 13), (8704,), 0, 8, jnp.int32)
        edge_weight = jax.random.uniform(jax.random.fold_in(_gk, 14), (8704,), jnp.float32, 0.0, 1)
        node_type_4 = jax.random.randint(jax.random.fold_in(_gk, 15), (512,), 0, 4, jnp.int32)
        return (x, src, dst, edge_type_8, edge_weight, node_type_4)
    x, src, dst, edge_type_8, edge_weight, node_type_4 = _rec_inputs()

    def _L0_gnn_setup():
        import jax, jax.numpy as jnp
        import numpy as np
        N_NODES = 512
        N_EDGES = 8192
        D_IN = 256
        D_OUT = 256
        key = jax.random.key(seed)
        k1, k2, k3, k4 = jax.random.split(key, 4)
        x = jax.random.normal(k1, (N_NODES, D_IN), dtype=jnp.float32)
        edge_index = jax.random.randint(k2, (2, N_EDGES), 0, N_NODES, dtype=jnp.int64)
        limit = float(np.sqrt(6.0 / (D_IN + D_OUT)))
        W = jax.random.uniform(k3, (D_OUT, D_IN), minval=-limit, maxval=limit, dtype=jnp.float32)
        B = jax.random.normal(k4, (D_OUT, D_IN), dtype=jnp.float32) * 0.02
        return {'x': x, 'edge_index': edge_index, 'W': W, 'B': B}
    _L0_gnn_all = _L0_gnn_setup()
    _L0_gnn_in = {k: v for k, v in _L0_gnn_all.items() if k in ('W', 'B')}
    del _L0_gnn_all

    def _L1_gnn_setup():
        import jax, jax.numpy as jnp
        import numpy as np
        N_NODES = 50000
        N_EDGES = 25000
        F_IN = 256
        F_OUT = 64
        HEADS = 4
        LEAKY_ALPHA = 0.2
        key = jax.random.key(seed)
        ks = jax.random.split(key, 8)
        x = jax.random.normal(ks[0], (N_NODES, F_IN), dtype=jnp.float32)
        W = jax.random.normal(ks[1], (HEADS, F_IN, F_OUT), dtype=jnp.float32) * 0.05
        a_self = jax.random.normal(ks[2], (HEADS, F_OUT), dtype=jnp.float32) * 0.05
        a_neigh = jax.random.normal(ks[3], (HEADS, F_OUT), dtype=jnp.float32) * 0.05
        bias = jnp.zeros((HEADS, F_OUT), dtype=jnp.float32)
        adj_val = jnp.ones((N_EDGES,), dtype=jnp.float32)
        edge_row = jax.random.randint(ks[4], (N_EDGES,), 0, N_NODES, dtype=jnp.int32)
        edge_col = jax.random.randint(ks[5], (N_EDGES,), 0, N_NODES, dtype=jnp.int32)
        return {'x': x, 'W': W, 'a_self': a_self, 'a_neigh': a_neigh, 'bias': bias, 'adj_val': adj_val, 'edge_row': edge_row, 'edge_col': edge_col}
    _L1_gnn_all = _L1_gnn_setup()
    _L1_gnn_in = {k: v for k, v in _L1_gnn_all.items() if k in ('W', 'a_self', 'a_neigh', 'bias')}
    del _L1_gnn_all

    def _L2_gnn_setup():
        import jax, jax.numpy as jnp
        import numpy as np
        ALPHA = 0.2
        N_NODES = 3125
        N_EDGES = 50000
        NFEAT = 256
        HID = 64
        NHEADS = 4

        def _gat_head(x, src, dst, Wh, ah, n_nodes):
            hid = Wh.shape[1]
            h = x @ Wh
            h = jnp.where(jnp.isnan(h), 0.0, h)
            a1, a2 = (ah[0, :hid], ah[0, hid:])
            alpha_src = h @ a1
            alpha_dst = h @ a2
            s = alpha_src[src] + alpha_dst[dst]
            e = jnp.exp(-jax.nn.leaky_relu(s, ALPHA))
            e = jnp.where(jnp.isnan(e), 0.0, e)
            rowsum = jax.ops.segment_sum(e, src, num_segments=n_nodes)
            hp = jax.ops.segment_sum(e[:, None] * h[dst], src, num_segments=n_nodes)
            hp = jnp.where(jnp.isnan(hp), 0.0, hp)
            hp = hp / rowsum[:, None]
            hp = jnp.where(jnp.isnan(hp), 0.0, hp)
            return jax.nn.elu(hp)
        key = jax.random.key(seed)
        k1, k2, k3, k4 = jax.random.split(key, 4)
        x = jax.random.normal(k1, (N_NODES, NFEAT), dtype=jnp.float32)
        edge_index = jax.random.randint(k2, (2, N_EDGES), 0, N_NODES, dtype=jnp.int64)
        W = jax.random.normal(k3, (NHEADS, NFEAT, HID), dtype=jnp.float32) * (1.414 * np.sqrt(2.0 / (NFEAT + HID)))
        a = jax.random.normal(k4, (NHEADS, 1, 2 * HID), dtype=jnp.float32) * (1.414 * np.sqrt(2.0 / (1 + 2 * HID)))
        return {'x': x, 'edge_index': edge_index, 'W': W, 'a': a}
    _L2_gnn_all = _L2_gnn_setup()
    _L2_gnn_in = {k: v for k, v in _L2_gnn_all.items() if k in ('W', 'a')}
    del _L2_gnn_all

    def _L3_gnn_setup():
        import jax, jax.numpy as jnp
        import numpy as np
        N_NODES = 625
        N_EDGES = 10000
        IN_DIM = 256
        OUT_DIM = 256
        N_HEADS = 4
        D_K = OUT_DIM // N_HEADS
        N_NTYPES = 4
        N_RELS = 8
        SQRT_DK = float(np.sqrt(D_K))

        def _typed_matmul(x, W, node_type):
            all_t = jnp.einsum('ni,tio->tno', x, W)
            return all_t[node_type, jnp.arange(x.shape[0])]
        key = jax.random.key(seed)
        ks = jax.random.split(key, 12)
        xav = lambda k, shape, fan: jax.random.normal(k, shape, jnp.float32) * (1.0 / np.sqrt(fan))
        return {'h': jax.random.normal(ks[0], (N_NODES, IN_DIM), jnp.float32), 'k_linears': xav(ks[1], (N_NTYPES, IN_DIM, OUT_DIM), IN_DIM), 'q_linears': xav(ks[2], (N_NTYPES, IN_DIM, OUT_DIM), IN_DIM), 'v_linears': xav(ks[3], (N_NTYPES, IN_DIM, OUT_DIM), IN_DIM), 'a_linears': xav(ks[4], (N_NTYPES, OUT_DIM, OUT_DIM), OUT_DIM), 'relation_att': xav(ks[5], (N_RELS, N_HEADS, D_K, D_K), D_K), 'relation_msg': xav(ks[6], (N_RELS, N_HEADS, D_K, D_K), D_K), 'relation_pri': jnp.ones((N_RELS, N_HEADS), jnp.float32), 'skip': jnp.ones((N_NTYPES,), jnp.float32), 'node_type': jax.random.randint(ks[7], (N_NODES,), 0, N_NTYPES), 'etype': jnp.sort(jax.random.randint(ks[8], (N_EDGES,), 0, N_RELS)), 'row_idx': jax.random.randint(ks[9], (N_EDGES,), 0, N_NODES), 'col_idx': jax.random.randint(ks[10], (N_EDGES,), 0, N_NODES)}
    _L3_gnn_all = _L3_gnn_setup()
    _L3_gnn_in = {k: v for k, v in _L3_gnn_all.items() if k in ('k_linears', 'q_linears', 'v_linears', 'a_linears', 'relation_att', 'relation_msg', 'relation_pri', 'skip')}
    del _L3_gnn_all
    return {'x': x, 'src': src, 'dst': dst, 'edge_type_8': edge_type_8, 'edge_weight': edge_weight, 'node_type_4': node_type_4, 'L0_gnn_W': _L0_gnn_in['W'], 'L0_gnn_B': _L0_gnn_in['B'], 'L1_gnn_W': _L1_gnn_in['W'], 'L1_gnn_a_self': _L1_gnn_in['a_self'], 'L1_gnn_a_neigh': _L1_gnn_in['a_neigh'], 'L1_gnn_bias': _L1_gnn_in['bias'], 'L2_gnn_W': _L2_gnn_in['W'], 'L2_gnn_a': _L2_gnn_in['a'], 'L3_gnn_k_linears': _L3_gnn_in['k_linears'], 'L3_gnn_q_linears': _L3_gnn_in['q_linears'], 'L3_gnn_v_linears': _L3_gnn_in['v_linears'], 'L3_gnn_a_linears': _L3_gnn_in['a_linears'], 'L3_gnn_relation_att': _L3_gnn_in['relation_att'], 'L3_gnn_relation_msg': _L3_gnn_in['relation_msg'], 'L3_gnn_relation_pri': _L3_gnn_in['relation_pri'], 'L3_gnn_skip': _L3_gnn_in['skip']}

def reference(x, src, dst, edge_type_8, edge_weight, node_type_4, L0_gnn_W, L0_gnn_B, L1_gnn_W, L1_gnn_a_self, L1_gnn_a_neigh, L1_gnn_bias, L2_gnn_W, L2_gnn_a, L3_gnn_k_linears, L3_gnn_q_linears, L3_gnn_v_linears, L3_gnn_a_linears, L3_gnn_relation_att, L3_gnn_relation_msg, L3_gnn_relation_pri, L3_gnn_skip):
    import jax
    import jax.numpy as jnp

    def _L0_gnn_ref(x, edge_index, W, B):
        import jax, jax.numpy as jnp
        import numpy as np
        N_NODES = 512
        N_EDGES = 8192
        D_IN = 256
        D_OUT = 256
        N = x.shape[0]
        src = edge_index[0]
        dst = edge_index[1]
        A = jnp.zeros((N, N), dtype=x.dtype).at[dst, src].set(1.0)
        deg = jnp.bincount(dst, length=N).astype(x.dtype)
        inv_deg = 1.0 / jnp.where(deg == 0, 1.0, deg)
        propagated = inv_deg[:, None] * (A @ x)
        return propagated @ W.T + x @ B.T

    def _L1_gnn_ref(x, W, a_self, a_neigh, bias, adj_val, edge_row, edge_col):
        import jax, jax.numpy as jnp
        import numpy as np
        N_NODES = 50000
        N_EDGES = 25000
        F_IN = 256
        F_OUT = 64
        HEADS = 4
        LEAKY_ALPHA = 0.2
        N = x.shape[0]
        feats = jnp.einsum('nf,hfo->hno', x, W)
        s_self = jnp.einsum('hno,ho->hn', feats, a_self)
        s_neigh = jnp.einsum('hno,ho->hn', feats, a_neigh)
        z = s_self[:, edge_row] + s_neigh[:, edge_col]
        e = jnp.where(z > 0, z, LEAKY_ALPHA * z) * adj_val[None, :]

        def seg_softmax(e_h):
            m = jax.ops.segment_max(e_h, edge_row, num_segments=N)
            ex = jnp.exp(e_h - m[edge_row])
            s = jax.ops.segment_sum(ex, edge_row, num_segments=N)
            return ex / s[edge_row]
        alpha = jax.vmap(seg_softmax)(e)

        def aggregate(alpha_h, feat_h):
            return jax.ops.segment_sum(alpha_h[:, None] * feat_h[edge_col], edge_row, num_segments=N)
        out = jax.vmap(aggregate)(alpha, feats) + bias[:, None, :]
        out = jnp.transpose(out, (1, 0, 2)).reshape(N, -1)
        return jax.nn.relu(out)

    def _L2_gnn_ref(x, edge_index, W, a):
        import jax, jax.numpy as jnp
        import numpy as np
        ALPHA = 0.2
        N_NODES = 3125
        N_EDGES = 50000
        NFEAT = 256
        HID = 64
        NHEADS = 4

        def _gat_head(x, src, dst, Wh, ah, n_nodes):
            hid = Wh.shape[1]
            h = x @ Wh
            h = jnp.where(jnp.isnan(h), 0.0, h)
            a1, a2 = (ah[0, :hid], ah[0, hid:])
            alpha_src = h @ a1
            alpha_dst = h @ a2
            s = alpha_src[src] + alpha_dst[dst]
            e = jnp.exp(-jax.nn.leaky_relu(s, ALPHA))
            e = jnp.where(jnp.isnan(e), 0.0, e)
            rowsum = jax.ops.segment_sum(e, src, num_segments=n_nodes)
            hp = jax.ops.segment_sum(e[:, None] * h[dst], src, num_segments=n_nodes)
            hp = jnp.where(jnp.isnan(hp), 0.0, hp)
            hp = hp / rowsum[:, None]
            hp = jnp.where(jnp.isnan(hp), 0.0, hp)
            return jax.nn.elu(hp)
        n_nodes = x.shape[0]
        src, dst = (edge_index[0], edge_index[1])
        outs = [_gat_head(x, src, dst, W[h], a[h], n_nodes) for h in range(W.shape[0])]
        out = jnp.concatenate(outs, axis=1)
        return jax.nn.elu(out)

    def _L3_gnn_ref(h, k_linears, q_linears, v_linears, a_linears, relation_att, relation_msg, relation_pri, skip, node_type, etype, row_idx, col_idx):
        import jax, jax.numpy as jnp
        import numpy as np
        N_NODES = 625
        N_EDGES = 10000
        IN_DIM = 256
        OUT_DIM = 256
        N_HEADS = 4
        D_K = OUT_DIM // N_HEADS
        N_NTYPES = 4
        N_RELS = 8
        SQRT_DK = float(np.sqrt(D_K))

        def _typed_matmul(x, W, node_type):
            all_t = jnp.einsum('ni,tio->tno', x, W)
            return all_t[node_type, jnp.arange(x.shape[0])]
        n = h.shape[0]
        k = _typed_matmul(h, k_linears, node_type).reshape(n, N_HEADS, D_K)
        q = _typed_matmul(h, q_linears, node_type).reshape(n, N_HEADS, D_K)
        v = _typed_matmul(h, v_linears, node_type).reshape(n, N_HEADS, D_K)
        q_att = jnp.einsum('nhd,rhde->rnhe', q, relation_att)
        v_msg = jnp.einsum('nhd,rhde->rnhe', v, relation_msg)
        aw_q_edge = q_att[etype, col_idx]
        msg_edge = v_msg[etype, row_idx]
        attn_score = jnp.sum(aw_q_edge * k[row_idx], axis=-1)
        score = attn_score * (relation_pri[etype] / SQRT_DK)
        m = jax.ops.segment_max(score, col_idx, num_segments=n)
        ex = jnp.exp(score - m[col_idx])
        denom = jax.ops.segment_sum(ex, col_idx, num_segments=n)
        alpha = ex / denom[col_idx]
        agg = jax.ops.segment_sum(alpha[..., None] * msg_edge, col_idx, num_segments=n)
        agg = agg.reshape(n, OUT_DIM)
        out = _typed_matmul(agg, a_linears, node_type)
        out = jax.nn.sigmoid(skip)[node_type][:, None] * out
        return out
    edge_index = jnp.stack([src, dst])
    x = _layernorm(x + _L0_gnn_ref(x, edge_index, L0_gnn_W, L0_gnn_B), axis=-1)
    x = _layernorm(x + _L1_gnn_ref(x, L1_gnn_W, L1_gnn_a_self, L1_gnn_a_neigh, L1_gnn_bias, edge_weight, src, dst), axis=-1)
    x = _layernorm(x + _L2_gnn_ref(x, edge_index, L2_gnn_W, L2_gnn_a), axis=-1)
    x = _layernorm(x + _L3_gnn_ref(x, L3_gnn_k_linears, L3_gnn_q_linears, L3_gnn_v_linears, L3_gnn_a_linears, L3_gnn_relation_att, L3_gnn_relation_msg, L3_gnn_relation_pri, L3_gnn_skip, node_type_4, edge_type_8, src, dst), axis=-1)
    return x

_drawn_inputs = setup_inputs


def setup_inputs(seed=0):
    import zlib

    import numpy as np

    out = dict(_drawn_inputs(seed))
    spreads = {'L1_gnn_bias': (0.0, 0.1), 'L3_gnn_relation_pri': (1.0, 0.2), 'L3_gnn_skip': (1.0, 0.6)}
    factors = {'edge_weight': 3.443, 'L1_gnn_a_self': 4.403}
    for name, (base, spread) in spreads.items():
        noise = np.random.default_rng([zlib.crc32(name.encode()), seed]).standard_normal(out[name].shape)
        drawn = base * np.exp(spread * noise) if base else spread * noise
        out[name] = jnp.asarray(drawn.astype(out[name].dtype))
    for name, factor in factors.items():
        out[name] = (out[name] * factor).astype(out[name].dtype)
    return out
```

```python
import concourse.bass as bass
from concourse import mybir
from contextlib import ExitStack

N = 512
E = 8704
D = 256
H = 4
DK = D // H
RELS = 8
TYPES = 4
P = 128
NB = N // P
KC = D // P
EC = E // P
TILES = EC + NB
W1 = 4 + D
W3 = 2 * D
BANK = 512
UN = 8
HALF = UN // 2
BIG = 2.0 ** 100
EPS = 1e-5
EARLY = 24


def gnn_kernel(nc, x_in, src_in, dst_in, etype_in, ew_in, ntype_in, w0_in, b0_in, w1_in, aself_in, aneigh_in,
               bias1_in, w2_in, a2_in, klin_in, qlin_in, vlin_in, alin_in, att_in, msg_in, pri_in, skip_in, out):
    f32, bf16, f16 = mybir.dt.float32, mybir.dt.bfloat16, mybir.dt.float16
    i32, u32 = mybir.dt.int32, mybir.dt.uint32
    ALU = mybir.AluOpType
    ACT = mybir.ActivationFunctionType
    X = mybir.AxisListType.X
    ctx = ExitStack()
    with ctx:
        def sb(name, shape, dt):
            return ctx.enter_context(nc.sbuf_tensor(name, shape, dt))

        def sem(name):
            return ctx.enter_context(nc.semaphore(name))

        slots_src = nc.dram_tensor("slots_src", (P * TILES, 4), f32, kind="Internal").ap()
        slots_dst = nc.dram_tensor("slots_dst", (P * TILES, 4), f32, kind="Internal").ap()
        table1 = nc.dram_tensor("table1", (N, W1), f32, kind="Internal").ap()
        table3 = nc.dram_tensor("table3", (RELS * N, W3), f32, kind="Internal").ap()

        region = sb("region", [P, TILES * W3], f32)

        def part(start, size):
            return region[:, start:start + size]

        rows1 = part(0, TILES * W1).rearrange("p (t w) -> p t w", w=W1)
        rows3 = region[:, :].rearrange("p (t w) -> p t w", w=W3)
        hot_ring = part(0, 2048).bitcast(bf16).rearrange("p (u k n) -> p u k n", u=4, k=2)
        adj = part(2048, 2048).rearrange("p (b n) -> p b n", b=NB)
        axT = part(4096, 1024).rearrange("p (c n) -> p c n", c=KC)
        w0_nat = part(5120, 512).rearrange("p (b i) -> p b i", b=KC)
        b0_nat = part(5632, 512).rearrange("p (b i) -> p b i", b=KC)
        w0T = part(6144, 512).rearrange("p (c o) -> p c o", c=KC)
        b0T = part(6656, 512).rearrange("p (c o) -> p c o", c=KC)
        group_tmp = part(8192, 2048)
        wa_tmp = part(10240, 256)
        abc = part(10496, 1024).rearrange("p (k f) -> p k f", k=4)
        type_row = part(11520, N).bitcast(i32)
        empty = part(12032, 4 * TILES).rearrange("p (t w) -> p t w", w=4)
        ends_f = part(12320, 2 * EC).rearrange("p (k j) -> p k j", k=2)
        edges_i = part(12456, 3 * EC).bitcast(i32).rearrange("p (k j) -> p k j", k=3)
        edge_w = part(12660, EC)
        block_f = part(12728, TILES)
        pair_w = part(0, 8192).rearrange("p (b h n) -> p b h n", b=NB, h=H)
        exp_ring = part(8192, 2048).rearrange("p (r k n) -> p r k n", r=2, k=2)
        hx = part(10240, NB * H * 65).rearrange("p (b h w) -> p b h w", b=NB, h=H)
        h_neg = part(11280, 264)
        a_dst = part(11544, 16).rearrange("p (b h) -> p b h", b=NB)
        a_neg = part(11560, 32).rearrange("p (k b h) -> p k b h", k=2, b=NB)
        elu_tmp = part(11592, 3072).rearrange("p (k f) -> p k f", k=3)
        stage = part(0, 8192).rearrange("p (k r w) -> p k r w", k=2, r=RELS)
        xmT = part(8192, 4096).rearrange("p (t c n) -> p t c n", t=TYPES, c=KC)
        kT = part(12288, 1024).rearrange("p (c n) -> p c n", c=KC)
        vT = part(13312, 1024).rearrange("p (c n) -> p c n", c=KC)
        q_f = part(14336, 1024)
        q_r = part(15360, 1024)
        kqv = part(18720, 6144).rearrange("p (k t c o) -> p k t c o", k=3, t=TYPES, c=KC)
        att_nat = part(24864, 2048).rearrange("p (r a w) -> p r a w", r=RELS, a=2)
        countT = part(24864, 2048).rearrange("p (b n) -> p b n", b=NB)
        attT = part(26912, 2048).rearrange("p (a r w) -> p a r w", r=RELS, a=2)
        msgD = part(28960, 2048).rearrange("p (a r w) -> p a r w", r=RELS, a=2)
        count = part(31008, 2048).rearrange("p (b n) -> p b n", b=NB)
        w1x = part(33056, 528).rearrange("p (c w) -> p c w", c=KC)
        w2x = part(33584, 528).rearrange("p (c w) -> p c w", c=KC)
        feat1 = part(34112, 1056).rearrange("p (b w) -> p b w", b=NB)
        xT = part(35168, 1024).rearrange("p (c n) -> p c n", c=KC)
        pri_bc = part(36192, 32)
        agg = part(0, 1024).rearrange("p (b f) -> p b f", b=NB)
        aggT = part(1024, 1024).rearrange("p (c n) -> p c n", c=KC)
        amT = part(2048, 4096).rearrange("p (t c n) -> p t c n", t=TYPES, c=KC)

        identf = sb("identf", [P, P], f32)
        identb = sb("identb", [P, P], bf16)
        bigI = sb("bigI", [P, P], bf16)
        before = sb("before", [P, P], bf16)
        onesb = sb("onesb", [P, P], bf16)
        ones_f = sb("ones_f", [P, 72], f32)
        zerob = sb("zerob", [P, W1], bf16)
        iota16 = sb("iota16", [P, N], f16)
        tile_at = sb("tile_at", [P, TILES], f32)
        x = sb("x", [P, NB, D], f32)
        alin = sb("alin", [P, TYPES, KC, D], f32)
        mask = sb("mask", [P, TYPES, N], bf16)
        bias1 = sb("bias1", [P, D], f32)
        skip_e = sb("skip_e", [P, 3, TYPES], f32)
        payload = [sb(f"payload{g}", [P, EC, 4], f32) for g in range(2)]
        address = [sb(f"address{g}", [P, EC], u32) for g in range(2)]
        slots = [sb(f"slots{g}", [P, TILES, 4], f32) for g in range(2)]
        block_of = [sb(f"block_of{g}", [P, TILES], i32) for g in range(2)]
        others = sb("others", [P, NB, TILES], f32)
        hotT = sb("hotT", [P, TILES, P], bf16)
        hotm1 = sb("hotm1", [P, UN, P], bf16)
        hotf = sb("hotf", [P, UN, P], f32)
        score = sb("score", [P, TILES, H], f32)
        score_s = sb("score_s", [P, UN, H], f32)
        score_b = sb("score_b", [P, UN, H], bf16)
        zt = sb("zt", [P, 2, HALF * H], f32)
        tmax = sb("tmax", [P, TILES, H], f32)
        comb = sb("comb", [P, H, TILES], f32)
        node_max = sb("node_max", [P, NB, H], bf16)
        parts3 = sb("parts3", [P, 3, NB, D], bf16)
        prod = sb("prod", [P, 1, D], f32)
        small = sb("small", [P, 128], f32)
        PS = ctx.enter_context(nc.psum_tensor("PS", [P, 8, BANK], f32))
        sums = PS[:, 4:8, :].rearrange("p b f -> p (b f)")

        loads = {n: sem("loaded_" + n) for n in
                 "edges x w0 w1 w2 kqv rel alin types".split()}
        fixed = sem("constants_made")
        pool_step = sem("pool_step")
        dve_step = sem("dve_step")
        act_step = sem("act_step")
        prefilled = sem("slots_prefilled")
        totals_ready = sem("group_totals_ready")
        prefix_done = sem("group_prefix_done")
        address_ready = sem("addresses_ready")
        scattered = [[sem(f"scattered{g}_{u}") for u in range(4)] for g in range(2)]
        slots_loaded = [sem(f"slots_loaded{g}") for g in range(2)]
        gathered = [[sem(f"gathered{g}_{u}") for u in range(4)] for g in range(2)]
        ends_ready = sem("edge_ends_ready")
        hots_ready = sem("one_hots_ready")
        hots_used = sem("one_hots_used")
        prep_done = sem("prep_transposed")
        prep_moved = sem("prep_moved")
        att_done = sem("att_transposed")
        att_moved = sem("att_moved")
        bx_done = sem("xB_done")
        count_moved = sem("counts_moved")
        adj_ready = sem("adjacency_ready")
        ax_done = sem("adj_x_done")
        ax_moved = sem("adj_x_moved")
        l0_done = sem("layer0_products_done")
        var_ready = sem("variances_ready")
        std_ready = sem("deviations_ready")
        x_ready = sem("x_ready")
        xT_done = sem("xT_done")
        xT_moved = sem("xT_moved")
        feat_done = sem("features_done")
        feat_moved = sem("features_moved")
        table1_written = sem("table1_written")
        self_split = sem("self_scores_split")
        cT_done = sem("counts_transposed")
        cT_moved = sem("countsT_moved")
        hotm1_ready = sem("hotm1_ready")
        hotT_done = sem("hotT_transposed")
        hotT_moved = sem("hotT_moved")
        near_done = sem("own_node_gathered")
        near_used = sem("own_node_used")
        score_ready = sem("scores_ready")
        spread_done = sem("scores_spread")
        spread_used = sem("maxima_taken")
        max_ready = sem("node_maxima_ready")
        maxe_done = sem("maxima_on_edges")
        diff_ready = sem("differences_ready")
        exp_ready = sem("exponentials_ready")
        message_ready = sem("messages_ready")
        hotf_ready = sem("hotf_ready")
        summed = sem("messages_summed")
        sums_done = sem("sums_done")
        wx_ready = sem("weight_vectors_ready")
        h_done = sem("h_done")
        spread2_done = sem("source_scores_spread")
        h_moved = sem("h_moved")
        pexp_ready = sem("pair_exp_ready")
        pw_ready = sem("pair_weights_ready")
        hp_done = sem("pair_sums_done")
        elu_in = sem("elu_arguments_ready")
        elu_exp = sem("elu_exp_ready")
        xm_ready = sem("typed_x_ready")
        kv_done = sem("keys_values_done")
        kv_moved = sem("keys_values_moved")
        q_done = sem("queries_done")
        q_split = sem("queries_split")
        rel_done = sem("relation_products_done")
        rel_moved_a = sem("relation_products_moved_act")
        rel_moved_v = sem("relation_products_moved_dve")
        t3_written = [sem(f"table3_written{k}") for k in range(2)]
        skip_in_s = sem("skip_exp_ready")
        am_ready = sem("typed_sums_ready")
        o_done = sem("output_products_done")
        out_written = sem("output_written")

        block = ctx.enter_context(nc.Block())

        @block.sync
        def _(sp):
            for k, a in enumerate((src_in, dst_in, etype_in)):
                sp.dma_start(edges_i[:, k, :], a.rearrange("(p j) -> p j", p=P)).then_inc(loads["edges"], 16)
            sp.dma_start(edge_w, ew_in.rearrange("(p j) -> p j", p=P)).then_inc(loads["edges"], 16)
            sp.dma_start(x[:, :, :], x_in.rearrange("(b p) f -> p b f", p=P)).then_inc(loads["x"], 16)
            sp.dma_start(w0_nat, w0_in.rearrange("(b p) i -> p b i", p=P)).then_inc(loads["w0"], 16)
            sp.dma_start(b0_nat, b0_in.rearrange("(b p) i -> p b i", p=P)).then_inc(loads["w0"], 16)
            for c in range(KC):
                sp.dma_start(w1x[:, c, 4:4 + D].rearrange("p (h o) -> p h o", h=H),
                             w1_in[:, c * P:(c + 1) * P, :].rearrange("h p o -> p h o")).then_inc(loads["w1"], 16)
                sp.dma_start(w2x[:, c, 0:D].rearrange("p (h o) -> p h o", h=H),
                             w2_in[:, c * P:(c + 1) * P, :].rearrange("h p o -> p h o")).then_inc(loads["w2"], 16)
            sp.dma_start(abc[:, 0, :], aneigh_in.rearrange("(o h) f -> o (h f)", o=1).broadcast_to([P, D])).then_inc(loads["w1"], 16)
            sp.dma_start(abc[:, 1, :], aself_in.rearrange("(o h) f -> o (h f)", o=1).broadcast_to([P, D])).then_inc(loads["w1"], 16)
            sp.dma_start(abc[:, 2:4, :], a2_in.rearrange("h o f -> o (h f)").broadcast_to([P, 2 * D])).then_inc(loads["w2"], 16)
            sp.dma_start(bias1[:, :], bias1_in.rearrange("(o h) f -> o (h f)", o=1).broadcast_to([P, D])).then_inc(loads["w1"], 16)
            for k, a in enumerate((klin_in, qlin_in, vlin_in)):
                sp.dma_start(kqv[:, k, :, :, :], a.rearrange("t (c p) o -> p t c o", p=P)).then_inc(loads["kqv"], 16)
            sp.dma_start(alin[:, :, :, :], alin_in.rearrange("t (c p) o -> p t c o", p=P)).then_inc(loads["alin"], 16)
            sp.dma_start(type_row, ntype_in.rearrange("(o n) -> o n", o=1).broadcast_to([P, N])).then_inc(loads["types"], 16)
            sp.dma_start(skip_e[:, 0, :], skip_in.rearrange("(o n) -> o n", o=1).broadcast_to([P, TYPES])).then_inc(loads["types"], 16)

            for g, table in ((0, slots_src), (1, slots_dst)):
                if g == 1:
                    sp.wait_ge(feat_moved, NB)
                    sp.dma_start(table1.rearrange("(b p) w -> p b w", p=P), feat1[:, :, 0:W1]).then_inc(table1_written, 16)
                for u in range(4):
                    sp.wait_ge(scattered[g][u], 16 * (EC // 4))
                sp.dma_start(slots[g][:, :, :], table.rearrange("(p t) w -> p t w", p=P)).then_inc(slots_loaded[g], 16)
            t3 = table3.rearrange("(r b p) w -> p b r w", p=P, b=NB)
            for b in range(NB):
                sp.wait_ge(rel_moved_a, 4 * (b + 1))
                sp.wait_ge(rel_moved_v, 4 * (b + 1))
                sp.dma_start(t3[:, b, :, :], stage[:, b % 2, :, :]).then_inc(t3_written[b % 2], 16)
            sp.wait_ge(x_ready, 4 * NB)
            sp.dma_start(out.rearrange("(b p) f -> p b f", p=P), x[:, :, :]).then_inc(out_written, 16)
            sp.wait_ge(out_written, 16)

        @block.gpsimd
        def _(pool):
            pool.memset(identf[:, :], 0.0).then_inc(pool_step, 1)
            pool.memset(empty[:, :, :], 0.0).then_inc(pool_step, 1)
            pool.memset(before[:, :], 0.0).then_inc(pool_step, 1)
            pool.wait_ge(pool_step, 3)
            pool.memset(empty[:, :, 0], -1.0).then_inc(pool_step, 1)
            pool.affine_select(out=identf[:, :], in_=identf[:, :], compare_op=ALU.not_equal, fill=1.0, base=0,
                               pattern=[[-1, P]], channel_multiplier=1).then_inc(pool_step, 1)
            pool.affine_select(out=before[:, :], in_=before[:, :], compare_op=ALU.is_ge, fill=1.0, base=0,
                               pattern=[[-1, P]], channel_multiplier=1).then_inc(fixed, 1)
            pool.memset(onesb[:, :], 1.0).then_inc(fixed, 1)
            pool.memset(ones_f[:, :], 1.0).then_inc(fixed, 1)
            pool.memset(zerob[:, :], 0.0).then_inc(fixed, 1)
            pool.iota(iota16[:, :], pattern=[[1, N]], base=0, channel_multiplier=0,
                      allow_small_or_imprecise_dtypes=True).then_inc(fixed, 1)
            pool.iota(tile_at[:, :], pattern=[[P, TILES]], base=0, channel_multiplier=0,
                      allow_small_or_imprecise_dtypes=True).then_inc(fixed, 1)
            pool.wait_ge(pool_step, 5)
            pool.tensor_copy(identb[:, :], identf[:, :]).then_inc(fixed, 1)
            pool.tensor_scalar(bigI[:, :], identf[:, :], BIG, None, ALU.mult).then_inc(fixed, 1)
            for table in (slots_src, slots_dst):
                pool.dma_start(table.rearrange("(p t) w -> p t w", p=P), empty[:, :, :]).then_inc(prefilled, 16)
            for name, a, nat in ((0, att_in, att_nat), (1, msg_in, msgD)):
                pool.memset(nat, 0.0).then_inc(pool_step, 1)
            pool.wait_ge(pool_step, 7)
            for h in range(H):
                a, s = h // 2, (h % 2) * DK
                pool.dma_start(att_nat[s:s + DK, :, a, s:s + DK], att_in[:, h, :, :].rearrange("r d e -> d r e")).then_inc(loads["rel"], 16)
                pool.dma_start(msgD[s:s + DK, a, :, s:s + DK], msg_in[:, h, :, :].rearrange("r d e -> d r e")).then_inc(loads["rel"], 16)
            pool.dma_start(pri_bc, pri_in.rearrange("(o r) h -> o (r h)", o=1).broadcast_to([P, RELS * H])).then_inc(loads["rel"], 16)

            def scatter(g, table, j):
                if j >= 4:
                    pool.wait_ge(scattered[g][j % 4], 16 * (j // 4))
                pool.indirect_dma_start(out=table, out_offset=bass.IndirectOffsetOnAxis(ap=address[g][:, j:j + 1], axis=0),
                                        in_=payload[g][:, j, :], in_offset=None).then_inc(scattered[g][j % 4], 16)

            def gather(g, table, rows, t):
                if t >= 4:
                    pool.wait_ge(gathered[g][t % 4], 16 * (t // 4))
                pool.indirect_dma_start(out=rows[:, t, :], out_offset=None, in_=table,
                                        in_offset=bass.IndirectOffsetOnAxis(ap=slots[g][:, t, 1:2].bitcast(u32), axis=0))\
                    .then_inc(gathered[g][t % 4], 16)

            pool.wait_ge(prefilled, 32)
            pool.wait_ge(address_ready, 1)
            for j in range(EC):
                scatter(0, slots_src, j)
            pool.wait_ge(address_ready, 2)
            for j in range(EARLY):
                scatter(1, slots_dst, j)
            pool.wait_ge(slots_loaded[0], 16)
            pool.wait_ge(table1_written, 16)
            for t in range(TILES):
                gather(0, table1, rows1, t)
            for j in range(EARLY, EC):
                scatter(1, slots_dst, j)
            pool.wait_ge(slots_loaded[1], 16)
            pool.wait_ge(t3_written[0], 32)
            pool.wait_ge(t3_written[1], 32)
            pool.wait_ge(q_split, 1)
            for t in range(TILES):
                gather(1, table3, rows3, t)

        @block.tensor
        def _(pe):
            def transposes(source, banks, done, waits=()):
                for c in range(KC):
                    for b in range(NB):
                        last = nc.tensor.transpose(PS[:, banks[c], b * P:(b + 1) * P], source[:, b, c * P:(c + 1) * P], identf[:, :])
                    last.then_inc(done, 1)

            def group_prefix(bank):
                nc.tensor.matmul(PS[:, bank, 0:4], before[:, :], small[:, 0:2].bitcast(bf16), start=True, stop=True)
                nc.tensor.matmul(PS[:, bank, 4:8], onesb[:, :], small[:, 0:2].bitcast(bf16), start=True, stop=True).then_inc(prefix_done, 1)

            pe.wait_ge(fixed, 8)
            pe.wait_ge(totals_ready, 1)
            group_prefix(4)
            pe.wait_ge(loads["x"], 16)
            transposes(x, (5, 6), prep_done)
            pe.wait_ge(loads["w0"], 32)
            for nat, bank in ((w0_nat, 7), (b0_nat, 5)):
                if bank == 5:
                    pe.wait_ge(prep_moved, 1)
                for c in range(KC):
                    for b in range(KC):
                        last = nc.tensor.transpose(PS[:, bank, c * D + b * P:c * D + (b + 1) * P], nat[:, b, c * P:(c + 1) * P], identf[:, :])
                last.then_inc(prep_done, 1)
            pe.wait_ge(prep_moved, 4)
            for b in range(NB):
                for c in range(KC):
                    last = nc.tensor.matmul(PS[:, 6 + b // 2, (b % 2) * D:(b % 2 + 1) * D], xT[:, c, b * P:(b + 1) * P], b0T[:, c, :],
                                            start=(c == 0), stop=(c == KC - 1))
            last.then_inc(bx_done, 1)
            def count_turn(i, first, last_turn):
                for u in range(4):
                    pe.wait_ge(hots_ready, i * 4 + (u + 1))
                    for b in range(NB):
                        ins = nc.tensor.matmul(PS[:, b, :], hot_ring[:, u, 0, b * P:(b + 1) * P], hot_ring[:, u, 1, :],
                                               start=(first and u == 0), stop=(last_turn and u == 3), skip_group_check=True)
                    ins.then_inc(hots_used, 1)

            count_turn(0, True, False)
            with pe.Fori(1, EC // 4 - 1) as i:
                count_turn(i, False, False)
            count_turn(EC // 4 - 1, False, True)
            pe.wait_ge(adj_ready, NB)
            for c in range(KC):
                for b in range(NB):
                    last = nc.tensor.matmul(PS[:, 4 + c, :], x[:, b, c * P:(c + 1) * P], adj[:, b, :], start=(b == 0), stop=(b == NB - 1))
                last.then_inc(ax_done, 1)
            pe.wait_ge(count_moved, NB)
            for d in range(NB):
                for b in range(NB):
                    nc.tensor.matmul(PS[:, 2, d:d + 1], count[:, b, d * P:(d + 1) * P], ones_f[:, 0:1], start=(b == 0), stop=(b == NB - 1))
            pe.wait_ge(totals_ready, 2)
            group_prefix(3)
            pe.wait_ge(ax_moved, 2)
            for b in range(NB):
                for c in range(KC):
                    last = nc.tensor.matmul(PS[:, b // 2, (b % 2) * D:(b % 2 + 1) * D], axT[:, c, b * P:(b + 1) * P], w0T[:, c, :],
                                            start=(c == 0), stop=(c == KC - 1))
            last.then_inc(l0_done, 1)

            pe.wait_ge(x_ready, NB)
            transposes(x, (4, 5), xT_done)
            pe.wait_ge(xT_moved, 2)
            pe.wait_ge(wx_ready, 4 * KC)
            for b in range(NB):
                for c in range(KC):
                    last = nc.tensor.matmul(PS[:, b, 0:264], xT[:, c, b * P:(b + 1) * P], w1x[:, c, :], start=(c == 0), stop=(c == KC - 1))
                last.then_inc(feat_done, 1)
            pe.wait_ge(loads["rel"], 16 * 9)
            for n in range(4):
                if n >= 2:
                    pe.wait_ge(att_moved, n - 1)
                for k in range(4):
                    last = nc.tensor.transpose(PS[:, 6 + n % 2, k * P:(k + 1) * P], att_nat[:, (n % 2) * 4 + k, n // 2, :], identf[:, :])
                last.then_inc(att_done, 1)
            pe.wait_ge(att_moved, 4)
            for d in range(NB):
                if d >= 2:
                    pe.wait_ge(cT_moved, d - 1)
                for b in range(NB):
                    last = nc.tensor.transpose(PS[:, 6 + d % 2, b * P:(b + 1) * P], count[:, b, d * P:(d + 1) * P], identf[:, :])
                last.then_inc(cT_done, 1)

            def edge_layer(g):
                width = H if g == 0 else D
                base = g * TILES
                bi = base // UN

                def masks(i, half):
                    pe.wait_ge(hotm1_ready, (i + bi) * UN + (half * HALF + HALF))
                    for u in range(half * HALF, (half + 1) * HALF):
                        last = nc.tensor.transpose(PS[:, half, :].bitcast(bf16)[:, (u % HALF) * P:(u % HALF + 1) * P], hotm1[:, u, :], identb[:, :])
                    last.then_inc(hotT_done, 1)
                    pe.wait_ge(hotT_moved, (i + bi) * 2 + (half + 1))
                    for u in range(half * HALF, (half + 1) * HALF):
                        v = pe.value_load(block_of[g][0:1, bass.ds(i * UN + u, 1)], min_val=0, max_val=NB - 1)
                        if g == 0:
                            dst = PS[:, 2 + half, (u % HALF) * H:(u % HALF + 1) * H]
                            table = parts3[:, :, :, 0:H]
                        else:
                            dst = PS[:, 2 + half * 2 + (u % HALF) // 2, (u % 2) * D:(u % 2 + 1) * D]
                        for k in range(3):
                            rhs = parts3[:, k, bass.ds(v, 1), 0:width].rearrange("p o w -> p (o w)")
                            last = nc.tensor.matmul(dst, hotT[:, bass.ds(i * UN + u, 1), :].rearrange("p o n -> p (o n)"), rhs,
                                                    start=(k == 0), stop=(k == 2), skip_group_check=True)
                        if g == 1:
                            last.then_inc(near_done, 1)
                    if g == 0:
                        last.then_inc(near_done, 1)

                def spread(i, half):
                    for u in range(half * HALF, (half + 1) * HALF):
                        if g == 0:
                            if u % HALF == 0:
                                pe.wait_ge(score_ready, i * 2 + (half + 1))
                        else:
                            pe.wait_ge(score_ready, i * UN + (u + 1 + 2 * TILES // UN))
                        if not (isinstance(i, int) and i == 0 and base == 0 and u < 2):
                            pe.wait_ge(spread_used, (i + bi) * UN + (u - 1))
                        bank = PS[:, 6 + u % 2, :].rearrange("p (h e) -> p h e", h=H)
                        nc.tensor.matmul(bank, hotm1[:, u, :], bigI[:, :].unsqueeze(1).broadcast_to([P, H, P]), start=True, stop=False,
                                         skip_group_check=True)
                        for h in range(H):
                            last = nc.tensor.matmul(bank[:, h, :], score_b[:, u, h:h + 1].broadcast_to([P, P]), identb[:, :],
                                                    start=False, stop=(h == H - 1), skip_group_check=True)
                        last.then_inc(spread_done, 1)

                def near_free(i, half):
                    if g == 0:
                        pe.wait_ge(near_used, i * 2 + (half - 1))
                    else:
                        pe.wait_ge(near_used, i * UN + (half * HALF - HALF + 2 * TILES // UN))

                pe.wait_ge(slots_loaded[g], 16)
                masks(0, 0)

                def turn(i, first, last_turn):
                    for half in range(2):
                        if half == 0:
                            if not first:
                                near_free(i, 1)
                            masks(i, 1)
                        elif not last_turn:
                            near_free(i + 1, 0)
                            masks(i + 1, 0)
                        spread(i, half)

                turn(0, True, False)
                with pe.Fori(1, TILES // UN - 1) as i:
                    turn(i, False, False)
                turn(TILES // UN - 1, False, True)

                pe.wait_ge(max_ready, g + 1)

                def maxima(i):
                    for u in range(UN):
                        v = pe.value_load(block_of[g][0:1, bass.ds(i * UN + u, 1)], min_val=0, max_val=NB - 1)
                        last = nc.tensor.matmul(PS[:, 0, bass.ds(i * (UN * H) + u * H, H)], hotT[:, bass.ds(i * UN + u, 1), :].rearrange("p o n -> p (o n)"),
                                                node_max[:, bass.ds(v, 1), :].rearrange("p o h -> p (o h)"), start=True, stop=True,
                                                skip_group_check=True)
                    return last

                with pe.Fori(0, TILES // UN - 1) as i:
                    maxima(i)
                maxima(TILES // UN - 1).then_inc(maxe_done, 1)
                for b in range(NB):
                    nc.tensor.matmul(PS[:, 4 + b, 0:W1], onesb[:, :], zerob[:, :], start=True, stop=False, skip_group_check=True)

                def sums_turn(i, start):
                    for u in range(UN):
                        if u % HALF == 0:
                            pe.wait_ge(message_ready, (i + bi) * 2 + (u // HALF + 1))
                        v = pe.value_load(block_of[g][0:1, bass.ds(i * UN + u, 1)], min_val=0, max_val=NB - 1)
                        src = rows1[:, bass.ds(i * UN + u, 1), :] if g == 0 else rows3[:, bass.ds(i * UN + u, 1), D - 4:W3]
                        nc.tensor.matmul(sums[:, bass.ds(v * BANK, W1)], hotf[:, u, :], src.rearrange("p o w -> p (o w)"),
                                         start=False, stop=False, skip_group_check=True).then_inc(summed, 1)

                with pe.Fori(0, TILES // UN) as i:
                    sums_turn(i, False)
                for b in range(NB):
                    last = nc.tensor.matmul(PS[:, 4 + b, 0:W1], onesb[:, :], zerob[:, :], start=False, stop=True, skip_group_check=True)
                last.then_inc(sums_done, 1)

            pe.wait_ge(self_split, 1)
            pe.wait_ge(feat_moved, NB)
            pe.wait_ge(cT_moved, 4)
            edge_layer(0)

            pe.wait_ge(x_ready, 2 * NB)
            transposes(x, (0, 1), xT_done)
            pe.wait_ge(xT_moved, 4)
            for h in range(H):
                for c in range(KC):
                    last = nc.tensor.matmul(PS[:, h, :], w2x[:, c, 260 + h:261 + h].broadcast_to([P, P]), xT[:, c, :],
                                            start=(c == 0), stop=(c == KC - 1))
                last.then_inc(spread2_done, 1)
                b = h
                for c in range(KC):
                    last = nc.tensor.matmul(PS[:, 4 + b, 0:260], xT[:, c, b * P:(b + 1) * P], w2x[:, c, 0:260], start=(c == 0), stop=(c == KC - 1))
                last.then_inc(h_done, 1)
            pe.wait_ge(h_moved, NB)
            for b in range(NB):
                for h in range(H):
                    pe.wait_ge(pw_ready, b * H + h + 1)
                    for s in range(NB):
                        last = nc.tensor.matmul(PS[:, 4 + s, h * 65:(h + 1) * 65], pair_w[:, b, h, s * P:(s + 1) * P], hx[:, b, h, :],
                                                start=(b == 0 and h == 0), stop=(b == NB - 1 and h == H - 1), skip_group_check=True)
            last.then_inc(hp_done, 1)

            pe.wait_ge(x_ready, 3 * NB)
            transposes(x, (0, 1), xT_done)
            pe.wait_ge(loads["kqv"], 48)
            for k, bank in ((0, 4), (2, 2)):
                for o in range(KC):
                    for t in range(TYPES):
                        pe.wait_ge(xm_ready, t + 1)
                        for c in range(KC):
                            last = nc.tensor.matmul(PS[:, bank + o, :], kqv[:, k, t, c, o * P:(o + 1) * P], xmT[:, t, c, :],
                                                    start=(t == 0 and c == 0), stop=(t == TYPES - 1 and c == KC - 1))
                    last.then_inc(kv_done, 1)
            for b in range(NB):
                for t in range(TYPES):
                    for c in range(KC):
                        last = nc.tensor.matmul(PS[:, 6 + b // 2, (b % 2) * D:(b % 2 + 1) * D], xmT[:, t, c, b * P:(b + 1) * P], kqv[:, 1, t, c, :],
                                                start=(t == 0 and c == 0), stop=(t == TYPES - 1 and c == KC - 1))
            last.then_inc(q_done, 1)
            pe.wait_ge(kv_moved, 4)
            pe.wait_ge(att_moved, 4)
            n = 0
            for b in range(NB):
                for a in range(2):
                    for r in range(0, RELS, 4):
                        if n >= 2:
                            pe.wait_ge(rel_moved_a, n - 1)
                        nc.tensor.matmul(PS[:, n % 2, :], kT[:, a, b * P:(b + 1) * P], attT[:, a, r:r + 4, :].rearrange("p r w -> p (r w)"),
                                         start=True, stop=True).then_inc(rel_done, 1)
                        if n >= 2:
                            pe.wait_ge(rel_moved_v, n - 1)
                        nc.tensor.matmul(PS[:, 4 + n % 2, :], vT[:, a, b * P:(b + 1) * P], msgD[:, a, r:r + 4, :].rearrange("p r w -> p (r w)"),
                                         start=True, stop=True).then_inc(rel_done, 1)
                        n += 1
            pe.wait_ge(q_split, 1)
            pe.wait_ge(rel_moved_a, 16)
            pe.wait_ge(rel_moved_v, 16)
            edge_layer(1)
            pe.wait_ge(am_ready, 1)
            transposes(agg, (0, 1), xT_done)
            pe.wait_ge(loads["alin"], 16)
            pe.wait_ge(am_ready, 5)
            for b in range(NB):
                for t in range(TYPES):
                    for c in range(KC):
                        last = nc.tensor.matmul(PS[:, 2 + b // 2, (b % 2) * D:(b % 2 + 1) * D], amT[:, t, c, b * P:(b + 1) * P], alin[:, t, c, :],
                                                start=(t == 0 and c == 0), stop=(t == TYPES - 1 and c == KC - 1))
            last.then_inc(o_done, 1)

        @block.scalar
        def _(act):
            def copy(dst, src, done, n=1):
                nc.scalar.activation(dst, src, ACT.Copy).then_inc(done, n)

            for n, (dst, bank) in enumerate(((xT[:, 0, :], 5), (xT[:, 1, :], 6), (w0T.rearrange("p c o -> p (c o)"), 7),
                                             (b0T.rearrange("p c o -> p (c o)"), 5))):
                act.wait_ge(prep_done, n + 1)
                copy(dst, PS[:, bank, :], prep_moved)
            act.wait_ge(hots_used, EC)
            for b in range(NB):
                copy(count[:, b, :], PS[:, b, :], count_moved)
            for c in range(KC):
                act.wait_ge(ax_done, c + 1)
                copy(axT[:, c, :], PS[:, 4 + c, :], ax_moved)

            def deviations(k):
                act.wait_ge(var_ready, k)
                nc.scalar.activation(small[:, 64:68], small[:, 60:64], ACT.Sqrt).then_inc(std_ready, 1)

            def move_xT(k, banks):
                dst = aggT if k == 4 else xT
                for c in range(KC):
                    act.wait_ge(xT_done, 2 * (k - 1) + c + 1)
                    copy(dst[:, c, :], PS[:, banks[c], :], xT_moved)

            def edge_layer(g):
                bi = g * TILES // UN

                def move_hotT(i, half):
                    act.wait_ge(hotT_done, (i + bi) * 2 + (half + 1))
                    nc.scalar.activation(hotT[:, bass.ds(i * UN + half * HALF, HALF), :].rearrange("p t n -> p (t n)"),
                                         PS[:, half, :].bitcast(bf16)[:, 0:HALF * P], ACT.Copy, bias=1.0).then_inc(hotT_moved, 1)

                with act.Fori(0, TILES // UN) as i:
                    for half in range(2):
                        move_hotT(i, half)
                act.wait_ge(diff_ready, g + 1)
                dst = rows1[:, :, 0:4] if g == 0 else rows3[:, :, D - 4:D]
                nc.scalar.activation(dst, score[:, :, :], ACT.Exp).then_inc(exp_ready, 1)

            deviations(1)
            move_xT(1, (4, 5))
            for b in range(NB):
                act.wait_ge(feat_done, b + 1)
                copy(feat1[:, b, :], PS[:, b, 0:264], feat_moved)
            act.wait_ge(att_moved, 4)
            for d in range(NB):
                act.wait_ge(cT_done, d + 1)
                copy(countT[:, d, :], PS[:, 6 + d % 2, :], cT_moved)
            edge_layer(0)
            deviations(2)
            move_xT(2, (0, 1))
            act.wait_ge(h_moved, NB)
            for b in range(NB):
                for h in range(H):
                    n = b * H + h
                    if n < H:
                        act.wait_ge(spread2_done, h + 1)
                    if n >= 2:
                        act.wait_ge(pw_ready, n - 1)
                    nc.scalar.activation(exp_ring[:, n % 2, 0, :], PS[:, h, :], ACT.Exp, bias=a_neg[:, 0, b, h:h + 1], scale=-1.0)
                    nc.scalar.activation(exp_ring[:, n % 2, 1, :], PS[:, h, :], ACT.Exp, bias=a_neg[:, 1, b, h:h + 1], scale=-0.2).then_inc(pexp_ready, 1)
            for k in range(2):
                act.wait_ge(elu_in, k + 1)
                nc.scalar.activation(elu_tmp[:, 1, :], elu_tmp[:, 0, :], ACT.Exp).then_inc(elu_exp, 1)
            act.wait_ge(loads["types"], 32)
            nc.scalar.activation(skip_e[:, 1, :], skip_e[:, 0, :], ACT.Exp, scale=-1.0).then_inc(skip_in_s, 1)
            deviations(3)
            move_xT(3, (0, 1))
            for n, dst in enumerate((kT[:, 0, :], kT[:, 1, :], vT[:, 0, :], vT[:, 1, :])):
                act.wait_ge(kv_done, n + 1)
                copy(dst, PS[:, (4, 5, 2, 3)[n], :], kv_moved)
            n = 0
            for b in range(NB):
                if b >= 2:
                    act.wait_ge(t3_written[b % 2], 16)
                for a in range(2):
                    for r in range(0, RELS, 4):
                        act.wait_ge(rel_done, 2 * n + 1)
                        copy(stage[:, b % 2, r:r + 4, a * P:(a + 1) * P], PS[:, n % 2, :].rearrange("p (r w) -> p r w", r=4), rel_moved_a)
                        n += 1
            edge_layer(1)
            move_xT(4, (0, 1))
            deviations(4)

        @block.vector
        def _(dve):
            v = nc.vector
            steps = [0]

            def then(ins):
                steps[0] += 1
                ins.then_inc(dve_step, 1)
                dve.wait_ge(dve_step, steps[0])

            def grouping(g, half, bank):
                key = edges_i[:, g, :]
                T = group_tmp
                ind = T[:, 0:272].rearrange("p (k j) -> p k j", k=NB)
                scan = T[:, 272:544].rearrange("p (k j) -> p k j", k=NB)
                tmp = T[:, 544:816].rearrange("p (k j) -> p k j", k=NB)
                loc_i = T[:, 816:884].bitcast(i32)
                blk_i = T[:, 884:952].bitcast(i32)
                pos_i = T[:, 952:1020].bitcast(i32)
                low_i = T[:, 1020:1088].bitcast(i32)
                pad_i = T[:, 1088:1092].bitcast(i32)
                pad_j = T[:, 1092:1096].bitcast(i32)
                pad_f = T[:, 1096:1100]
                start = T[:, 1100:1104]
                base = T[:, 1104:1108]
                if half == 0:
                    group_totals(g, key, ind, scan, loc_i, blk_i)
                    return
                dve.wait_ge(prefix_done, g + 1)
                then(v.tensor_scalar(pad_i, PS[:, bank, 4:8], float(P - 1), None, ALU.add))
                then(v.tensor_scalar(pad_j, pad_i, -P, None, ALU.bitwise_and))
                then(v.tensor_copy(pad_f, pad_j))
                then(v.memset(start[:, 0:1], 0.0))
                for k in range(1, NB):
                    then(v.tensor_tensor(start[:, k:k + 1], start[:, k - 1:k], pad_f[:, k - 1:k], ALU.add))
                then(v.scalar_tensor_tensor(base, PS[:, bank, 0:4], -1.0, start, ALU.add, ALU.add))
                for k in range(NB):
                    ins = v.scalar_tensor_tensor(tmp[:, k, :], scan[:, k, :], base[:, k:k + 1], ind[:, k, :], ALU.add, ALU.mult)
                then(ins)
                then(v.tensor_tensor(tmp[:, 0:2, :], tmp[:, 0:2, :], tmp[:, 2:4, :], ALU.add))
                then(v.tensor_tensor(pos_i, tmp[:, 0, :], tmp[:, 1, :], ALU.add))
                then(v.tensor_scalar(low_i, pos_i, P - 1, None, ALU.bitwise_and))
                then(v.tensor_scalar(blk_i, pos_i, 7, None, ALU.arith_shift_right))
                v.scalar_tensor_tensor(address[g][:, :], low_i, float(TILES), blk_i, ALU.mult, ALU.add).then_inc(address_ready, 1)
                then(v.tensor_scalar(block_f, tile_at[:, :], start[:, 1:2], None, ALU.is_ge))
                then(v.scalar_tensor_tensor(block_f, tile_at[:, :], start[:, 2:3], block_f, ALU.is_ge, ALU.add))
                then(v.scalar_tensor_tensor(block_f, tile_at[:, :], start[:, 3:4], block_f, ALU.is_ge, ALU.add))
                then(v.tensor_copy(block_of[g][:, :], block_f))

            def group_totals(g, key, ind, scan, loc_i, blk_i):
                v.tensor_scalar(loc_i, key, P - 1, None, ALU.bitwise_and)
                v.memset(payload[g][:, :, 3], 0.0)
                then(v.tensor_scalar(blk_i, key, 7, None, ALU.arith_shift_right))
                v.tensor_copy(payload[g][:, :, 0], loc_i)
                if g == 0:
                    v.tensor_copy(payload[g][:, :, 1].bitcast(i32), edges_i[:, 1, :])
                else:
                    v.scalar_tensor_tensor(payload[g][:, :, 1].bitcast(i32), edges_i[:, 2, :], float(N), edges_i[:, 0, :], ALU.mult, ALU.add)
                v.tensor_copy(payload[g][:, :, 2], edge_w)
                for k in range(NB):
                    ins = v.tensor_scalar(ind[:, k, :], blk_i, float(k), None, ALU.is_equal)
                then(ins)
                for k in range(NB):
                    ins = v.tensor_tensor_scan(scan[:, k, :], ones_f[:, 0:EC], ind[:, k, :], 0.0, ALU.mult, ALU.add)
                then(ins)
                v.tensor_copy(small[:, 0:2].bitcast(bf16), scan[:, :, EC - 1]).then_inc(totals_ready, 1)

            dve.wait_ge(loads["edges"], 64)
            dve.wait_ge(fixed, 8)
            grouping(0, 0, 4)
            grouping(0, 1, 4)
            then(v.tensor_copy(ends_f[:, :, :], edges_i[:, 0:2, :]))

            def hot_turn(i, first):
                for u in range(4):
                    if not first:
                        dve.wait_ge(hots_used, i * 4 + (u - 3))
                    for k in range(2):
                        ins = v.tensor_scalar(hot_ring[:, u, k, :], iota16[:, :], ends_f[:, k, bass.ds(i * 4 + u, 1)], None, ALU.is_equal)
                    ins.then_inc(hots_ready, 1)

            hot_turn(0, True)
            with dve.Fori(1, EC // 4) as i:
                hot_turn(i, False)

            dve.wait_ge(loads["w1"], 16 * 5)
            dve.wait_ge(loads["w2"], 16 * 3)
            a2 = abc[:, 2:4, :].rearrange("p k f -> p (k f)").rearrange("p (h z f) -> p z h f", h=H, z=2)
            tmp3 = wa_tmp.rearrange("p (h f) -> p h f", h=H)
            vectors = 0
            for c in range(KC):
                w1h = w1x[:, c, 4:4 + D].rearrange("p (h f) -> p h f", h=H)
                w2h = w2x[:, c, 0:D].rearrange("p (h f) -> p h f", h=H)
                for wh, vec, dst in ((w1h, abc[:, 0, :].rearrange("p (h f) -> p h f", h=H), w1x[:, c, 0:4]),
                                     (w1h, abc[:, 1, :].rearrange("p (h f) -> p h f", h=H), w1x[:, c, 260:264]),
                                     (w2h, a2[:, 1, :, :], w2x[:, c, 256:260]),
                                     (w2h, a2[:, 0, :, :], w2x[:, c, 260:264])):
                    then(v.tensor_tensor(tmp3, wh, vec, ALU.mult))
                    v.tensor_reduce(dst, tmp3, X, ALU.add).then_inc(wx_ready, 1)
                    vectors += 1
                    dve.wait_ge(wx_ready, vectors)
            dve.wait_ge(loads["types"], 32)
            for t in range(TYPES):
                v.tensor_scalar(mask[:, t, :], type_row, float(t), None, ALU.is_equal)

            grouping(1, 0, 3)
            for b in range(NB):
                dve.wait_ge(count_moved, b + 1)
                v.tensor_scalar(adj[:, b, :], count[:, b, :], 1.0, None, ALU.min).then_inc(adj_ready, 1)

            mv = small[:, 40:48].rearrange("p (b k) -> p b k", k=2)
            stats = small[:, 8:32].rearrange("p (b k) -> p b k", k=6)

            def layernorm(k):
                for b in range(NB):
                    ins = v.bn_stats(stats[:, b, :], x[:, b, :])
                then(ins)
                for b in range(NB):
                    ins = v.bn_aggr(mv[:, b, :], stats[:, b, :])
                then(ins)
                v.tensor_scalar(small[:, 60:64], mv[:, :, 1], EPS, None, ALU.add).then_inc(var_ready, 1)
                dve.wait_ge(std_ready, k)
                then(v.reciprocal(small[:, 68:72], small[:, 64:68]))
                for b in range(NB):
                    v.tensor_scalar(x[:, b, :], x[:, b, :], mv[:, b, 0:1], small[:, 68 + b:69 + b], ALU.subtract, ALU.mult).then_inc(x_ready, 1)

            grouping(1, 1, 3)
            dve.wait_ge(l0_done, 1)
            dve.wait_ge(bx_done, 1)
            then(v.tensor_scalar(small[:, 32:36], PS[:, 2, 0:4], 1.0, None, ALU.max))
            then(v.reciprocal(small[:, 36:40], small[:, 32:36]))
            for b in range(NB):
                ins = v.scalar_tensor_tensor(x[:, b, :], PS[:, b // 2, (b % 2) * D:(b % 2 + 1) * D], small[:, 36 + b:37 + b], x[:, b, :], ALU.mult, ALU.add)
            then(ins)
            for b in range(NB):
                ins = v.tensor_tensor(x[:, b, :], x[:, b, :], PS[:, 6 + b // 2, (b % 2) * D:(b % 2 + 1) * D], ALU.add)
            then(ins)
            layernorm(1)

            def split(dst, src, rest):
                then(v.tensor_copy(dst[0], src))
                then(v.tensor_tensor(rest, src, dst[0], ALU.subtract))
                then(v.tensor_copy(dst[1], rest))
                then(v.tensor_tensor(rest, rest, dst[1], ALU.subtract))
                return v.tensor_copy(dst[2], rest)

            dve.wait_ge(feat_moved, NB)
            split([parts3[:, k, :, 0:H] for k in range(3)], feat1[:, :, 260:264], small[:, 72:88].rearrange("p (b h) -> p b h", b=NB)).then_inc(self_split, 1)

            dve.wait_ge(loads["rel"], 16 * 9)
            pri = pri_bc.rearrange("p (r a z) -> p a r z", r=RELS, a=2)
            for a in range(2):
                for r in range(0, RELS, 4):
                    n = a * 2 + r // 4
                    dve.wait_ge(att_done, n + 1)
                    for rr in range(4):
                        ins = v.scalar_tensor_tensor(attT[:, a, r + rr, :].rearrange("p (z w) -> p z w", z=2),
                                                     PS[:, 6 + n % 2, rr * P:(rr + 1) * P].rearrange("p (z w) -> p z w", z=2), DK ** -0.5,
                                                     pri[:, a, r + rr, :].unsqueeze(2).broadcast_to([P, 2, DK]), ALU.mult, ALU.mult)
                    ins.then_inc(att_moved, 1)

            def edge_layer(g):
                bi = g * TILES // UN

                def hots(i, half):
                    for u in range(half * HALF, (half + 1) * HALF):
                        v.tensor_scalar(hotm1[:, u, :], iota16[:, 0:P], slots[g][:, bass.ds(i * UN + u, 1), 0], 1.0, ALU.is_equal, ALU.subtract)\
                            .then_inc(hotm1_ready, 1)

                def scores(i, half, n0):
                    t0 = i * UN + half * HALF
                    if g == 0:
                        for u in range(HALF):
                            dve.wait_ge(gathered[g][u], i * 32 + (16 * (half + 1)))
                        dve.wait_ge(near_done, i * 2 + (half + 1))
                        z = zt[:, 0, :].rearrange("p (t h) -> p t h", t=HALF)
                        y = zt[:, 1, :].rearrange("p (t h) -> p t h", t=HALF)
                        own = PS[:, 2 + half, 0:HALF * H].rearrange("p (t h) -> p t h", t=HALF)
                        v.tensor_tensor(z, rows1[:, bass.ds(t0, HALF), 0:4], own, ALU.add).then_inc(near_used, 1)
                        dve.wait_ge(near_used, i * 2 + (half + 1))
                        step(v.scalar_tensor_tensor(y, z, 0.2, z, ALU.mult, ALU.max))
                        weight = slots[g][:, bass.ds(t0, HALF), 2:3].broadcast_to([P, HALF, H])
                        v.tensor_tensor(score_b[:, half * HALF:(half + 1) * HALF, :], y, weight, ALU.mult).then_inc(score_ready, 1)
                        v.tensor_tensor(score[:, bass.ds(t0, HALF), :], y, weight, ALU.mult)
                    else:
                        for u in range(half * HALF, (half + 1) * HALF):
                            dve.wait_ge(gathered[g][u % 4], i * 32 + (16 * (half + 1)))
                            dve.wait_ge(near_done, i * UN + (u - u % 2 + 2 + 2 * TILES // UN))
                            own = PS[:, 2 + half * 2 + (u % HALF) // 2, (u % 2) * D:(u % 2 + 1) * D]
                            v.tensor_tensor(prod[:, 0, :], rows3[:, bass.ds(i * UN + u, 1), 0:D].rearrange("p o w -> p (o w)"), own, ALU.mult)\
                                .then_inc(near_used, 1)
                            dve.wait_ge(near_used, i * UN + (u + 1 + 2 * TILES // UN))
                            step(v.tensor_reduce(score_s[:, u, :], prod[:, 0, :].rearrange("p (h w) -> p h w", h=H), X, ALU.add))
                            v.tensor_copy(score_b[:, u, :], score_s[:, u, :]).then_inc(score_ready, 1)
                            v.tensor_copy(score[:, bass.ds(i * UN + u, 1), :].rearrange("p o h -> p (o h)"), score_s[:, u, :])

                def maxima(i, half):
                    for u in range(half * HALF, (half + 1) * HALF):
                        dve.wait_ge(spread_done, (i + bi) * UN + (u + 1))
                        v.tensor_reduce(tmax[:, bass.ds(i * UN + u, 1), :].rearrange("p o h -> p (o h)"),
                                        PS[:, 6 + u % 2, :].rearrange("p (h e) -> p h e", h=H), X, ALU.max).then_inc(spread_used, 1)

                dve.wait_ge(slots_loaded[g], 16)
                per_turn = 2 if g == 0 else 8
                turn_base = steps[0]
                in_turn = [0]
                at = [0]

                def step(ins):
                    in_turn[0] += 1
                    ins.then_inc(dve_step, 1)
                    dve.wait_ge(dve_step, at[0] * per_turn + (in_turn[0] + turn_base))

                for b in range(NB):
                    v.tensor_scalar(others[:, b, :], block_of[g][:, :], float(b), -BIG, ALU.not_equal, ALU.mult)
                hots(0, 0)

                def turn(i, first, last_turn):
                    at[0], in_turn[0] = i, 0
                    for half in range(2):
                        if half == 0:
                            hots(i, 1)
                        elif not last_turn:
                            hots(i + 1, 0)
                        scores(i, half, 0)
                        maxima(i, half)
                    assert in_turn[0] == per_turn, in_turn

                turn(0, True, False)
                with dve.Fori(1, TILES // UN - 1) as i:
                    turn(i, False, False)
                turn(TILES // UN - 1, False, True)
                steps[0] += per_turn * (TILES // UN)

                dve.wait_ge(spread_used, (g + 1) * TILES)
                for b in range(NB):
                    then(v.tensor_tensor(comb[:, :, :], tmax[:, :, :].rearrange("p t h -> p h t"),
                                         others[:, b, :].unsqueeze(1).broadcast_to([P, H, TILES]), ALU.add))
                    ins = v.tensor_reduce(node_max[:, b, :], comb[:, :, :], X, ALU.max)
                    if b < NB - 1:
                        then(ins)
                ins.then_inc(max_ready, 1)
                dve.wait_ge(maxe_done, g + 1)
                v.tensor_tensor(score[:, :, :], score[:, :, :], PS[:, 0, 0:TILES * H].rearrange("p (t h) -> p t h", h=H), ALU.subtract)\
                    .then_inc(diff_ready, 1)
                dve.wait_ge(exp_ready, g + 1)

                def messages(i, half, guard):
                    t0 = i * UN + half * HALF
                    for u in range(half * HALF, (half + 1) * HALF):
                        if guard:
                            dve.wait_ge(summed, (i + bi) * UN + (u + 1 - UN))
                        v.tensor_scalar(hotf[:, u, :], iota16[:, 0:P], slots[g][:, bass.ds(i * UN + u, 1), 0], None, ALU.is_equal)
                    if g == 0:
                        feats, ex = rows1[:, bass.ds(t0, HALF), 4:W1], rows1[:, bass.ds(t0, HALF), 0:4]
                    else:
                        feats, ex = rows3[:, bass.ds(t0, HALF), D:W3], rows3[:, bass.ds(t0, HALF), D - 4:D]
                    feats = feats.rearrange("p t (h f) -> p t h f", h=H)
                    v.tensor_tensor(feats, feats, ex.unsqueeze(3).broadcast_to([P, HALF, H, DK]), ALU.mult).then_inc(message_ready, 1)

                for half in range(2):
                    messages(0, half, g == 1)
                with dve.Fori(1, TILES // UN) as i:
                    for half in range(2):
                        messages(i, half, True)
                dve.wait_ge(sums_done, g + 1)

            rden = small[:, 88:104].rearrange("p (b h) -> p b h", b=NB)

            def denominators(col):
                then(v.tensor_scalar(rden, PS[:, 4:8, col[0]:col[0] + col[1] * (H - 1) + 1:col[1]], 1e-30, None, ALU.max))
                then(v.reciprocal(rden, rden))

            edge_layer(0)
            denominators((0, 1))
            t1 = rows1[:, 0, 0:1]
            o1 = part(0, 1024).rearrange("p (b f) -> p b f", b=NB)
            for b in range(NB):
                ins = v.tensor_tensor(o1[:, b, :].rearrange("p (h f) -> p h f", h=H), PS[:, 4 + b, 4:W1].rearrange("p (h f) -> p h f", h=H),
                                      rden[:, b, :].unsqueeze(2).broadcast_to([P, H, DK]), ALU.mult)
            then(ins)
            then(v.tensor_tensor(o1, o1, bias1[:, :].unsqueeze(1).broadcast_to([P, NB, D]), ALU.add))
            then(v.scalar_tensor_tensor(x[:, :, :], o1, 0.0, x[:, :, :], ALU.max, ALU.add))
            layernorm(2)

            v.memset(hx[:, :, :, 64], 1.0)
            for b in range(NB):
                dve.wait_ge(h_done, b + 1)
                then(v.tensor_scalar(h_neg[:, 0:260], PS[:, 4 + b, 0:260], 0.0, None, ALU.min))
                then(v.scalar_tensor_tensor(hx[:, b, :, 0:64], PS[:, 4 + b, 0:D].rearrange("p (h f) -> p h f", h=H), 0.0,
                                            h_neg[:, 0:D].rearrange("p (h f) -> p h f", h=H), ALU.max, ALU.add))
                then(v.scalar_tensor_tensor(a_dst[:, b, :], PS[:, 4 + b, D:260], 0.0, h_neg[:, D:260], ALU.max, ALU.add))
                then(v.tensor_scalar(a_neg[:, 0, b, :], a_dst[:, b, :], -1.0, None, ALU.mult))
                v.tensor_scalar(a_neg[:, 1, b, :], a_dst[:, b, :], -0.2, None, ALU.mult).then_inc(h_moved, 1)
            for b in range(NB):
                for h in range(H):
                    n = b * H + h
                    dve.wait_ge(pexp_ready, n + 1)
                    then(v.tensor_tensor(exp_ring[:, n % 2, 0, :], exp_ring[:, n % 2, 0, :], exp_ring[:, n % 2, 1, :], ALU.min))
                    v.scalar_tensor_tensor(pair_w[:, b, h, :], exp_ring[:, n % 2, 0, :], 0.0, countT[:, b, :], ALU.max, ALU.mult).then_inc(pw_ready, 1)
            dve.wait_ge(hp_done, 1)
            denominators((64, 65))
            hp = part(0, 1024).rearrange("p (b h f) -> p b h f", b=NB, h=H)
            hp_flat = part(0, 1024)
            for b in range(NB):
                ins = v.tensor_tensor(hp[:, b, :, :], PS[:, 4 + b, 0:260].rearrange("p (h w) -> p h w", h=H)[:, :, 0:64],
                                      rden[:, b, :].unsqueeze(2).broadcast_to([P, H, DK]), ALU.mult)
            then(ins)
            v.tensor_scalar(elu_tmp[:, 0, :], hp_flat, 0.0, None, ALU.min).then_inc(elu_in, 1)
            dve.wait_ge(elu_exp, 1)
            then(v.scalar_tensor_tensor(elu_tmp[:, 2, :], hp_flat, 0.0, elu_tmp[:, 1, :], ALU.max, ALU.add))
            then(v.tensor_scalar(elu_tmp[:, 2, :], elu_tmp[:, 2, :], 1.0, None, ALU.subtract))
            v.tensor_scalar(elu_tmp[:, 0, :], elu_tmp[:, 2, :], 0.0, None, ALU.min).then_inc(elu_in, 1)
            dve.wait_ge(elu_exp, 2)
            then(v.scalar_tensor_tensor(elu_tmp[:, 2, :], elu_tmp[:, 2, :], 0.0, elu_tmp[:, 1, :], ALU.max, ALU.add))
            xf = x[:, :, :].rearrange("p b f -> p (b f)")
            then(v.scalar_tensor_tensor(xf, elu_tmp[:, 2, :], 1.0, xf, ALU.subtract, ALU.add))
            dve.wait_ge(skip_in_s, 1)
            then(v.tensor_scalar(skip_e[:, 1, :], skip_e[:, 1, :], 1.0, None, ALU.add))
            then(v.reciprocal(skip_e[:, 2, :], skip_e[:, 1, :]))
            layernorm(3)

            dve.wait_ge(xT_moved, 6)
            for t in range(TYPES):
                v.tensor_tensor(xmT[:, t, :, :], xT[:, :, :], mask[:, t, :].unsqueeze(1).broadcast_to([P, KC, N]), ALU.mult).then_inc(xm_ready, 1)
            n = 0
            for b in range(NB):
                if b >= 2:
                    dve.wait_ge(t3_written[b % 2], 16)
                for a in range(2):
                    for r in range(0, RELS, 4):
                        dve.wait_ge(rel_done, 2 * n + 2)
                        v.tensor_copy(stage[:, b % 2, r:r + 4, D + a * P:D + (a + 1) * P], PS[:, 4 + n % 2, :].rearrange("p (r w) -> p r w", r=4))\
                            .then_inc(rel_moved_v, 1)
                        n += 1
            dve.wait_ge(q_done, 1)
            then(v.tensor_copy(q_f, PS[:, 6:8, :].rearrange("p b f -> p (b f)")))
            split([parts3[:, k, :, :].rearrange("p b f -> p (b f)") for k in range(3)], q_f, q_r).then_inc(q_split, 1)
            edge_layer(1)
            denominators((0, 1))
            for b in range(NB):
                ins = v.tensor_tensor(agg[:, b, :].rearrange("p (h f) -> p h f", h=H), PS[:, 4 + b, 4:W1].rearrange("p (h f) -> p h f", h=H),
                                      rden[:, b, :].unsqueeze(2).broadcast_to([P, H, DK]), ALU.mult)
            ins.then_inc(am_ready, 1)
            dve.wait_ge(xT_moved, 8)
            for t in range(TYPES):
                for c in range(KC):
                    ins = v.scalar_tensor_tensor(amT[:, t, c, :], aggT[:, c, :], skip_e[:, 2, t:t + 1], mask[:, t, :], ALU.mult, ALU.mult)
                ins.then_inc(am_ready, 1)
            dve.wait_ge(o_done, 1)
            for b in range(NB):
                ins = v.tensor_tensor(x[:, b, :], x[:, b, :], PS[:, 2 + b // 2, (b % 2) * D:(b % 2 + 1) * D], ALU.add)
            then(ins)
            layernorm(4)


_INS = ['x', 'src', 'dst', 'edge_type_8', 'edge_weight', 'node_type_4', 'L0_gnn_W', 'L0_gnn_B', 'L1_gnn_W', 'L1_gnn_a_self',
        'L1_gnn_a_neigh', 'L1_gnn_bias', 'L2_gnn_W', 'L2_gnn_a', 'L3_gnn_k_linears', 'L3_gnn_q_linears', 'L3_gnn_v_linears',
        'L3_gnn_a_linears', 'L3_gnn_relation_att', 'L3_gnn_relation_msg', 'L3_gnn_relation_pri', 'L3_gnn_skip']


def kernel(**inputs):
    import numpy as _np
    import concourse.bacc as _bacc
    from concourse import mybir as _mybir
    from concourse.bass_utils import run_bass_kernel_spmd as _run

    nc = _bacc.Bacc("TRN2", target_bir_lowering=False, num_devices=1)
    arrays, args = {}, []
    for name in _INS:
        a = _np.ascontiguousarray(inputs[name])
        arrays[f"in_{name}_dram"] = a
        args.append(nc.dram_tensor(f"in_{name}_dram", a.shape, _mybir.dt.from_np(a.dtype), kind="ExternalInput").ap())
    args.append(nc.dram_tensor("out_0_dram", (N, D), _mybir.dt.float32, kind="ExternalOutput").ap())
    gnn_kernel(nc, *args)
    r = _run(nc, [arrays], core_ids=[0])
    return r.results[0]["out_0_dram"]
```

```python
import concourse.bass as bass
from concourse import mybir
from contextlib import ExitStack

N = 512
E = 8704
D = 256
H = 4
DK = D // H
RELS = 8
TYPES = 4
P = 128
NB = N // P
KC = D // P
EC = E // P
TILES = EC + NB
W1 = 4 + D
W3 = 2 * D
BANK = 512
HALVES = 18
UN = 8
HALF = UN // 2
assert HALVES == TILES // HALF and EC % UN == HALF
BIG = 2.0 ** 100
EPS = 1e-5
EARLY = 24


def gnn_kernel(nc, x_in, src_in, dst_in, etype_in, ew_in, ntype_in, w0_in, b0_in, w1_in, aself_in, aneigh_in,
               bias1_in, w2_in, a2_in, klin_in, qlin_in, vlin_in, alin_in, att_in, msg_in, pri_in, skip_in, out):
    f32, bf16, f16 = mybir.dt.float32, mybir.dt.bfloat16, mybir.dt.float16
    i32, u32 = mybir.dt.int32, mybir.dt.uint32
    ALU = mybir.AluOpType
    ACT = mybir.ActivationFunctionType
    UNROLLED = ()
    X = mybir.AxisListType.X
    ctx = ExitStack()
    with ctx:
        def sb(name, shape, dt):
            return ctx.enter_context(nc.sbuf_tensor(name, shape, dt))

        def sem(name):
            return ctx.enter_context(nc.semaphore(name))

        slots_src = nc.dram_tensor("slots_src", (P * TILES, 4), f32, kind="Internal").ap()
        slots_dst = nc.dram_tensor("slots_dst", (P * TILES, 4), f32, kind="Internal").ap()
        table1 = nc.dram_tensor("table1", (N, W1), f32, kind="Internal").ap()
        table3 = nc.dram_tensor("table3", (RELS * N, W3), f32, kind="Internal").ap()

        region = sb("region", [P, TILES * W3], f32)

        def part(start, size):
            return region[:, start:start + size]

        rows1 = part(0, TILES * W1).rearrange("p (t w) -> p t w", w=W1)
        rows3 = region[:, :].rearrange("p (t w) -> p t w", w=W3)
        hot_ring = part(12800, 4096).bitcast(bf16).rearrange("p (u k n) -> p u k n", u=UN, k=2)
        xb0 = part(12800, 1024).rearrange("p (b f) -> p b f", b=NB)
        adj = part(2048, 2048).rearrange("p (b n) -> p b n", b=NB)
        axT = part(4096, 1024).rearrange("p (c n) -> p c n", c=KC)
        w0_nat = part(5120, 512).rearrange("p (b i) -> p b i", b=KC)
        b0_nat = part(5632, 512).rearrange("p (b i) -> p b i", b=KC)
        w0T = part(6144, 512).rearrange("p (c o) -> p c o", c=KC)
        b0T = part(6656, 512).rearrange("p (c o) -> p c o", c=KC)
        group_tmp = part(8192, 2048)
        wa_tmp = part(10240, 256)
        abc = part(10496, 1024).rearrange("p (k f) -> p k f", k=4)
        type_row = part(11520, N).bitcast(i32)
        empty = part(12032, 4 * TILES).rearrange("p (t w) -> p t w", w=4)
        ends_f = part(12320, 2 * EC).rearrange("p (k j) -> p k j", k=2)
        edges_i = part(12456, 3 * EC).bitcast(i32).rearrange("p (k j) -> p k j", k=3)
        edge_w = part(12660, EC)
        block_f = part(12728, TILES)
        pair_w = part(0, 8192).rearrange("p (b h n) -> p b h n", b=NB, h=H)
        exp_ring = part(8192, 4096).rearrange("p (r k n) -> p r k n", r=4, k=2)
        hx = part(12288, NB * H * 65).rearrange("p (b h w) -> p b h w", b=NB, h=H)
        h_neg = part(13328, 264)
        a_dst = part(13592, 16).rearrange("p (b h) -> p b h", b=NB)
        a_neg = part(13608, 32).rearrange("p (k b h) -> p k b h", k=2, b=NB)
        elu_tmp = part(13640, 3072).rearrange("p (k f) -> p k f", k=3)
        stage = part(0, 8192).rearrange("p (k r w) -> p k r w", k=2, r=RELS)
        kT = part(12288, 1024).rearrange("p (c n) -> p c n", c=KC)
        vT = part(13312, 1024).rearrange("p (c n) -> p c n", c=KC)
        kqv = part(18720, 6144).rearrange("p (k t c o) -> p k t c o", k=3, t=TYPES, c=KC)
        att_nat = part(24864, 2048).rearrange("p (r a w) -> p r a w", r=RELS, a=2)
        countT = part(24864, 2048).rearrange("p (b n) -> p b n", b=NB)
        attT = part(26912, 2048).rearrange("p (a r w) -> p a r w", r=RELS, a=2)
        msgD = part(28960, 2048).rearrange("p (a r w) -> p a r w", r=RELS, a=2)
        count = part(31008, 2048).rearrange("p (b n) -> p b n", b=NB)
        w1x = part(33056, 528).rearrange("p (c w) -> p c w", c=KC)
        w2x = part(33584, 528).rearrange("p (c w) -> p c w", c=KC)
        feat1 = part(34112, 1056).rearrange("p (b w) -> p b w", b=NB)
        xT = part(35168, 1024).rearrange("p (c n) -> p c n", c=KC)
        pri_bc = part(36192, 32)
        payload = [part(36224 + g * 4 * EC, 4 * EC).rearrange("p (j w) -> p j w", w=4) for g in range(2)]
        xmT = part(31008, 4096).rearrange("p (t c n) -> p t c n", t=TYPES, c=KC)
        q_f = part(22816, 1024)
        q_r = part(23840, 1024)
        LATE = 20768 // W3
        agg = part(0, 1024).rearrange("p (b f) -> p b f", b=NB)
        aggT = part(1024, 1024).rearrange("p (c n) -> p c n", c=KC)
        amT = part(2048, 4096).rearrange("p (t c n) -> p t c n", t=TYPES, c=KC)

        identf = sb("identf", [P, P], f32)
        identb = sb("identb", [P, P], bf16)
        bigI = sb("bigI", [P, P], bf16)
        before = sb("before", [P, P], bf16)
        onesb = sb("onesb", [P, P], bf16)
        ones_f = sb("ones_f", [P, 72], f32)
        zerob = sb("zerob", [P, W1], bf16)
        iota16 = sb("iota16", [P, N], f16)
        tile_at = sb("tile_at", [P, TILES], f32)
        x = sb("x", [P, NB, D], f32)
        alin = sb("alin", [P, TYPES, KC, D], f32)
        mask = sb("mask", [P, TYPES, N], bf16)
        bias1 = sb("bias1", [P, D], f32)
        skip_e = sb("skip_e", [P, 3, TYPES], f32)
        address = [sb(f"address{g}", [P, EC], u32) for g in range(2)]
        slots = [sb(f"slots{g}", [P, TILES, 4], f32) for g in range(2)]
        block_of = [sb(f"block_of{g}", [P, TILES], i32) for g in range(2)]
        others = sb("others", [P, NB, TILES], f32)
        hotT = sb("hotT", [P, TILES, P], bf16)
        hotm1 = sb("hotm1", [P, UN, P], bf16)
        hotf = sb("hotf", [P, UN, P], f32)
        score = sb("score", [P, TILES, H], f32)
        score_s = sb("score_s", [P, UN, H], f32)
        score_b = sb("score_b", [P, UN, H], bf16)
        zt = sb("zt", [P, 2, HALF * H], f32)
        tmax = sb("tmax", [P, TILES, H], f32)
        comb = sb("comb", [P, H, TILES], f32)
        node_max = sb("node_max", [P, NB, H], f32)
        tile_max = sb("tile_max", [P, TILES, H], bf16)
        parts3 = sb("parts3", [P, 3, NB, D], bf16)
        self3 = parts3[:, :, :, :].rearrange("p k b f -> p (k b f)")[:, 0:3 * TILES * H].rearrange("p (k t h) -> p k t h", k=3, h=H)
        prod = sb("prod", [P, 2, D], f32)
        small = sb("small", [P, 128], f32)
        PS = ctx.enter_context(nc.psum_tensor("PS", [P, 8, BANK], f32))
        sums = PS[:, 4:8, :].rearrange("p b f -> p (b f)")

        loads = {n: sem("loaded_" + n) for n in
                 "edges x w0 w1 w2 kqv rel alin types".split()}
        fixed = sem("constants_made")
        pool_step = sem("pool_step")
        dve_step = sem("dve_step")
        act_step = sem("act_step")
        prefilled = sem("slots_prefilled")
        totals_ready = sem("group_totals_ready")
        prefix_done = sem("group_prefix_done")
        address_ready = sem("addresses_ready")
        scattered = [[sem(f"scattered{g}_{u}") for u in range(4)] for g in range(2)]
        slots_loaded = [sem(f"slots_loaded{g}") for g in range(2)]
        gathered = [[sem(f"gathered{g}_{u}") for u in range(4)] for g in range(2)]
        ends_ready = sem("edge_ends_ready")
        hots_ready = sem("one_hots_ready")
        hots_used = sem("one_hots_used")
        prep_done = sem("prep_transposed")
        prep_moved = sem("prep_moved")
        att_done = sem("att_transposed")
        att_moved = sem("att_moved")
        bx_done = sem("xB_done")
        count_moved = sem("counts_moved")
        adj_ready = sem("adjacency_ready")
        ax_done = sem("adj_x_done")
        ax_moved = sem("adj_x_moved")
        l0_done = sem("layer0_products_done")
        var_ready = sem("variances_ready")
        std_ready = sem("deviations_ready")
        x_ready = sem("x_ready")
        xT_done = sem("xT_done")
        xT_moved = sem("xT_moved")
        feat_done = sem("features_done")
        feat_moved = sem("features_moved")
        table1_written = sem("table1_written")
        self_split = sem("self_scores_split")
        cT_done = sem("counts_transposed")
        cT_moved = sem("countsT_moved")
        hotm1_ready = sem("hotm1_ready")
        hotT_done = sem("hotT_transposed")
        hotT_moved = sem("hotT_moved")
        near_done = sem("own_node_gathered")
        near_used = sem("own_node_used")
        score_ready = sem("scores_ready")
        spread_done = sem("scores_spread")
        spread_used = sem("maxima_taken")
        max_ready = sem("node_maxima_ready")
        maxe_done = sem("maxima_on_edges")
        diff_ready = sem("differences_ready")
        exp_ready = sem("exponentials_ready")
        message_ready = sem("messages_ready")
        hotf_ready = sem("hotf_ready")
        summed = sem("messages_summed")
        sums_done = sem("sums_done")
        wx_ready = sem("weight_vectors_ready")
        h_done = sem("h_done")
        spread2_done = sem("source_scores_spread")
        h_moved = sem("h_moved")
        pexp_ready = sem("pair_exp_ready")
        pmin_ready = sem("pair_minima_for_pool")
        pw_by_pool = sem("pair_weights_by_pool")
        pw_ready = sem("pair_weights_ready")
        hp_done = sem("pair_sums_done")
        elu_in = sem("elu_arguments_ready")
        elu_exp = sem("elu_exp_ready")
        xm_ready = sem("typed_x_ready")
        kv_done = sem("keys_values_done")
        kv_moved = sem("keys_values_moved")
        q_done = sem("queries_done")
        q_split = sem("queries_split")
        rel_done = sem("relation_products_done")
        rel_moved_a = sem("relation_products_moved_act")
        rel_moved_v = sem("relation_products_moved_dve")
        t3_written = [sem(f"table3_written{k}") for k in range(2)]
        skip_in_s = sem("skip_exp_ready")
        am_ready = sem("typed_sums_ready")
        o_done = sem("output_products_done")
        out_written = sem("output_written")

        block = ctx.enter_context(nc.Block())

        def turns(engine, first, end):
            if engine.engine in UNROLLED:
                yield from range(first, end)
            else:
                with engine.Fori(first, end) as i:
                    yield i

        def pair_weights_done(engine, n):
            if n % 3 == 2:
                engine.wait_ge(pw_by_pool, n // 3 + 1)
            else:
                engine.wait_ge(pw_ready, n - n // 3 + 1 - (n % 3 == 2))

        @block.sync
        def _(sp):
            for k, a in enumerate((src_in, dst_in, etype_in)):
                sp.dma_start(edges_i[:, k, :], a.rearrange("(p j) -> p j", p=P)).then_inc(loads["edges"], 16)
            sp.dma_start(edge_w, ew_in.rearrange("(p j) -> p j", p=P)).then_inc(loads["edges"], 16)
            sp.dma_start(x[:, :, :], x_in.rearrange("(b p) f -> p b f", p=P)).then_inc(loads["x"], 16)
            sp.dma_start(w0_nat, w0_in.rearrange("(b p) i -> p b i", p=P)).then_inc(loads["w0"], 16)
            sp.dma_start(b0_nat, b0_in.rearrange("(b p) i -> p b i", p=P)).then_inc(loads["w0"], 16)
            for c in range(KC):
                sp.dma_start(w1x[:, c, 4:4 + D].rearrange("p (h o) -> p h o", h=H),
                             w1_in[:, c * P:(c + 1) * P, :].rearrange("h p o -> p h o")).then_inc(loads["w1"], 16)
                sp.dma_start(w2x[:, c, 0:D].rearrange("p (h o) -> p h o", h=H),
                             w2_in[:, c * P:(c + 1) * P, :].rearrange("h p o -> p h o")).then_inc(loads["w2"], 16)
            sp.dma_start(abc[:, 0, :], aneigh_in.rearrange("(o h) f -> o (h f)", o=1).broadcast_to([P, D])).then_inc(loads["w1"], 16)
            sp.dma_start(abc[:, 1, :], aself_in.rearrange("(o h) f -> o (h f)", o=1).broadcast_to([P, D])).then_inc(loads["w1"], 16)
            sp.dma_start(abc[:, 2:4, :], a2_in.rearrange("h o f -> o (h f)").broadcast_to([P, 2 * D])).then_inc(loads["w2"], 16)
            sp.dma_start(bias1[:, :], bias1_in.rearrange("(o h) f -> o (h f)", o=1).broadcast_to([P, D])).then_inc(loads["w1"], 16)
            for k, a in enumerate((klin_in, qlin_in, vlin_in)):
                sp.dma_start(kqv[:, k, :, :, :], a.rearrange("t (c p) o -> p t c o", p=P)).then_inc(loads["kqv"], 16)
            sp.wait_ge(pool_step, 7)
            for h in range(H):
                a, s = h // 2, (h % 2) * DK
                sp.dma_start(att_nat[s:s + DK, :, a, s:s + DK], att_in[:, h, :, :].rearrange("r d e -> d r e")).then_inc(loads["rel"], 16)
                sp.dma_start(msgD[s:s + DK, a, :, s:s + DK], msg_in[:, h, :, :].rearrange("r d e -> d r e")).then_inc(loads["rel"], 16)
            sp.dma_start(pri_bc, pri_in.rearrange("(o r) h -> o (r h)", o=1).broadcast_to([P, RELS * H])).then_inc(loads["rel"], 16)
            sp.dma_start(alin[:, :, :, :], alin_in.rearrange("t (c p) o -> p t c o", p=P)).then_inc(loads["alin"], 16)
            sp.dma_start(type_row, ntype_in.rearrange("(o n) -> o n", o=1).broadcast_to([P, N])).then_inc(loads["types"], 16)
            sp.dma_start(skip_e[:, 0, :], skip_in.rearrange("(o n) -> o n", o=1).broadcast_to([P, TYPES])).then_inc(loads["types"], 16)

            for g, table in ((0, slots_src), (1, slots_dst)):
                if g == 1:
                    sp.wait_ge(feat_moved, NB)
                    sp.dma_start(table1.rearrange("(b p) w -> p b w", p=P), feat1[:, :, 0:W1]).then_inc(table1_written, 16)
                for u in range(4):
                    sp.wait_ge(scattered[g][u], 16 * (EC // 4))
                sp.dma_start(slots[g][:, :, :], table.rearrange("(p t) w -> p t w", p=P)).then_inc(slots_loaded[g], 16)
            t3 = table3.rearrange("(r b p) w -> p b r w", p=P, b=NB)
            for b in range(NB):
                sp.wait_ge(rel_moved_a, 4 * (b + 1))
                sp.wait_ge(rel_moved_v, 4 * (b + 1))
                sp.dma_start(t3[:, b, :, :], stage[:, b % 2, :, :]).then_inc(t3_written[b % 2], 16)
            sp.wait_ge(x_ready, 4 * NB)
            sp.dma_start(out.rearrange("(b p) f -> p b f", p=P), x[:, :, :]).then_inc(out_written, 16)
            sp.wait_ge(out_written, 16)

        @block.gpsimd
        def _(pool):
            pool.memset(identf[:, :], 0.0).then_inc(pool_step, 1)
            pool.memset(empty[:, :, :], 0.0).then_inc(pool_step, 1)
            pool.memset(before[:, :], 0.0).then_inc(pool_step, 1)
            pool.wait_ge(pool_step, 3)
            pool.memset(empty[:, :, 0], -1.0).then_inc(pool_step, 1)
            pool.affine_select(out=identf[:, :], in_=identf[:, :], compare_op=ALU.not_equal, fill=1.0, base=0,
                               pattern=[[-1, P]], channel_multiplier=1).then_inc(pool_step, 1)
            pool.affine_select(out=before[:, :], in_=before[:, :], compare_op=ALU.is_ge, fill=1.0, base=0,
                               pattern=[[-1, P]], channel_multiplier=1).then_inc(fixed, 1)
            pool.memset(onesb[:, :], 1.0).then_inc(fixed, 1)
            pool.memset(ones_f[:, :], 1.0).then_inc(fixed, 1)
            pool.memset(zerob[:, :], 0.0).then_inc(fixed, 1)
            pool.iota(iota16[:, :], pattern=[[1, N]], base=0, channel_multiplier=0,
                      allow_small_or_imprecise_dtypes=True).then_inc(fixed, 1)
            pool.iota(tile_at[:, :], pattern=[[P, TILES]], base=0, channel_multiplier=0,
                      allow_small_or_imprecise_dtypes=True).then_inc(fixed, 1)
            pool.wait_ge(pool_step, 5)
            pool.tensor_copy(identb[:, :], identf[:, :]).then_inc(fixed, 1)
            pool.tensor_scalar(bigI[:, :], identf[:, :], BIG, None, ALU.mult).then_inc(fixed, 1)
            for table in (slots_src, slots_dst):
                pool.dma_start(table.rearrange("(p t) w -> p t w", p=P), empty[:, :, :]).then_inc(prefilled, 16)
            for nat in (att_nat, msgD):
                pool.memset(nat, 0.0).then_inc(pool_step, 1)

            def scatter(g, table, j):
                if j >= 4:
                    pool.wait_ge(scattered[g][j % 4], 16 * (j // 4))
                pool.indirect_dma_start(out=table, out_offset=bass.IndirectOffsetOnAxis(ap=address[g][:, j:j + 1], axis=0),
                                        in_=payload[g][:, j, :], in_offset=None).then_inc(scattered[g][j % 4], 16)

            def gather(g, table, rows, t):
                if t >= 4:
                    pool.wait_ge(gathered[g][t % 4], 16 * (t // 4))
                pool.indirect_dma_start(out=rows[:, t, :], out_offset=None, in_=table,
                                        in_offset=bass.IndirectOffsetOnAxis(ap=slots[g][:, t, 1:2].bitcast(u32), axis=0))\
                    .then_inc(gathered[g][t % 4], 16)

            pool.wait_ge(prefilled, 32)
            pool.wait_ge(address_ready, 1)
            for j in range(EC):
                scatter(0, slots_src, j)
            pool.wait_ge(address_ready, 2)
            for j in range(EARLY):
                scatter(1, slots_dst, j)
            pool.wait_ge(slots_loaded[0], 16)
            pool.wait_ge(table1_written, 16)
            for t in range(TILES):
                gather(0, table1, rows1, t)
            for j in range(EARLY, EC):
                scatter(1, slots_dst, j)
            for n in range(2, NB * H, 3):
                pool.wait_ge(pmin_ready, n // 3 + 1)
                pool.tensor_tensor(pair_w[:, n // H, n % H, :], exp_ring[:, n % 4, 0, :], countT[:, n // H, :], ALU.mult).then_inc(pw_by_pool, 1)
            pool.wait_ge(slots_loaded[1], 16)
            pool.wait_ge(t3_written[0], 32)
            pool.wait_ge(t3_written[1], 32)
            for t in range(TILES):
                if t == LATE:
                    pool.wait_ge(q_split, 1)
                gather(1, table3, rows3, t)

        @block.tensor
        def _(pe):
            def blocks_of(g, t0):
                return nc.values_load_multi_w_load_instructions(
                    block_of[g][0:1, bass.ds(t0, HALF)], engines=(mybir.EngineType.PE,), min_val=0, max_val=NB - 1,
                    skip_runtime_bounds_check_because="a sum of three comparisons, each 0 or 1")[1]

            def transposes(source, banks, done, waits=()):
                for c in range(KC):
                    for b in range(NB):
                        last = nc.tensor.transpose(PS[:, banks[c], b * P:(b + 1) * P], source[:, b, c * P:(c + 1) * P], identf[:, :])
                    last.then_inc(done, 1)

            def group_prefix(bank):
                nc.tensor.matmul(PS[:, bank, 0:4], before[:, :], small[:, 0:2].bitcast(bf16), start=True, stop=True)
                nc.tensor.matmul(PS[:, bank, 4:8], onesb[:, :], small[:, 0:2].bitcast(bf16), start=True, stop=True).then_inc(prefix_done, 1)

            pe.wait_ge(fixed, 8)
            pe.wait_ge(totals_ready, 1)
            def count_turn(i, first, n=UN):
                for u in range(n):
                    pe.wait_ge(hots_ready, i * UN + (u + 1))
                    for b in range(NB):
                        ins = nc.tensor.matmul(PS[:, b, :], hot_ring[:, u, 0, b * P:(b + 1) * P], hot_ring[:, u, 1, :],
                                               start=(first and u == 0), stop=(n < UN and u == n - 1), skip_group_check=True)
                    ins.then_inc(hots_used, 1)

            count_turn(0, True)
            pe.wait_ge(totals_ready, 1)
            group_prefix(4)
            for i in turns(pe, 1, EC // UN):
                count_turn(i, False)
            count_turn(EC // UN, False, EC % UN)
            pe.wait_ge(loads["x"], 16)
            transposes(x, (5, 6), prep_done)
            pe.wait_ge(loads["w0"], 32)
            for nat, bank in ((w0_nat, 7), (b0_nat, 4)):
                if bank == 4:
                    pe.wait_ge(address_ready, 1)
                for c in range(KC):
                    for b in range(KC):
                        last = nc.tensor.transpose(PS[:, bank, c * D + b * P:c * D + (b + 1) * P], nat[:, b, c * P:(c + 1) * P], identf[:, :])
                last.then_inc(prep_done, 1)
            pe.wait_ge(count_moved, NB)
            for d in range(NB):
                for b in range(NB):
                    nc.tensor.matmul(PS[:, 2, d:d + 1], count[:, b, d * P:(d + 1) * P], ones_f[:, 0:1], start=(b == 0), stop=(b == NB - 1))
            pe.wait_ge(totals_ready, 2)
            group_prefix(3)
            pe.wait_ge(prep_moved, 4)
            for b in range(NB):
                for c in range(KC):
                    last = nc.tensor.matmul(PS[:, 6 + b // 2, (b % 2) * D:(b % 2 + 1) * D], xT[:, c, b * P:(b + 1) * P], b0T[:, c, :],
                                            start=(c == 0), stop=(c == KC - 1))
            last.then_inc(bx_done, 1)
            pe.wait_ge(adj_ready, NB)
            for c in range(KC):
                for b in range(NB):
                    last = nc.tensor.matmul(PS[:, 4 + c, :], x[:, b, c * P:(c + 1) * P], adj[:, b, :], start=(b == 0), stop=(b == NB - 1))
                last.then_inc(ax_done, 1)
            pe.wait_ge(ax_moved, 2)
            for b in range(NB):
                for c in range(KC):
                    last = nc.tensor.matmul(PS[:, b // 2, (b % 2) * D:(b % 2 + 1) * D], axT[:, c, b * P:(b + 1) * P], w0T[:, c, :],
                                            start=(c == 0), stop=(c == KC - 1))
                if b % 2:
                    last.then_inc(l0_done, 1)

            def mask_group(g, q, first=False):
                n = q + g * HALVES
                for half in range(2):
                    pe.wait_ge(hotm1_ready, n + (g * HALVES + half + 1))
                    if not first:
                        pe.wait_ge(hotT_moved, n + (half - 1))
                    for u in range(HALF):
                        last = nc.tensor.transpose(PS[:, half, :].bitcast(bf16)[:, u * P:(u + 1) * P], hotm1[:, half * HALF + u, :], identb[:, :])
                    last.then_inc(hotT_done, 1)

            pe.wait_ge(x_ready, NB)
            transposes(x, (4, 5), xT_done)
            pe.wait_ge(xT_moved, 2)
            pe.wait_ge(wx_ready, 4 * KC)
            for b in range(NB):
                for c in range(KC):
                    last = nc.tensor.matmul(PS[:, b, 0:264], xT[:, c, b * P:(b + 1) * P], w1x[:, c, :], start=(c == 0), stop=(c == KC - 1))
                last.then_inc(feat_done, 1)
            pe.wait_ge(feat_moved, NB)
            mask_group(0, 0, True)
            for i in turns(pe, 1, TILES // UN):
                mask_group(0, i * 2)
            pe.wait_ge(loads["rel"], 16 * 9)
            for n in range(4):
                if n >= 2:
                    pe.wait_ge(att_moved, n - 1)
                for k in range(4):
                    last = nc.tensor.transpose(PS[:, 6 + n % 2, k * P:(k + 1) * P], att_nat[:, (n % 2) * 4 + k, n // 2, :], identf[:, :])
                last.then_inc(att_done, 1)
            pe.wait_ge(att_moved, 4)
            for d in range(NB):
                if d >= 2:
                    pe.wait_ge(cT_moved, d - 1)
                for b in range(NB):
                    last = nc.tensor.transpose(PS[:, 6 + d % 2, b * P:(b + 1) * P], count[:, b, d * P:(d + 1) * P], identf[:, :])
                last.then_inc(cT_done, 1)

            def edge_layer(g):
                bi = g * TILES // UN

                def near(s):
                    half = s % 2
                    if g == 1:
                        block = blocks_of(g, s * HALF)
                        if s >= 2:
                            pe.wait_ge(near_used, HALVES + 2 * (s - 1))
                    elif s >= 2:
                        pe.wait_ge(near_used, s - 1)
                    for u in range(HALF):
                        t = s * HALF + u
                        if g == 0:
                            dst = PS[:, 2 + half, u * H:(u + 1) * H]
                        else:
                            dst = PS[:, 2 + half * 2 + u // 2, (u % 2) * D:(u % 2 + 1) * D]
                        for k in range(3):
                            rhs = self3[:, k, t, :] if g == 0 else parts3[:, k, bass.ds(block[u], 1), :].rearrange("p o w -> p (o w)")
                            last = nc.tensor.matmul(dst, hotT[:, t, :], rhs, start=(k == 0), stop=(k == 2), skip_group_check=True)
                        if u == HALF - 1 or (g == 1 and u % 2):
                            last.then_inc(near_done, 1)

                def spread(s):
                    pe.wait_ge(score_ready, g * HALVES + s + 1)
                    pe.wait_ge(hotm1_ready, (2 * g + 1) * HALVES + s + 1)
                    for u in range(HALF):
                        t = s * HALF + u + g * TILES
                        if t >= 2:
                            pe.wait_ge(spread_used, t - 1)
                        r = (s % 2) * HALF + u
                        bank = PS[:, 6 + t % 2, :].rearrange("p (h e) -> p h e", h=H)
                        nc.tensor.matmul(bank, hotm1[:, r, :], bigI[:, :].unsqueeze(1).broadcast_to([P, H, P]), start=True, stop=False,
                                         skip_group_check=True)
                        for h in range(H):
                            last = nc.tensor.matmul(bank[:, h, :], score_b[:, r, h:h + 1].broadcast_to([P, P]), identb[:, :],
                                                    start=False, stop=(h == H - 1), skip_group_check=True)
                        last.then_inc(spread_done, 1)

                pe.wait_ge(hotT_moved, (g + 1) * HALVES)
                near(0)
                for s in range(HALVES):
                    if s + 1 < HALVES:
                        near(s + 1)
                    spread(s)

                pe.wait_ge(max_ready, g + 1)

                for t in range(TILES):
                    last = nc.tensor.matmul(PS[:, 0, t * H:(t + 1) * H], hotT[:, t, :], tile_max[:, t, :], start=True, stop=True,
                                            skip_group_check=True)
                last.then_inc(maxe_done, 1)
                for b in range(NB):
                    nc.tensor.matmul(PS[:, 4 + b, 0:W1], onesb[:, :], zerob[:, :], start=True, stop=False, skip_group_check=True)

                def sums_turn(i):
                    for u in range(UN):
                        if u % HALF == 0:
                            block = blocks_of(g, i * UN + u)
                            pe.wait_ge(message_ready, (i + bi) * 2 + (u // HALF + 1))
                        src = rows1[:, bass.ds(i * UN + u, 1), :] if g == 0 else rows3[:, bass.ds(i * UN + u, 1), D - 4:W3]
                        nc.tensor.matmul(sums[:, bass.ds(block[u % HALF] * BANK, W1)], hotf[:, u, :], src.rearrange("p o w -> p (o w)"),
                                         start=False, stop=False, skip_group_check=True).then_inc(summed, 1)

                for i in turns(pe, 0, TILES // UN):
                    sums_turn(i)
                for b in range(NB):
                    last = nc.tensor.matmul(PS[:, 4 + b, 0:W1], onesb[:, :], zerob[:, :], start=False, stop=True, skip_group_check=True)
                last.then_inc(sums_done, 1)

            pe.wait_ge(self_split, 1)
            pe.wait_ge(cT_moved, 4)
            edge_layer(0)

            pe.wait_ge(x_ready, 2 * NB)
            transposes(x, (0, 1), xT_done)
            pe.wait_ge(xT_moved, 4)
            for h in range(H):
                for c in range(KC):
                    last = nc.tensor.matmul(PS[:, h, :], w2x[:, c, 260 + h:261 + h].broadcast_to([P, P]), xT[:, c, :],
                                            start=(c == 0), stop=(c == KC - 1))
                last.then_inc(spread2_done, 1)
                b = h
                for c in range(KC):
                    last = nc.tensor.matmul(PS[:, 4 + b, 0:260], xT[:, c, b * P:(b + 1) * P], w2x[:, c, 0:260], start=(c == 0), stop=(c == KC - 1))
                last.then_inc(h_done, 1)
            pe.wait_ge(h_moved, NB)
            for b in range(NB):
                for h in range(H):
                    pair_weights_done(pe, b * H + h)
                    for s in range(NB):
                        last = nc.tensor.matmul(PS[:, 4 + s, h * 65:(h + 1) * 65], pair_w[:, b, h, s * P:(s + 1) * P], hx[:, b, h, :],
                                                start=(b == 0 and h == 0), stop=(b == NB - 1 and h == H - 1), skip_group_check=True)
            last.then_inc(hp_done, 1)

            pe.wait_ge(x_ready, 3 * NB)
            transposes(x, (0, 1), xT_done)
            pe.wait_ge(loads["kqv"], 48)
            group = 0
            for k, bank in ((0, 4), (2, 2)):
                for o in range(KC):
                    for t in range(TYPES):
                        pe.wait_ge(xm_ready, t + 1)
                        for c in range(KC):
                            last = nc.tensor.matmul(PS[:, bank + o, :], kqv[:, k, t, c, o * P:(o + 1) * P], xmT[:, t, c, :],
                                                    start=(t == 0 and c == 0), stop=(t == TYPES - 1 and c == KC - 1))
                        if t == TYPES - 1:
                            last.then_inc(kv_done, 1)
                        if t % 2 and group < HALVES // 2:
                            if group == 0:
                                pe.wait_ge(xT_moved, 6)
                            mask_group(1, 2 * group)
                            group += 1
            mask_group(1, 2 * group)
            pe.wait_ge(kv_moved, 4)
            pe.wait_ge(hotT_moved, 2 * HALVES)
            n = 0
            for b in range(NB):
                for a in range(2):
                    for r in range(0, RELS, 4):
                        if n >= 2:
                            pe.wait_ge(rel_moved_a, n - 1)
                        nc.tensor.matmul(PS[:, n % 2, :], kT[:, a, b * P:(b + 1) * P], attT[:, a, r:r + 4, :].rearrange("p r w -> p (r w)"),
                                         start=True, stop=True).then_inc(rel_done, 1)
                        if n >= 2:
                            pe.wait_ge(rel_moved_v, n - 1)
                        nc.tensor.matmul(PS[:, 4 + n % 2, :], vT[:, a, b * P:(b + 1) * P], msgD[:, a, r:r + 4, :].rearrange("p r w -> p (r w)"),
                                         start=True, stop=True).then_inc(rel_done, 1)
                        n += 1
            for b in range(NB):
                for t in range(TYPES):
                    for c in range(KC):
                        last = nc.tensor.matmul(PS[:, 6 + b // 2, (b % 2) * D:(b % 2 + 1) * D], xmT[:, t, c, b * P:(b + 1) * P], kqv[:, 1, t, c, :],
                                                start=(t == 0 and c == 0), stop=(t == TYPES - 1 and c == KC - 1))
            last.then_inc(q_done, 1)
            pe.wait_ge(q_split, 1)
            pe.wait_ge(rel_moved_a, 16)
            pe.wait_ge(rel_moved_v, 16)
            edge_layer(1)
            pe.wait_ge(am_ready, 1)
            transposes(agg, (0, 1), xT_done)
            pe.wait_ge(loads["alin"], 16)
            for t in range(TYPES):
                pe.wait_ge(am_ready, t + 2)
                for b in range(NB):
                    for c in range(KC):
                        last = nc.tensor.matmul(PS[:, 2 + b // 2, (b % 2) * D:(b % 2 + 1) * D], amT[:, t, c, b * P:(b + 1) * P], alin[:, t, c, :],
                                                start=(t == 0 and c == 0 and b % 2 == 0), stop=(t == TYPES - 1 and c == KC - 1), skip_group_check=True)
            last.then_inc(o_done, 1)

        @block.scalar
        def _(act):
            def copy(dst, src, done, n=1):
                nc.scalar.activation(dst, src, ACT.Copy).then_inc(done, n)

            act.wait_ge(hots_used, EC)
            for b in range(NB):
                copy(count[:, b, :], PS[:, b, :], count_moved)
            for n, (dst, bank) in enumerate(((xT[:, 0, :], 5), (xT[:, 1, :], 6), (w0T.rearrange("p c o -> p (c o)"), 7),
                                             (b0T.rearrange("p c o -> p (c o)"), 4))):
                act.wait_ge(prep_done, n + 1)
                copy(dst, PS[:, bank, :], prep_moved)
            for c in range(KC):
                act.wait_ge(ax_done, c + 1)
                copy(axT[:, c, :], PS[:, 4 + c, :], ax_moved)

            def deviations(k):
                act.wait_ge(var_ready, k)
                nc.scalar.activation(small[:, 64:68], small[:, 60:64], ACT.Sqrt).then_inc(std_ready, 1)

            def move_xT(k, banks):
                dst = aggT if k == 4 else xT
                for c in range(KC):
                    act.wait_ge(xT_done, 2 * (k - 1) + c + 1)
                    copy(dst[:, c, :], PS[:, banks[c], :], xT_moved)

            def move_hotT(g, q):
                for half in range(2):
                    act.wait_ge(hotT_done, q + (g * HALVES + half + 1))
                    nc.scalar.activation(hotT[:, bass.ds((q + half) * HALF, HALF), :].rearrange("p t n -> p (t n)"),
                                         PS[:, half, :].bitcast(bf16)[:, 0:HALF * P], ACT.Copy, bias=1.0).then_inc(hotT_moved, 1)

            def edge_layer(g):
                act.wait_ge(diff_ready, g + 1)
                dst = rows1[:, :, 0:4] if g == 0 else rows3[:, :, D - 4:D]
                nc.scalar.activation(dst, score[:, :, :], ACT.Exp).then_inc(exp_ready, 1)

            deviations(1)
            move_xT(1, (4, 5))
            for b in range(NB):
                act.wait_ge(feat_done, b + 1)
                copy(feat1[:, b, :], PS[:, b, 0:264], feat_moved)
            for i in turns(act, 0, TILES // UN):
                move_hotT(0, i * 2)
            act.wait_ge(att_moved, 4)
            for d in range(NB):
                act.wait_ge(cT_done, d + 1)
                copy(countT[:, d, :], PS[:, 6 + d % 2, :], cT_moved)
            edge_layer(0)
            deviations(2)
            move_xT(2, (0, 1))
            act.wait_ge(h_moved, NB)
            for b in range(NB):
                for h in range(H):
                    n = b * H + h
                    if n < H:
                        act.wait_ge(spread2_done, h + 1)
                    if n >= 4:
                        pair_weights_done(act, n - 4)
                    nc.scalar.activation(exp_ring[:, n % 4, 0, :], PS[:, h, :], ACT.Exp, bias=a_neg[:, 0, b, h:h + 1], scale=-1.0)
                    nc.scalar.activation(exp_ring[:, n % 4, 1, :], PS[:, h, :], ACT.Exp, bias=a_neg[:, 1, b, h:h + 1], scale=-0.2).then_inc(pexp_ready, 1)
            for k in range(2):
                act.wait_ge(elu_in, k + 1)
                nc.scalar.activation(elu_tmp[:, 1, :], elu_tmp[:, 0, :], ACT.Exp).then_inc(elu_exp, 1)
            act.wait_ge(loads["types"], 32)
            nc.scalar.activation(skip_e[:, 1, :], skip_e[:, 0, :], ACT.Exp, scale=-1.0).then_inc(skip_in_s, 1)
            deviations(3)
            move_xT(3, (0, 1))
            for n, dst in enumerate((kT[:, 0, :], kT[:, 1, :], vT[:, 0, :], vT[:, 1, :])):
                for q in range(4 * n, 4 * n + 4, 2):
                    move_hotT(1, q)
                act.wait_ge(kv_done, n + 1)
                copy(dst, PS[:, (4, 5, 2, 3)[n], :], kv_moved)
            move_hotT(1, HALVES - 2)
            n = 0
            for b in range(NB):
                if b >= 2:
                    act.wait_ge(t3_written[b % 2], 16)
                for a in range(2):
                    for r in range(0, RELS, 4):
                        act.wait_ge(rel_done, 2 * n + 1)
                        copy(stage[:, b % 2, r:r + 4, a * P:(a + 1) * P], PS[:, n % 2, :].rearrange("p (r w) -> p r w", r=4), rel_moved_a)
                        n += 1
            edge_layer(1)
            move_xT(4, (0, 1))
            deviations(4)

        @block.vector
        def _(dve):
            v = nc.vector
            steps = [0]

            def then(ins):
                steps[0] += 1
                ins.then_inc(dve_step, 1)
                dve.wait_ge(dve_step, steps[0])

            def grouping(g, half, bank):
                key = edges_i[:, g, :]
                T = group_tmp
                ind = T[:, 0:272].rearrange("p (k j) -> p k j", k=NB)
                scan = T[:, 272:544].rearrange("p (k j) -> p k j", k=NB)
                tmp = T[:, 544:816].rearrange("p (k j) -> p k j", k=NB)
                loc_i = T[:, 816:884].bitcast(i32)
                blk_i = T[:, 884:952].bitcast(i32)
                pos_i = T[:, 952:1020].bitcast(i32)
                low_i = T[:, 1020:1088].bitcast(i32)
                pad_i = T[:, 1088:1092].bitcast(i32)
                pad_j = T[:, 1092:1096].bitcast(i32)
                pad_f = T[:, 1096:1100]
                start = T[:, 1100:1104]
                base = T[:, 1104:1108]
                if half == 0:
                    group_totals(g, key, ind, scan, loc_i, blk_i)
                    return
                dve.wait_ge(prefix_done, g + 1)
                then(v.tensor_scalar(pad_i, PS[:, bank, 4:8], float(P - 1), None, ALU.add))
                then(v.tensor_scalar(pad_j, pad_i, -P, None, ALU.bitwise_and))
                then(v.tensor_copy(pad_f, pad_j))
                then(v.memset(start[:, 0:1], 0.0))
                for k in range(1, NB):
                    then(v.tensor_tensor(start[:, k:k + 1], start[:, k - 1:k], pad_f[:, k - 1:k], ALU.add))
                then(v.scalar_tensor_tensor(base, PS[:, bank, 0:4], -1.0, start, ALU.add, ALU.add))
                for k in range(NB):
                    ins = v.scalar_tensor_tensor(tmp[:, k, :], scan[:, k, :], base[:, k:k + 1], ind[:, k, :], ALU.add, ALU.mult)
                then(ins)
                then(v.tensor_tensor(tmp[:, 0:2, :], tmp[:, 0:2, :], tmp[:, 2:4, :], ALU.add))
                then(v.tensor_tensor(pos_i, tmp[:, 0, :], tmp[:, 1, :], ALU.add))
                then(v.tensor_scalar(low_i, pos_i, P - 1, None, ALU.bitwise_and))
                then(v.tensor_scalar(blk_i, pos_i, 7, None, ALU.arith_shift_right))
                v.scalar_tensor_tensor(address[g][:, :], low_i, float(TILES), blk_i, ALU.mult, ALU.add).then_inc(address_ready, 1)
                then(v.tensor_scalar(block_f, tile_at[:, :], start[:, 1:2], None, ALU.is_ge))
                then(v.scalar_tensor_tensor(block_f, tile_at[:, :], start[:, 2:3], block_f, ALU.is_ge, ALU.add))
                then(v.scalar_tensor_tensor(block_f, tile_at[:, :], start[:, 3:4], block_f, ALU.is_ge, ALU.add))
                then(v.tensor_copy(block_of[g][:, :], block_f))

            def group_totals(g, key, ind, scan, loc_i, blk_i):
                v.tensor_scalar(loc_i, key, P - 1, None, ALU.bitwise_and)
                v.memset(payload[g][:, :, 3], 0.0)
                then(v.tensor_scalar(blk_i, key, 7, None, ALU.arith_shift_right))
                v.tensor_copy(payload[g][:, :, 0], loc_i)
                if g == 0:
                    v.tensor_copy(payload[g][:, :, 1].bitcast(i32), edges_i[:, 1, :])
                else:
                    v.scalar_tensor_tensor(payload[g][:, :, 1].bitcast(i32), edges_i[:, 2, :], float(N), edges_i[:, 0, :], ALU.mult, ALU.add)
                v.tensor_copy(payload[g][:, :, 2], edge_w)
                for k in range(NB):
                    ins = v.tensor_scalar(ind[:, k, :], blk_i, float(k), None, ALU.is_equal)
                then(ins)
                for k in range(NB):
                    ins = v.tensor_tensor_scan(scan[:, k, :], ones_f[:, 0:EC], ind[:, k, :], 0.0, ALU.mult, ALU.add)
                then(ins)
                v.tensor_copy(small[:, 0:2].bitcast(bf16), scan[:, :, EC - 1]).then_inc(totals_ready, 1)

            dve.wait_ge(loads["edges"], 64)
            dve.wait_ge(fixed, 8)
            then(v.tensor_copy(ends_f[:, :, :], edges_i[:, 0:2, :]))

            def hot_turn(i, first, n=UN):
                for u in range(n):
                    if not first:
                        dve.wait_ge(hots_used, i * UN + (u - (UN - 1)))
                    for k in range(2):
                        ins = v.tensor_scalar(hot_ring[:, u, k, :], iota16[:, :], ends_f[:, k, bass.ds(i * UN + u, 1)], None, ALU.is_equal)
                    ins.then_inc(hots_ready, 1)

            hot_turn(0, True)
            grouping(0, 0, 4)
            grouping(0, 1, 4)
            for i in turns(dve, 1, 4):
                hot_turn(i, False)

            dve.wait_ge(loads["w1"], 16 * 5)
            dve.wait_ge(loads["w2"], 16 * 3)
            a2 = abc[:, 2:4, :].rearrange("p k f -> p (k f)").rearrange("p (h z f) -> p z h f", h=H, z=2)
            tmp3 = wa_tmp.rearrange("p (h f) -> p h f", h=H)
            vectors = 0
            for c in range(KC):
                w1h = w1x[:, c, 4:4 + D].rearrange("p (h f) -> p h f", h=H)
                w2h = w2x[:, c, 0:D].rearrange("p (h f) -> p h f", h=H)
                for wh, vec, dst in ((w1h, abc[:, 0, :].rearrange("p (h f) -> p h f", h=H), w1x[:, c, 0:4]),
                                     (w1h, abc[:, 1, :].rearrange("p (h f) -> p h f", h=H), w1x[:, c, 260:264]),
                                     (w2h, a2[:, 1, :, :], w2x[:, c, 256:260]),
                                     (w2h, a2[:, 0, :, :], w2x[:, c, 260:264])):
                    then(v.tensor_tensor(tmp3, wh, vec, ALU.mult))
                    v.tensor_reduce(dst, tmp3, X, ALU.add).then_inc(wx_ready, 1)
                    vectors += 1
                    dve.wait_ge(wx_ready, vectors)
            for i in turns(dve, 4, 6):
                hot_turn(i, False)
            grouping(1, 0, 3)
            for i in turns(dve, 6, EC // UN):
                hot_turn(i, False)
            hot_turn(EC // UN, False, EC % UN)
            dve.wait_ge(loads["types"], 32)
            for t in range(TYPES):
                v.tensor_scalar(mask[:, t, :], type_row, float(t), None, ALU.is_equal)

            for b in range(NB):
                dve.wait_ge(count_moved, b + 1)
                v.tensor_scalar(adj[:, b, :], count[:, b, :], 1.0, None, ALU.min).then_inc(adj_ready, 1)

            mv = small[:, 40:48].rearrange("p (b k) -> p b k", k=2)
            stats = small[:, 8:32].rearrange("p (b k) -> p b k", k=6)

            def layernorm(k):
                for b in range(NB):
                    ins = v.bn_stats(stats[:, b, :], x[:, b, :])
                then(ins)
                for b in range(NB):
                    ins = v.bn_aggr(mv[:, b, :], stats[:, b, :])
                then(ins)
                v.tensor_scalar(small[:, 60:64], mv[:, :, 1], EPS, None, ALU.add).then_inc(var_ready, 1)
                dve.wait_ge(std_ready, k)
                then(v.reciprocal(small[:, 68:72], small[:, 64:68]))
                for b in range(NB):
                    v.tensor_scalar(x[:, b, :], x[:, b, :], mv[:, b, 0:1], small[:, 68 + b:69 + b], ALU.subtract, ALU.mult).then_inc(x_ready, 1)

            grouping(1, 1, 3)
            dve.wait_ge(bx_done, 1)
            v.tensor_tensor(xb0.rearrange("p b f -> p (b f)"), x[:, :, :].rearrange("p b f -> p (b f)"),
                            PS[:, 6:8, :].rearrange("p b f -> p (b f)"), ALU.add)
            dve.wait_ge(l0_done, 1)
            then(v.tensor_scalar(small[:, 32:36], PS[:, 2, 0:4], 1.0, None, ALU.max))
            then(v.reciprocal(small[:, 36:40], small[:, 32:36]))
            for b in range(NB):
                dve.wait_ge(l0_done, b // 2 + 1)
                ins = v.scalar_tensor_tensor(x[:, b, :], PS[:, b // 2, (b % 2) * D:(b % 2 + 1) * D], small[:, 36 + b:37 + b], xb0[:, b, :], ALU.mult, ALU.add)
            then(ins)
            layernorm(1)

            def split(dst, src, rest):
                then(v.tensor_copy(dst[0], src))
                then(v.tensor_tensor(rest, src, dst[0], ALU.subtract))
                then(v.tensor_copy(dst[1], rest))
                then(v.tensor_tensor(rest, rest, dst[1], ALU.subtract))
                return v.tensor_copy(dst[2], rest)

            def hots(g, t0, half, sub=True):
                for u in range(HALF):
                    ins = v.tensor_scalar(hotm1[:, half * HALF + u, :], iota16[:, 0:P], slots[g][:, bass.ds(t0 + u, 1), 0], 1.0, ALU.is_equal, ALU.subtract)
                ins.then_inc(hotm1_ready, 1)

            def mask_turn(g, q, first=False):
                for half in range(2):
                    if not first:
                        dve.wait_ge(hotT_done, q + (g * HALVES + half - 1))
                    hots(g, (q + half) * HALF, half)

            def masks(g):
                dve.wait_ge(slots_loaded[g], 16)
                if g == 1:
                    dve.wait_ge(spread_done, TILES)
                mask_turn(g, 0, True)
                for i in turns(dve, 1, TILES // UN):
                    mask_turn(g, i * 2)

            masks(0)

            def by_tile(f, h):
                return f.unsqueeze(2).broadcast_to([P, TILES, H]) if h is None else h.unsqueeze(1).broadcast_to([P, TILES, H])

            for b in range(NB):
                v.tensor_scalar(others[:, b, :], block_of[0][:, :], float(b), None, ALU.is_equal).then_inc(dve_step, 1)
                steps[0] += 1
            dve.wait_ge(dve_step, steps[0])
            dve.wait_ge(feat_moved, NB)
            own_f = comb[:, :, :].rearrange("p h t -> p (h t)").rearrange("p (t h) -> p t h", h=H)
            then(v.tensor_tensor(own_f, by_tile(others[:, 0, :], None), by_tile(None, feat1[:, 0, 260:264]), ALU.mult))
            for b in range(1, NB):
                then(v.tensor_tensor(tmax[:, :, :], by_tile(others[:, b, :], None), by_tile(None, feat1[:, b, 260:264]), ALU.mult))
                then(v.tensor_tensor(own_f, own_f, tmax[:, :, :], ALU.add))
            split([self3[:, k, :, :] for k in range(3)], own_f, tmax[:, :, :]).then_inc(self_split, 1)

            dve.wait_ge(loads["rel"], 16 * 9)
            pri = pri_bc.rearrange("p (r a z) -> p a r z", r=RELS, a=2)
            for a in range(2):
                for r in range(0, RELS, 4):
                    n = a * 2 + r // 4
                    dve.wait_ge(att_done, n + 1)
                    for rr in range(4):
                        ins = v.scalar_tensor_tensor(attT[:, a, r + rr, :].rearrange("p (z w) -> p z w", z=2),
                                                     PS[:, 6 + n % 2, rr * P:(rr + 1) * P].rearrange("p (z w) -> p z w", z=2), DK ** -0.5,
                                                     pri[:, a, r + rr, :].unsqueeze(2).broadcast_to([P, 2, DK]), ALU.mult, ALU.mult)
                    ins.then_inc(att_moved, 1)

            def edge_layer(g):
                bi = g * TILES // UN

                def scores(i, half):
                    t0 = i * UN + half * HALF
                    half %= 2
                    for u in range(HALF):
                        dve.wait_ge(gathered[g][u], t0 * 4 + 16)
                    if g == 0:
                        dve.wait_ge(near_done, half_of(i, t0) + 1)
                        z = zt[:, 0, :].rearrange("p (t h) -> p t h", t=HALF)
                        y = zt[:, 1, :].rearrange("p (t h) -> p t h", t=HALF)
                        own = PS[:, 2 + half, 0:HALF * H].rearrange("p (t h) -> p t h", t=HALF)
                        v.tensor_tensor(z, rows1[:, bass.ds(t0, HALF), 0:4], own, ALU.add).then_inc(near_used, 1)
                        dve.wait_ge(near_used, half_of(i, t0) + 1)
                        step(v.scalar_tensor_tensor(y, z, 0.2, z, ALU.mult, ALU.max))
                        weight = slots[g][:, bass.ds(t0, HALF), 2:3].broadcast_to([P, HALF, H])
                        v.tensor_tensor(score_b[:, half * HALF:(half + 1) * HALF, :], y, weight, ALU.mult).then_inc(score_ready, 1)
                        v.tensor_tensor(score[:, bass.ds(t0, HALF), :], y, weight, ALU.mult)
                    else:
                        for pair in range(2):
                            dve.wait_ge(near_done, half_of(i, t0) * 2 + (HALVES + pair + 1))
                            own = PS[:, 2 + half * 2 + pair, :].rearrange("p (t f) -> p t f", t=2)
                            v.tensor_tensor(prod[:, :, :], rows3[:, bass.ds(t0 + 2 * pair, 2), 0:D], own, ALU.mult).then_inc(near_used, 1)
                            dve.wait_ge(near_used, half_of(i, t0) * 2 + (HALVES + pair + 1))
                            at = half * HALF + pair * 2
                            step(v.tensor_reduce(score_s[:, at:at + 2, :].rearrange("p t h -> p (t h)"),
                                                 prod[:, :, :].rearrange("p t (h w) -> p (t h) w", h=H), X, ALU.add))
                        v.tensor_copy(score_b[:, half * HALF:(half + 1) * HALF, :], score_s[:, half * HALF:(half + 1) * HALF, :]).then_inc(score_ready, 1)
                        v.tensor_copy(score[:, bass.ds(t0, HALF), :], score_s[:, half * HALF:(half + 1) * HALF, :])

                def maxima(i, half):
                    for u in range(half * HALF, (half + 1) * HALF):
                        dve.wait_ge(spread_done, i * UN + (u + 1 + g * TILES))
                        v.tensor_reduce(tmax[:, bass.ds(i * UN + u, 1), :].rearrange("p o h -> p (o h)"),
                                        PS[:, 6 + u % 2, :].rearrange("p (h e) -> p h e", h=H), X, ALU.max).then_inc(spread_used, 1)

                for b in range(NB):
                    ins = v.tensor_scalar(others[:, b, :], block_of[g][:, :], float(b), -BIG, ALU.not_equal, ALU.mult)
                then(ins)
                dve.wait_ge(hotT_done, (g + 1) * HALVES)
                hots(g, 0, 0)
                hots(g, HALF, 1)
                per_half = 1 if g == 0 else 2
                per_turn = 2 * per_half
                turn_base = [steps[0]]
                in_turn = [0]
                at_turn = [0]

                def half_of(i, t0):
                    return i * 2 + offset[0]

                offset = [0]

                def step(ins):
                    in_turn[0] += 1
                    ins.then_inc(dve_step, 1)
                    dve.wait_ge(dve_step, at_turn[0] * per_turn + (in_turn[0] + turn_base[0]))

                scores(0, 0)
                turn_base[0] += per_half

                def turn(i, last_turn):
                    at_turn[0], in_turn[0] = i, 0
                    for half in range(2):
                        if not (last_turn and half):
                            offset[0] = half + 1
                            scores(i, half + 1)
                        maxima(i, half)
                        if not last_turn:
                            hots(g, i * UN + (UN + half * HALF), half)

                for i in turns(dve, 0, TILES // UN - 1):
                    turn(i, False)
                turn(TILES // UN - 1, True)
                steps[0] += HALVES * per_half
                dve.wait_ge(spread_used, (g + 1) * TILES)

                dve.wait_ge(spread_used, (g + 1) * TILES)
                for b in range(NB):
                    then(v.tensor_tensor(comb[:, :, :], tmax[:, :, :].rearrange("p t h -> p h t"),
                                         others[:, b, :].unsqueeze(1).broadcast_to([P, H, TILES]), ALU.add))
                    ins = v.tensor_reduce(node_max[:, b, :], comb[:, :, :], X, ALU.max)
                    then(ins)
                own_max = comb[:, :, :].rearrange("p h t -> p (h t)").rearrange("p (t h) -> p t h", h=H)
                then(v.tensor_tensor(own_max, by_tile(others[:, 0, :], None), by_tile(None, node_max[:, 0, :]), ALU.add))
                for b in range(1, NB):
                    then(v.tensor_tensor(tmax[:, :, :], by_tile(others[:, b, :], None), by_tile(None, node_max[:, b, :]), ALU.add))
                    ins = v.tensor_tensor(tile_max[:, :, :] if b == NB - 1 else own_max, own_max, tmax[:, :, :], ALU.max)
                    if b < NB - 1:
                        then(ins)
                ins.then_inc(max_ready, 1)
                dve.wait_ge(maxe_done, g + 1)
                v.tensor_tensor(score[:, :, :], score[:, :, :], PS[:, 0, 0:TILES * H].rearrange("p (t h) -> p t h", h=H), ALU.subtract)\
                    .then_inc(diff_ready, 1)
                dve.wait_ge(exp_ready, g + 1)

                def messages(i, half, guard):
                    t0 = i * UN + half * HALF
                    for u in range(half * HALF, (half + 1) * HALF):
                        if guard:
                            dve.wait_ge(summed, (i + bi) * UN + (u + 1 - UN))
                        v.tensor_scalar(hotf[:, u, :], iota16[:, 0:P], slots[g][:, bass.ds(i * UN + u, 1), 0], None, ALU.is_equal)
                    if g == 0:
                        feats, ex = rows1[:, bass.ds(t0, HALF), 4:W1], rows1[:, bass.ds(t0, HALF), 0:4]
                    else:
                        feats, ex = rows3[:, bass.ds(t0, HALF), D:W3], rows3[:, bass.ds(t0, HALF), D - 4:D]
                    feats = feats.rearrange("p t (h f) -> p t h f", h=H)
                    v.tensor_tensor(feats, feats, ex.unsqueeze(3).broadcast_to([P, HALF, H, DK]), ALU.mult).then_inc(message_ready, 1)

                for half in range(2):
                    messages(0, half, g == 1)
                for i in turns(dve, 1, TILES // UN):
                    for half in range(2):
                        messages(i, half, True)
                dve.wait_ge(sums_done, g + 1)

            rden = small[:, 88:104].rearrange("p (b h) -> p b h", b=NB)

            def denominators(col):
                then(v.tensor_scalar(rden, PS[:, 4:8, col[0]:col[0] + col[1] * (H - 1) + 1:col[1]], 1e-30, None, ALU.max))
                then(v.reciprocal(rden, rden))

            edge_layer(0)
            denominators((0, 1))
            t1 = rows1[:, 0, 0:1]
            o1 = part(0, 1024).rearrange("p (b f) -> p b f", b=NB)
            for b in range(NB):
                ins = v.tensor_tensor(o1[:, b, :].rearrange("p (h f) -> p h f", h=H), PS[:, 4 + b, 4:W1].rearrange("p (h f) -> p h f", h=H),
                                      rden[:, b, :].unsqueeze(2).broadcast_to([P, H, DK]), ALU.mult)
            then(ins)
            then(v.tensor_tensor(o1, o1, bias1[:, :].unsqueeze(1).broadcast_to([P, NB, D]), ALU.add))
            then(v.scalar_tensor_tensor(x[:, :, :], o1, 0.0, x[:, :, :], ALU.max, ALU.add))
            layernorm(2)

            v.memset(hx[:, :, :, 64], 1.0)
            for b in range(NB):
                dve.wait_ge(h_done, b + 1)
                then(v.tensor_scalar(h_neg[:, 0:260], PS[:, 4 + b, 0:260], 0.0, None, ALU.min))
                then(v.scalar_tensor_tensor(hx[:, b, :, 0:64], PS[:, 4 + b, 0:D].rearrange("p (h f) -> p h f", h=H), 0.0,
                                            h_neg[:, 0:D].rearrange("p (h f) -> p h f", h=H), ALU.max, ALU.add))
                then(v.scalar_tensor_tensor(a_dst[:, b, :], PS[:, 4 + b, D:260], 0.0, h_neg[:, D:260], ALU.max, ALU.add))
                then(v.tensor_scalar(a_neg[:, 0, b, :], a_dst[:, b, :], -1.0, None, ALU.mult))
                v.tensor_scalar(a_neg[:, 1, b, :], a_dst[:, b, :], -0.2, None, ALU.mult).then_inc(h_moved, 1)
            for b in range(NB):
                for h in range(H):
                    n = b * H + h
                    dve.wait_ge(pexp_ready, n + 1)
                    ins = v.scalar_tensor_tensor(exp_ring[:, n % 4, 0, :], exp_ring[:, n % 4, 0, :], 0.0, exp_ring[:, n % 4, 1, :], ALU.max, ALU.min)
                    if n % 3 == 2:
                        ins.then_inc(pmin_ready, 1)
                    else:
                        then(ins)
                        v.tensor_tensor(pair_w[:, b, h, :], exp_ring[:, n % 4, 0, :], countT[:, b, :], ALU.mult).then_inc(pw_ready, 1)
            dve.wait_ge(hp_done, 1)
            denominators((64, 65))
            hp = part(0, 1024).rearrange("p (b h f) -> p b h f", b=NB, h=H)
            hp_flat = part(0, 1024)
            for b in range(NB):
                ins = v.tensor_tensor(hp[:, b, :, :], PS[:, 4 + b, 0:260].rearrange("p (h w) -> p h w", h=H)[:, :, 0:64],
                                      rden[:, b, :].unsqueeze(2).broadcast_to([P, H, DK]), ALU.mult)
            then(ins)
            v.tensor_scalar(elu_tmp[:, 0, :], hp_flat, 0.0, None, ALU.min).then_inc(elu_in, 1)
            dve.wait_ge(elu_exp, 1)
            then(v.scalar_tensor_tensor(elu_tmp[:, 2, :], hp_flat, 0.0, elu_tmp[:, 1, :], ALU.max, ALU.add))
            then(v.tensor_scalar(elu_tmp[:, 2, :], elu_tmp[:, 2, :], 1.0, None, ALU.subtract))
            v.tensor_scalar(elu_tmp[:, 0, :], elu_tmp[:, 2, :], 0.0, None, ALU.min).then_inc(elu_in, 1)
            dve.wait_ge(elu_exp, 2)
            then(v.scalar_tensor_tensor(elu_tmp[:, 2, :], elu_tmp[:, 2, :], 0.0, elu_tmp[:, 1, :], ALU.max, ALU.add))
            xf = x[:, :, :].rearrange("p b f -> p (b f)")
            then(v.scalar_tensor_tensor(xf, elu_tmp[:, 2, :], 1.0, xf, ALU.subtract, ALU.add))
            dve.wait_ge(skip_in_s, 1)
            then(v.tensor_scalar(skip_e[:, 1, :], skip_e[:, 1, :], 1.0, None, ALU.add))
            then(v.reciprocal(skip_e[:, 2, :], skip_e[:, 1, :]))
            layernorm(3)

            dve.wait_ge(xT_moved, 6)
            for t in range(TYPES):
                v.tensor_tensor(xmT[:, t, :, :], xT[:, :, :], mask[:, t, :].unsqueeze(1).broadcast_to([P, KC, N]), ALU.mult).then_inc(xm_ready, 1)
            masks(1)
            n = 0
            for b in range(NB):
                if b >= 2:
                    dve.wait_ge(t3_written[b % 2], 16)
                for a in range(2):
                    for r in range(0, RELS, 4):
                        dve.wait_ge(rel_done, 2 * n + 2)
                        v.tensor_copy(stage[:, b % 2, r:r + 4, D + a * P:D + (a + 1) * P], PS[:, 4 + n % 2, :].rearrange("p (r w) -> p r w", r=4))\
                            .then_inc(rel_moved_v, 1)
                        n += 1
            dve.wait_ge(q_done, 1)
            then(v.tensor_copy(q_f, PS[:, 6:8, :].rearrange("p b f -> p (b f)")))
            split([parts3[:, k, :, :].rearrange("p b f -> p (b f)") for k in range(3)], q_f, q_r).then_inc(q_split, 1)
            edge_layer(1)
            denominators((0, 1))
            for b in range(NB):
                ins = v.tensor_tensor(agg[:, b, :].rearrange("p (h f) -> p h f", h=H), PS[:, 4 + b, 4:W1].rearrange("p (h f) -> p h f", h=H),
                                      rden[:, b, :].unsqueeze(2).broadcast_to([P, H, DK]), ALU.mult)
            ins.then_inc(am_ready, 1)
            dve.wait_ge(xT_moved, 8)
            for t in range(TYPES):
                for c in range(KC):
                    ins = v.scalar_tensor_tensor(amT[:, t, c, :], aggT[:, c, :], skip_e[:, 2, t:t + 1], mask[:, t, :], ALU.mult, ALU.mult)
                ins.then_inc(am_ready, 1)
            dve.wait_ge(o_done, 1)
            for b in range(NB):
                ins = v.tensor_tensor(x[:, b, :], x[:, b, :], PS[:, 2 + b // 2, (b % 2) * D:(b % 2 + 1) * D], ALU.add)
            then(ins)
            layernorm(4)


_INS = ['x', 'src', 'dst', 'edge_type_8', 'edge_weight', 'node_type_4', 'L0_gnn_W', 'L0_gnn_B', 'L1_gnn_W', 'L1_gnn_a_self',
        'L1_gnn_a_neigh', 'L1_gnn_bias', 'L2_gnn_W', 'L2_gnn_a', 'L3_gnn_k_linears', 'L3_gnn_q_linears', 'L3_gnn_v_linears',
        'L3_gnn_a_linears', 'L3_gnn_relation_att', 'L3_gnn_relation_msg', 'L3_gnn_relation_pri', 'L3_gnn_skip']


def kernel(**inputs):
    import numpy as _np
    import concourse.bacc as _bacc
    from concourse import mybir as _mybir
    from concourse.bass_utils import run_bass_kernel_spmd as _run

    nc = _bacc.Bacc("TRN2", target_bir_lowering=False, num_devices=1)
    arrays, args = {}, []
    for name in _INS:
        a = _np.ascontiguousarray(inputs[name])
        arrays[f"in_{name}_dram"] = a
        args.append(nc.dram_tensor(f"in_{name}_dram", a.shape, _mybir.dt.from_np(a.dtype), kind="ExternalInput").ap())
    args.append(nc.dram_tensor("out_0_dram", (N, D), _mybir.dt.float32, kind="ExternalOutput").ap())
    gnn_kernel(nc, *args)
    r = _run(nc, [arrays], core_ids=[0])
    return r.results[0]["out_0_dram"]
```

```python
import concourse.bass as bass
from concourse import mybir
from contextlib import ExitStack

N = 512
E = 8704
D = 256
H = 4
DK = D // H
RELS = 8
TYPES = 4
P = 128
NB = N // P
KC = D // P
EC = E // P
TILES = EC + NB
W1 = 4 + D
W3 = 2 * D
BANK = 512
HALVES = 18
UN = 8
HALF = UN // 2
assert HALVES == TILES // HALF and EC % UN == HALF
BIG = 2.0 ** 100
EPS = 1e-5
SPREAD = (0, 1, 6, 7)
SPARE = (6, 7, 1, 2, 3, 6, 7, 1)
EARLY = 18


def gnn_kernel(nc, x_in, src_in, dst_in, etype_in, ew_in, ntype_in, w0_in, b0_in, w1_in, aself_in, aneigh_in,
               bias1_in, w2_in, a2_in, klin_in, qlin_in, vlin_in, alin_in, att_in, msg_in, pri_in, skip_in, out):
    f32, bf16, f16 = mybir.dt.float32, mybir.dt.bfloat16, mybir.dt.float16
    i32, u32 = mybir.dt.int32, mybir.dt.uint32
    ALU = mybir.AluOpType
    ACT = mybir.ActivationFunctionType
    X = mybir.AxisListType.X
    ctx = ExitStack()
    with ctx:
        def sb(name, shape, dt):
            return ctx.enter_context(nc.sbuf_tensor(name, shape, dt))

        def sem(name):
            return ctx.enter_context(nc.semaphore(name))

        slots_src = nc.dram_tensor("slots_src", (P * TILES, 4), f32, kind="Internal").ap()
        slots_dst = nc.dram_tensor("slots_dst", (P * TILES, 4), f32, kind="Internal").ap()
        locals_dst = nc.dram_tensor("locals_dst", (TILES * P,), bf16, kind="Internal").ap()
        table1 = nc.dram_tensor("table1", (N, W1), f32, kind="Internal").ap()
        table3 = nc.dram_tensor("table3", (RELS * N, W3), f32, kind="Internal").ap()

        region = sb("region", [P, TILES * W3], f32)

        def part(start, size):
            return region[:, start:start + size]

        rows1 = part(0, TILES * W1).rearrange("p (t w) -> p t w", w=W1)
        rows3 = region[:, :].rearrange("p (t w) -> p t w", w=W3)
        hot_ring = part(12800, 4096).bitcast(bf16).rearrange("p (u k n) -> p u k n", u=UN, k=2)
        xb0 = part(12800, 1024).rearrange("p (b f) -> p b f", b=NB)
        adj = part(2048, 2048).rearrange("p (b n) -> p b n", b=NB)
        axT = part(4096, 1024).rearrange("p (c n) -> p c n", c=KC)
        w0_nat = part(5120, 512).rearrange("p (b i) -> p b i", b=KC)
        b0_nat = part(5632, 512).rearrange("p (b i) -> p b i", b=KC)
        w0T = part(6144, 512).rearrange("p (c o) -> p c o", c=KC)
        b0T = part(6656, 512).rearrange("p (c o) -> p c o", c=KC)
        group_tmp = part(8192, 2048)
        wa_tmp = part(10240, 256)
        abc = part(10496, 1024).rearrange("p (k f) -> p k f", k=4)
        type_row = part(11520, N).bitcast(i32)
        empty = part(12032, 4 * TILES).rearrange("p (t w) -> p t w", w=4)
        ends_f = part(12320, 2 * EC).rearrange("p (k j) -> p k j", k=2)
        edges_i = part(12456, 3 * EC).bitcast(i32).rearrange("p (k j) -> p k j", k=3)
        edge_w = part(12660, EC)
        block_f = part(12728, TILES)
        pair_w = part(0, 8192).rearrange("p (b h n) -> p b h n", b=NB, h=H)
        exp_ring = part(8192, 4096).rearrange("p (r k n) -> p r k n", r=4, k=2)
        hx = part(12288, NB * H * 65).rearrange("p (b h w) -> p b h w", b=NB, h=H)
        h_neg = part(13328, 264)
        a_dst = part(13592, 16).rearrange("p (b h) -> p b h", b=NB)
        a_neg = part(13608, 32).rearrange("p (k b h) -> p k b h", k=2, b=NB)
        hpT = part(13640, H * N).rearrange("p (h n) -> p h n", h=H)
        elu_tmp = part(15688, 2048).rearrange("p (k f) -> p k f", k=2)
        stage = part(0, 8192).rearrange("p (k r w) -> p k r w", k=2, r=RELS)
        kT = part(12288, 1024).rearrange("p (c n) -> p c n", c=KC)
        vT = part(13312, 1024).rearrange("p (c n) -> p c n", c=KC)
        hot_src = part(18720, TILES * P // 2).bitcast(bf16).rearrange("p (t n) -> p t n", t=TILES)
        kqv = part(18720, 6144).rearrange("p (k t c o) -> p k t c o", k=3, t=TYPES, c=KC)
        att_nat = part(24864, 2048).rearrange("p (r a w) -> p r a w", r=RELS, a=2)
        countT = part(24864, 2048).rearrange("p (b n) -> p b n", b=NB)
        attT = part(26912, 2048).rearrange("p (a r w) -> p a r w", r=RELS, a=2)
        msgD = part(28960, 2048).rearrange("p (a r w) -> p a r w", r=RELS, a=2)
        count = part(31008, 2048).rearrange("p (b n) -> p b n", b=NB)
        w1x = part(33056, 528).rearrange("p (c w) -> p c w", c=KC)
        w2x = part(33584, 528).rearrange("p (c w) -> p c w", c=KC)
        feat1 = part(34112, 1056).rearrange("p (b w) -> p b w", b=NB)
        xT = part(35168, 1024).rearrange("p (c n) -> p c n", c=KC)
        pri_bc = part(36192, 32)
        payload = [part(36224 + g * 4 * EC, 4 * EC).rearrange("p (j w) -> p j w", w=4) for g in range(2)]
        xmT = part(31008, 4096).rearrange("p (t c n) -> p t c n", t=TYPES, c=KC)
        q_f = part(22816, 1024)
        q_r = part(23840, 1024)
        LATE = 20768 // W3
        agg = part(0, 1024).rearrange("p (b f) -> p b f", b=NB)
        aggT = part(1024, 1024).rearrange("p (c n) -> p c n", c=KC)

        identf = sb("identf", [P, P], f32)
        identb = sb("identb", [P, P], bf16)
        bigI = sb("bigI", [P, P], bf16)
        before = sb("before", [P, P], bf16)
        onesb = sb("onesb", [P, P], bf16)
        ones_f = sb("ones_f", [P, 72], f32)
        zerob = sb("zerob", [P, W1], bf16)
        iota16 = sb("iota16", [P, N], f16)
        tile_at = sb("tile_at", [P, TILES], f32)
        x = sb("x", [P, NB, D], f32)
        alin = sb("alin", [P, TYPES, KC, D], f32)
        mask = sb("mask", [P, TYPES, N], bf16)
        bias1 = sb("bias1", [P, D], f32)
        skip_e = sb("skip_e", [P, 3, TYPES], f32)
        address = [sb(f"address{g}", [P, EC], u32) for g in range(2)]
        slots = [sb(f"slots{g}", [P, TILES, 4], f32) for g in range(2)]
        block_of = [sb(f"block_of{g}", [P, TILES], i32) for g in range(2)]
        others = sb("others", [P, NB, TILES], f32)
        hotT = sb("hotT", [P, TILES, P], bf16)
        loc_rows = sb("loc_rows", [TILES, P], bf16)
        hotf = sb("hotf", [P, UN, P], f32)
        wide = hotf[:, :, :].rearrange("p u n -> p (u n)").bitcast(bf16).rearrange("p (t h e) -> p t h e", t=HALF, h=H)
        score = sb("score", [P, TILES, H], f32)
        score_b = sb("score_b", [P, UN, H], bf16)
        zt = sb("zt", [P, 2, HALF * H], f32)
        tmax = sb("tmax", [P, TILES, H], f32)
        comb = sb("comb", [P, H, TILES], f32)
        node_max = sb("node_max", [P, NB, H], f32)
        tile_max = sb("tile_max", [P, TILES, H], bf16)
        parts3 = sb("parts3", [P, 3, NB, D], bf16)
        self3 = parts3[:, :, :, :].rearrange("p k b f -> p (k b f)")[:, 0:3 * TILES * H].rearrange("p (k t h) -> p k t h", k=3, h=H)
        prod = sb("prod", [P, 2, D], f32)[:, :, :]
        narrow = prod.rearrange("p k f -> p (k f)").bitcast(bf16).rearrange("p (k e) -> p k e", e=P // 2)
        free3 = mask[:, :, :].rearrange("p t n -> p (t n)")
        narrow3 = free3[:, 0:1024].rearrange("p (k e) -> p k e", e=P // 2)
        products = [prod, free3[:, 1024:2048].bitcast(f32).rearrange("p (t f) -> p t f", t=2)]
        small = sb("small", [P, 128], f32)
        minus_one_f = small[:, 105:106]
        partition = small[:, 110:111]
        types_i = small[:, 106:106 + NB].bitcast(i32)
        type_w = small[:, 112:112 + NB * TYPES].rearrange("p (b t) -> p b t", b=NB)
        minus_one = small[:, 104:105].bitcast(bf16)[:, 0:1]
        PS = ctx.enter_context(nc.psum_tensor("PS", [P, 8, BANK], f32))
        sums = PS[:, 4:8, :].rearrange("p b f -> p (b f)")

        loads = {n: sem("loaded_" + n) for n in
                 "edges x w0 w1 w2 kqv rel alin types".split()}
        fixed = sem("constants_made")
        index_made = sem("partition_index_made")
        pool_step = sem("pool_step")
        dve_step = sem("dve_step")
        act_step = sem("act_step")
        prefilled = sem("slots_prefilled")
        totals_ready = sem("group_totals_ready")
        prefix_done = sem("group_prefix_done")
        address_ready = sem("addresses_ready")
        scattered = [[sem(f"scattered{g}_{u}") for u in range(4)] for g in range(2)]
        slots_loaded = [sem(f"slots_loaded{g}") for g in range(2)]
        gathered = [[sem(f"gathered{g}_{u}") for u in range(4)] for g in range(2)]
        hots_ready = sem("one_hots_ready")
        hots_used = sem("one_hots_used")
        prep_done = sem("prep_transposed")
        prep_moved = sem("prep_moved")
        att_done = sem("att_transposed")
        att_moved = sem("att_moved")
        bx_done = sem("xB_done")
        count_moved = sem("counts_moved")
        adj_ready = sem("adjacency_ready")
        ax_done = sem("adj_x_done")
        ax_moved = sem("adj_x_moved")
        l0_done = sem("layer0_products_done")
        var_ready = sem("variances_ready")
        std_ready = sem("deviations_ready")
        x_ready = sem("x_ready")
        xT_done = sem("xT_done")
        xT_moved = sem("xT_moved")
        feat_done = sem("features_done")
        feat_moved = sem("features_moved")
        table1_written = [sem(f"table1_written{b}") for b in range(NB)]
        self_split = sem("self_scores_split")
        cT_done = sem("counts_transposed")
        cT_moved = sem("countsT_moved")
        hot_src_ready = sem("source_hots_ready")
        hotT_src_done = sem("source_hotT_transposed")
        hotT_src_moved = sem("source_hotT_moved")
        loc_done = sem("slot_nodes_transposed")
        loc_moved = sem("slot_nodes_moved")
        loc_written = sem("slot_nodes_written")
        loc_spread = sem("slot_nodes_on_every_partition")
        hotT_ready = sem("target_hotT_ready")
        near_done = sem("own_node_gathered")
        near_used = sem("own_node_used")
        score_ready = sem("scores_ready")
        spread_done = sem("scores_spread")
        priors_ready = sem("priors_ready")
        wide_ready = sem("spread_scores_moved")
        wide_used = sem("spread_scores_halved")
        max_ready = sem("node_maxima_ready")
        maxe_done = sem("maxima_on_edges")
        diff_ready = sem("differences_ready")
        exp_ready = sem("exponentials_ready")
        message_ready = sem("messages_ready")
        hotf_ready = sem("hotf_ready")
        summed = sem("messages_summed")
        sums_done = sem("sums_done")
        wx_ready = sem("weight_vectors_ready")
        h_done = sem("h_done")
        spread2_done = sem("source_scores_spread")
        h_moved = sem("h_moved")
        pexp_ready = sem("pair_exp_ready")
        pmin_ready = sem("pair_minima_for_pool")
        pw_by_pool = sem("pair_weights_by_pool")
        pw_ready = sem("pair_weights_ready")
        hpT_done = sem("pair_sumsT_done")
        hpT_moved = sem("pair_sumsT_moved")
        hp_done = sem("pair_sums_done")
        elu_in = sem("elu_arguments_ready")
        elu_exp = sem("elu_exp_ready")
        xm_ready = sem("typed_x_ready")
        kv_done = sem("keys_values_done")
        kv_moved = sem("keys_values_moved")
        q_done = sem("queries_done")
        q_split = sem("queries_split")
        rel_done = sem("relation_products_done")
        rel_moved_a = sem("relation_products_moved_act")
        rel_moved_v = sem("relation_products_moved_dve")
        t3_written = [sem(f"table3_written{k}") for k in range(2)]
        skip_exp = sem("skip_exp_ready")
        agg_ready = sem("aggregates_ready")
        o_done = sem("output_products_done")
        out_written = [sem(f"output_written{b}") for b in range(NB)]

        block = ctx.enter_context(nc.Block())

        def turns(engine, first, end):
            with engine.Fori(first, end) as i:
                yield i

        def pair_weights_done(engine, n):
            engine.wait_ge(pw_by_pool if n % 2 else pw_ready, n // 2 + 1)

        @block.sync
        def _(sp):
            for k, a in enumerate((src_in, dst_in, etype_in)):
                sp.dma_start(edges_i[:, k, :], a.rearrange("(p j) -> p j", p=P)).then_inc(loads["edges"], 16)
            sp.dma_start(edge_w, ew_in.rearrange("(p j) -> p j", p=P)).then_inc(loads["edges"], 16)
            sp.dma_start(x[:, :, :], x_in.rearrange("(b p) f -> p b f", p=P)).then_inc(loads["x"], 16)
            sp.dma_start(w0_nat, w0_in.rearrange("(b p) i -> p b i", p=P)).then_inc(loads["w0"], 16)
            sp.dma_start(b0_nat, b0_in.rearrange("(b p) i -> p b i", p=P)).then_inc(loads["w0"], 16)
            for c in range(KC):
                sp.dma_start(w1x[:, c, 4:4 + D].rearrange("p (h o) -> p h o", h=H),
                             w1_in[:, c * P:(c + 1) * P, :].rearrange("h p o -> p h o")).then_inc(loads["w1"], 16)
                sp.dma_start(w2x[:, c, 0:D].rearrange("p (h o) -> p h o", h=H),
                             w2_in[:, c * P:(c + 1) * P, :].rearrange("h p o -> p h o")).then_inc(loads["w2"], 16)
            sp.dma_start(abc[:, 0, :], aneigh_in.rearrange("(o h) f -> o (h f)", o=1).broadcast_to([P, D])).then_inc(loads["w1"], 16)
            sp.dma_start(abc[:, 1, :], aself_in.rearrange("(o h) f -> o (h f)", o=1).broadcast_to([P, D])).then_inc(loads["w1"], 16)
            sp.dma_start(abc[:, 2:4, :], a2_in.rearrange("h o f -> o (h f)").broadcast_to([P, 2 * D])).then_inc(loads["w2"], 16)
            sp.dma_start(bias1[:, :], bias1_in.rearrange("(o h) f -> o (h f)", o=1).broadcast_to([P, D])).then_inc(loads["w1"], 16)
            sp.wait_ge(pool_step, 7)
            for h in range(H):
                a, s = h // 2, (h % 2) * DK
                sp.dma_start(att_nat[s:s + DK, :, a, s:s + DK], att_in[:, h, :, :].rearrange("r d e -> d r e")).then_inc(loads["rel"], 16)
                sp.dma_start(msgD[s:s + DK, a, :, s:s + DK], msg_in[:, h, :, :].rearrange("r d e -> d r e")).then_inc(loads["rel"], 16)
            sp.dma_start(pri_bc, pri_in.rearrange("(o r) h -> o (r h)", o=1).broadcast_to([P, RELS * H])).then_inc(loads["rel"], 16)
            sp.dma_start(alin[:, :, :, :], alin_in.rearrange("t (c p) o -> p t c o", p=P)).then_inc(loads["alin"], 16)
            sp.dma_start(type_row, ntype_in.rearrange("(o n) -> o n", o=1).broadcast_to([P, N])).then_inc(loads["types"], 16)
            with nc.allow_non_contiguous_dma(reason="512 types, once"):
                sp.dma_start(types_i, ntype_in.rearrange("(b p) -> p b", p=P)).then_inc(loads["types"], 16)
            sp.dma_start(skip_e[:, 0, :], skip_in.rearrange("(o n) -> o n", o=1).broadcast_to([P, TYPES])).then_inc(loads["types"], 16)

            for g, table in ((0, slots_src), (1, slots_dst)):
                if g == 1:
                    for b in range(NB):
                        sp.wait_ge(feat_moved, b + 1)
                        sp.dma_start(table1[b * P:(b + 1) * P, :], feat1[:, b, 0:W1]).then_inc(table1_written[b], 16)
                for u in range(4):
                    sp.wait_ge(scattered[g][u], 16 * (EC // 4))
                sp.dma_start(slots[g][:, :, :], table.rearrange("(p t) w -> p t w", p=P)).then_inc(slots_loaded[g], 16)
            sp.wait_ge(hotf_ready, HALVES)
            for k, a in enumerate((klin_in, qlin_in, vlin_in)):
                sp.dma_start(kqv[:, k, :, :, :], a.rearrange("t (c p) o -> p t c o", p=P)).then_inc(loads["kqv"], 16)
            sp.wait_ge(loc_moved, 1)
            sp.dma_start(locals_dst.rearrange("(t p) -> t p", t=TILES), loc_rows[:, :]).then_inc(loc_written, 16)
            sp.wait_ge(loc_written, 16)
            sp.dma_start(hotT[:, :, :].rearrange("p t n -> p (t n)"), locals_dst.rearrange("(o n) -> o n", o=1).broadcast_to([P, TILES * P]))\
                .then_inc(loc_spread, 16)
            t3 = table3.rearrange("(r b p) w -> p b r w", p=P, b=NB)
            for b in range(NB):
                sp.wait_ge(rel_moved_a, 4 * (b + 1))
                sp.wait_ge(rel_moved_v, 4 * (b + 1))
                sp.dma_start(t3[:, b, :, :], stage[:, b % 2, :, :]).then_inc(t3_written[b % 2], 16)
            for b in range(NB):
                sp.wait_ge(x_ready, 3 * NB + b + 1)
                sp.dma_start(out[b * P:(b + 1) * P, :], x[:, b, :]).then_inc(out_written[b], 16)
            for b in range(NB):
                sp.wait_ge(out_written[b], 16)

        @block.gpsimd
        def _(pool):
            pool.memset(identf[:, :], 0.0).then_inc(pool_step, 1)
            pool.memset(empty[:, :, :], 0.0).then_inc(pool_step, 1)
            pool.memset(before[:, :], 0.0).then_inc(pool_step, 1)
            pool.wait_ge(pool_step, 3)
            pool.memset(empty[:, :, 0], -1.0).then_inc(pool_step, 1)
            pool.affine_select(out=identf[:, :], in_=identf[:, :], compare_op=ALU.not_equal, fill=1.0, base=0,
                               pattern=[[-1, P]], channel_multiplier=1).then_inc(pool_step, 1)
            pool.affine_select(out=before[:, :], in_=before[:, :], compare_op=ALU.is_ge, fill=1.0, base=0,
                               pattern=[[-1, P]], channel_multiplier=1).then_inc(fixed, 1)
            pool.memset(onesb[:, :], 1.0).then_inc(fixed, 1)
            pool.memset(minus_one_f, -1.0).then_inc(fixed, 1)
            pool.memset(small[:, 104:105].bitcast(bf16), -1.0).then_inc(fixed, 1)
            pool.memset(ones_f[:, :], 1.0).then_inc(fixed, 1)
            pool.memset(zerob[:, :], 0.0).then_inc(fixed, 1)
            pool.iota(iota16[:, :], pattern=[[1, N]], base=0, channel_multiplier=0,
                      allow_small_or_imprecise_dtypes=True).then_inc(fixed, 1)
            pool.iota(tile_at[:, :], pattern=[[P, TILES]], base=0, channel_multiplier=0,
                      allow_small_or_imprecise_dtypes=True).then_inc(fixed, 1)
            pool.wait_ge(pool_step, 5)
            pool.tensor_copy(identb[:, :], identf[:, :]).then_inc(fixed, 1)
            pool.tensor_scalar(bigI[:, :], identf[:, :], BIG, None, ALU.mult).then_inc(fixed, 1)
            for table in (slots_src, slots_dst):
                pool.dma_start(table.rearrange("(p t) w -> p t w", p=P), empty[:, :, :]).then_inc(prefilled, 16)
            for nat in (att_nat, msgD):
                pool.memset(nat, 0.0).then_inc(pool_step, 1)
            pool.iota(partition, pattern=[[0, 1]], base=0, channel_multiplier=1, allow_small_or_imprecise_dtypes=True).then_inc(index_made, 1)

            def scatter(g, table, j):
                if j >= 4:
                    pool.wait_ge(scattered[g][j % 4], 16 * (j // 4))
                pool.indirect_dma_start(out=table, out_offset=bass.IndirectOffsetOnAxis(ap=address[g][:, j:j + 1], axis=0),
                                        in_=payload[g][:, j, :], in_offset=None).then_inc(scattered[g][j % 4], 16)

            def gather(g, table, rows, t):
                if t >= 4:
                    pool.wait_ge(gathered[g][t % 4], 16 * (t // 4))
                pool.indirect_dma_start(out=rows[:, t, :], out_offset=None, in_=table,
                                        in_offset=bass.IndirectOffsetOnAxis(ap=slots[g][:, t, 1:2].bitcast(u32), axis=0))\
                    .then_inc(gathered[g][t % 4], 16)

            pool.wait_ge(prefilled, 32)
            pool.wait_ge(address_ready, 1)
            for j in range(EC):
                scatter(0, slots_src, j)
            pool.wait_ge(address_ready, 2)
            for j in range(EARLY):
                scatter(1, slots_dst, j)
            pool.wait_ge(slots_loaded[0], 16)
            for b in range(NB):
                pool.wait_ge(table1_written[b], 16)
            for t in range(TILES):
                gather(0, table1, rows1, t)
            for j in range(EARLY, EC):
                scatter(1, slots_dst, j)
            for n in range(1, NB * H, 2):
                pool.wait_ge(pmin_ready, n // 2 + 1)
                pool.tensor_tensor(pair_w[:, n // H, n % H, :], exp_ring[:, n % 4, 0, :], countT[:, n // H, :], ALU.mult).then_inc(pw_by_pool, 1)
            pool.wait_ge(slots_loaded[1], 16)
            pool.wait_ge(t3_written[0], 32)
            pool.wait_ge(t3_written[1], 32)
            for t in range(TILES):
                if t == LATE:
                    pool.wait_ge(q_split, 2)
                gather(1, table3, rows3, t)

            def target_hotf(i, first):
                for half in range(2):
                    if not first:
                        pool.wait_ge(summed, i * UN + (half * HALF + HALF - UN + TILES))
                    for u in range(half * HALF, half * HALF + 2):
                        ins = pool.tensor_scalar(hotf[:, u, :], iota16[:, 0:P], slots[1][:, i * UN + u, 0:1], None, ALU.is_equal)
                    ins.then_inc(hotf_ready, 1)

            pool.wait_ge(max_ready, 2)
            target_hotf(0, True)
            for i in range(1, TILES // UN):
                target_hotf(i, False)

        @block.tensor
        def _(pe):
            def blocks_of(g, t0):
                return nc.values_load_multi_w_load_instructions(
                    block_of[g][0:1, bass.ds(t0, HALF)], engines=(mybir.EngineType.PE,), min_val=0, max_val=NB - 1,
                    skip_runtime_bounds_check_because="a sum of three comparisons, each 0 or 1")[1]

            def transposes(source, banks, done):
                for c in range(KC):
                    for b in range(NB):
                        last = nc.tensor.transpose(PS[:, banks[c], b * P:(b + 1) * P], source[:, b, c * P:(c + 1) * P], identf[:, :])
                    last.then_inc(done, 1)

            def group_prefix(bank):
                nc.tensor.matmul(PS[:, bank, 0:4], before[:, :], small[:, 0:2].bitcast(bf16), start=True, stop=True)
                nc.tensor.matmul(PS[:, bank, 4:8], onesb[:, :], small[:, 0:2].bitcast(bf16), start=True, stop=True).then_inc(prefix_done, 1)

            pe.wait_ge(fixed, 10)
            pe.wait_ge(totals_ready, 1)
            group_prefix(4)
            def count_turn(i, first, n=UN):
                for u in range(n):
                    pe.wait_ge(hots_ready, i * UN + (u + 1))
                    for b in range(NB):
                        ins = nc.tensor.matmul(PS[:, b, :], hot_ring[:, u, 0, b * P:(b + 1) * P], hot_ring[:, u, 1, :],
                                               start=(first and u == 0), stop=(n < UN and u == n - 1), skip_group_check=True)
                    ins.then_inc(hots_used, 1)

            count_turn(0, True)
            for i in turns(pe, 1, EC // UN):
                count_turn(i, False)
            count_turn(EC // UN, False, EC % UN)
            pe.wait_ge(loads["x"], 16)
            transposes(x, (5, 6), prep_done)
            pe.wait_ge(loads["w0"], 32)
            for nat, bank in ((w0_nat, 7), (b0_nat, 4)):
                if bank == 4:
                    pe.wait_ge(address_ready, 1)
                for c in range(KC):
                    for b in range(KC):
                        last = nc.tensor.transpose(PS[:, bank, c * D + b * P:c * D + (b + 1) * P], nat[:, b, c * P:(c + 1) * P], identf[:, :])
                last.then_inc(prep_done, 1)
            pe.wait_ge(count_moved, NB)
            for d in range(NB):
                for b in range(NB):
                    nc.tensor.matmul(PS[:, 2, d:d + 1], count[:, b, d * P:(d + 1) * P], ones_f[:, 0:1], start=(b == 0), stop=(b == NB - 1))
            pe.wait_ge(totals_ready, 2)
            group_prefix(3)
            pe.wait_ge(adj_ready, NB)
            pe.wait_ge(prep_moved, 4)
            for c in range(KC):
                for b in range(NB):
                    last = nc.tensor.matmul(PS[:, 4 + c, :], x[:, b, c * P:(c + 1) * P], adj[:, b, :], start=(b == 0), stop=(b == NB - 1))
                last.then_inc(ax_done, 1)
            for b in range(NB):
                for c in range(KC):
                    last = nc.tensor.matmul(PS[:, 6 + b // 2, (b % 2) * D:(b % 2 + 1) * D], xT[:, c, b * P:(b + 1) * P], b0T[:, c, :],
                                            start=(c == 0), stop=(c == KC - 1))
            last.then_inc(bx_done, 1)
            pe.wait_ge(ax_moved, 2)
            for b in range(NB):
                for c in range(KC):
                    last = nc.tensor.matmul(PS[:, b // 2, (b % 2) * D:(b % 2 + 1) * D], axT[:, c, b * P:(b + 1) * P], w0T[:, c, :],
                                            start=(c == 0), stop=(c == KC - 1))
                if b % 2:
                    last.then_inc(l0_done, 1)

            def source_masks():
                for i in range(TILES // UN):
                    pe.wait_ge(hot_src_ready, i + 1)
                    if i >= 2:
                        pe.wait_ge(hotT_src_moved, i - 1)
                    for u in range(UN):
                        last = nc.tensor.transpose(PS[:, 6 + i % 2, :].bitcast(bf16)[:, u * P:(u + 1) * P], hot_src[:, i * UN + u, :], identb[:, :])
                    last.then_inc(hotT_src_done, 1)

            pe.wait_ge(x_ready, NB)
            transposes(x, (4, 5), xT_done)
            pe.wait_ge(xT_moved, 2)
            pe.wait_ge(wx_ready, 4 * KC)
            for b in range(NB):
                for c in range(KC):
                    last = nc.tensor.matmul(PS[:, b, 0:264], xT[:, c, b * P:(b + 1) * P], w1x[:, c, :], start=(c == 0), stop=(c == KC - 1))
                last.then_inc(feat_done, 1)
            source_masks()
            pe.wait_ge(feat_moved, NB)

            def for_later_layers():
                pe.wait_ge(loads["rel"], 16 * 9)
                for n in range(4):
                    for k in range(4):
                        last = nc.tensor.transpose(PS[:, SPARE[n], k * P:(k + 1) * P], att_nat[:, (n % 2) * 4 + k, n // 2, :], identf[:, :])
                    last.then_inc(att_done, 1)
                for d in range(NB):
                    if d >= 1:
                        pe.wait_ge(att_moved, 8 * d)
                    for b in range(NB):
                        last = nc.tensor.transpose(PS[:, SPARE[4 + d], b * P:(b + 1) * P], count[:, b, d * P:(d + 1) * P], identf[:, :])
                    last.then_inc(cT_done, 1)

            def edge_layer(g):
                bi = g * TILES // UN

                def near(s):
                    half = s % 2
                    if g == 1:
                        block = blocks_of(g, s * HALF)
                        if s >= 2:
                            pe.wait_ge(near_used, HALVES + 2 * (s - 1))
                    elif s >= 2:
                        pe.wait_ge(near_used, s - 1)
                    for u in range(HALF):
                        t = s * HALF + u
                        if g == 0:
                            dst = PS[:, 2 + half, u * H:(u + 1) * H]
                        else:
                            dst = PS[:, 2 + half * 2 + u // 2, (u % 2) * D:(u % 2 + 1) * D]
                        for k in range(3):
                            rhs = self3[:, k, t, :] if g == 0 else parts3[:, k, bass.ds(block[u], 1), :].rearrange("p o w -> p (o w)")
                            last = nc.tensor.matmul(dst, hotT[:, t, :], rhs, start=(k == 0), stop=(k == 2), skip_group_check=True)
                        if u == HALF - 1 or (g == 1 and u % 2):
                            last.then_inc(near_done, 1)

                def spread(s):
                    pe.wait_ge(score_ready, g * HALVES + s + 1)
                    for u in range(HALF):
                        if s > 0 and u % 2 == 0:
                            pe.wait_ge(wide_ready, 2 * (g * HALVES + s - 1) + u // 2 + 1)
                        t, r = s * HALF + u, (s % 2) * HALF + u
                        bank = PS[:, SPREAD[u], :].rearrange("p (h e) -> p h e", h=H)
                        if g == 0:
                            nc.tensor.matmul(bank, hot_src[:, t, :], bigI[:, :].unsqueeze(1).broadcast_to([P, H, P]), start=True, stop=False,
                                             skip_group_check=True)
                        else:
                            nc.tensor.matmul(bank, bigI[:, :], hotT[:, t, :].unsqueeze(1).broadcast_to([P, H, P]), start=True, stop=False,
                                             skip_group_check=True)
                            nc.tensor.matmul(PS[:, SPREAD[u], :], bigI[:, :], minus_one.broadcast_to([P, BANK]), start=False, stop=False,
                                             skip_group_check=True)
                        for h in range(H):
                            last = nc.tensor.matmul(bank[:, h, :], score_b[:, r, h:h + 1].broadcast_to([P, P]), identb[:, :],
                                                    start=False, stop=(h == H - 1), skip_group_check=True)
                        if u % 2:
                            last.then_inc(spread_done, 1)

                if g == 0:
                    pe.wait_ge(hotT_src_moved, TILES // UN)
                else:
                    pe.wait_ge(hotT_ready, 1)
                near(0)
                for s in range(HALVES):
                    if s + 1 < HALVES:
                        near(s + 1)
                    spread(s)

                if g == 0:
                    pe.wait_ge(wide_ready, 2 * HALVES)
                    for_later_layers()
                pe.wait_ge(max_ready, g + 1)

                for t in range(TILES):
                    last = nc.tensor.matmul(PS[:, 0, t * H:(t + 1) * H], hotT[:, t, :], tile_max[:, t, :], start=True, stop=True,
                                            skip_group_check=True)
                last.then_inc(maxe_done, 1)
                if g == 0:
                    pe.wait_ge(cT_moved, NB)
                for b in range(NB):
                    nc.tensor.matmul(PS[:, 4 + b, 0:W1], onesb[:, :], zerob[:, :], start=True, stop=False, skip_group_check=True)

                def sums_turn(i):
                    for u in range(UN):
                        if u % HALF == 0:
                            block = blocks_of(g, i * UN + u)
                            pe.wait_ge(message_ready, (i + bi) * 2 + (u // HALF + 1))
                            pe.wait_ge(hotf_ready, (i + bi) * 2 + (u // HALF + 1))
                        src = rows1[:, bass.ds(i * UN + u, 1), :] if g == 0 else rows3[:, bass.ds(i * UN + u, 1), D - 4:W3]
                        nc.tensor.matmul(sums[:, bass.ds(block[u % HALF] * BANK, W1)], hotf[:, u, :], src.rearrange("p o w -> p (o w)"),
                                         start=False, stop=False, skip_group_check=True).then_inc(summed, 1)

                for i in turns(pe, 0, TILES // UN):
                    sums_turn(i)
                for b in range(NB):
                    last = nc.tensor.matmul(PS[:, 4 + b, 0:W1], onesb[:, :], zerob[:, :], start=False, stop=True, skip_group_check=True)
                last.then_inc(sums_done, 1)

            pe.wait_ge(self_split, 1)
            edge_layer(0)

            pe.wait_ge(slots_loaded[1], 16)
            nc.tensor.transpose(PS[0:TILES, 3, 0:P], slots[1][:, :, 0], identf[:, :]).then_inc(loc_done, 1)

            pe.wait_ge(x_ready, 2 * NB)
            transposes(x, (0, 1), xT_done)
            pe.wait_ge(xT_moved, 4)
            pe.wait_ge(loc_moved, 1)
            for h in range(H):
                for c in range(KC):
                    last = nc.tensor.matmul(PS[:, h, :], w2x[:, c, 260 + h:261 + h].broadcast_to([P, P]), xT[:, c, :],
                                            start=(c == 0), stop=(c == KC - 1))
                last.then_inc(spread2_done, 1)
                b = h
                for c in range(KC):
                    last = nc.tensor.matmul(PS[:, 4 + b, 0:260], xT[:, c, b * P:(b + 1) * P], w2x[:, c, 0:260], start=(c == 0), stop=(c == KC - 1))
                last.then_inc(h_done, 1)
            pe.wait_ge(h_moved, NB)
            for b in range(NB):
                for h in range(H):
                    pair_weights_done(pe, b * H + h)
                    last = nc.tensor.matmul(PS[0:DK + 1, 4 + h, :], hx[:, b, h, :], pair_w[:, b, h, :], start=(b == 0), stop=(b == NB - 1))
                    if b == NB - 1:
                        last.then_inc(hpT_done, 1)
            for h in range(H):
                pe.wait_ge(hpT_moved, h + 1)
                for s in range(NB):
                    last = nc.tensor.transpose(PS[:, s, h * 65:(h + 1) * 65], hpT[0:DK + 1, h, s * P:(s + 1) * P], identf[0:DK + 1, 0:DK + 1])
            last.then_inc(hp_done, 1)

            pe.wait_ge(x_ready, 3 * NB)
            transposes(x, (0, 1), xT_done)
            pe.wait_ge(loads["kqv"], 48)
            for k, bank in ((0, 4), (2, 2)):
                for o in range(KC):
                    for t in range(TYPES):
                        pe.wait_ge(xm_ready, t + 1)
                        for c in range(KC):
                            last = nc.tensor.matmul(PS[:, bank + o, :], kqv[:, k, t, c, o * P:(o + 1) * P], xmT[:, t, c, :],
                                                    start=(t == 0 and c == 0), stop=(t == TYPES - 1 and c == KC - 1))
                        if t == TYPES - 1:
                            last.then_inc(kv_done, 1)
            pe.wait_ge(kv_moved, 4)
            n = 0
            for b in range(NB):
                for a in range(2):
                    for r in range(0, RELS, 4):
                        if n >= 2:
                            pe.wait_ge(rel_moved_a, n - 1)
                        nc.tensor.matmul(PS[:, n % 2, :], kT[:, a, b * P:(b + 1) * P], attT[:, a, r:r + 4, :].rearrange("p r w -> p (r w)"),
                                         start=True, stop=True).then_inc(rel_done, 1)
                        if n >= 2:
                            pe.wait_ge(rel_moved_v, n - 1)
                        nc.tensor.matmul(PS[:, 4 + n % 2, :], vT[:, a, b * P:(b + 1) * P], msgD[:, a, r:r + 4, :].rearrange("p r w -> p (r w)"),
                                         start=True, stop=True).then_inc(rel_done, 1)
                        n += 1
            for b in range(NB):
                for t in range(TYPES):
                    for c in range(KC):
                        last = nc.tensor.matmul(PS[:, 6 + b // 2, (b % 2) * D:(b % 2 + 1) * D], xmT[:, t, c, b * P:(b + 1) * P], kqv[:, 1, t, c, :],
                                                start=(t == 0 and c == 0), stop=(t == TYPES - 1 and c == KC - 1))
                if b % 2:
                    last.then_inc(q_done, 1)
            pe.wait_ge(q_split, 2)
            pe.wait_ge(rel_moved_a, 16)
            pe.wait_ge(rel_moved_v, 16)
            edge_layer(1)
            pe.wait_ge(agg_ready, 1)
            transposes(agg, (0, 1), xT_done)
            pe.wait_ge(loads["alin"], 16)
            pe.wait_ge(xT_moved, 8)
            for b in range(NB):
                for t in range(TYPES):
                    for c in range(KC):
                        last = nc.tensor.matmul(PS[:, 2 * b + t // 2, (t % 2) * D:(t % 2 + 1) * D], aggT[:, c, b * P:(b + 1) * P], alin[:, t, c, :],
                                                start=(c == 0), stop=(c == KC - 1))
                    if t % 2:
                        last.then_inc(o_done, 1)

        @block.scalar
        def _(act):
            def copy(dst, src, done, n=1):
                nc.scalar.activation(dst, src, ACT.Copy).then_inc(done, n)

            act.wait_ge(hots_used, EC)
            for b in range(NB):
                copy(count[:, b, :], PS[:, b, :], count_moved)
            for n, (dst, bank) in enumerate(((xT[:, 0, :], 5), (xT[:, 1, :], 6), (w0T.rearrange("p c o -> p (c o)"), 7),
                                             (b0T.rearrange("p c o -> p (c o)"), 4))):
                act.wait_ge(prep_done, n + 1)
                copy(dst, PS[:, bank, :], prep_moved)
            for c in range(KC):
                act.wait_ge(ax_done, c + 1)
                copy(axT[:, c, :], PS[:, 4 + c, :], ax_moved)

            def deviations(k):
                act.wait_ge(var_ready, k)
                nc.scalar.activation(small[:, 64:68], small[:, 60:64], ACT.Sqrt).then_inc(std_ready, 1)

            def move_xT(k, banks):
                dst = aggT if k == 4 else xT
                for c in range(KC):
                    act.wait_ge(xT_done, 2 * (k - 1) + c + 1)
                    copy(dst[:, c, :], PS[:, banks[c], :], xT_moved)

            def source_hotT():
                for i in range(TILES // UN):
                    act.wait_ge(hotT_src_done, i + 1)
                    nc.scalar.activation(hotT[:, i * UN:(i + 1) * UN, :].rearrange("p t n -> p (t n)"), PS[:, 6 + i % 2, :].bitcast(bf16),
                                         ACT.Copy, bias=1.0).then_inc(hotT_src_moved, 1)

            def move_spread(g, s, first=False):
                for pair in range(2):
                    act.wait_ge(spread_done, s * 2 + (2 * g * HALVES + pair + 1))
                    if pair == 0 and not first:
                        act.wait_ge(wide_used, s + g * HALVES)
                    copy(wide[:, 2 * pair:2 * pair + 2, :, :].rearrange("p t h e -> p t (h e)"), PS[:, SPREAD[2 * pair]:SPREAD[2 * pair] + 2, :], wide_ready)

            def edge_layer(g):
                move_spread(g, 0, g == 0)
                for s in turns(act, 1, HALVES):
                    move_spread(g, s)
                if g == 0:
                    act.wait_ge(priors_ready, 1)
                    for n in range(4):
                        act.wait_ge(att_done, n + 1)
                        for k in range(8):
                            a, rel, z = n // 2, (n % 2) * 4 + k // 2, k % 2
                            nc.scalar.activation(attT[:, a, rel, z * DK:(z + 1) * DK], PS[:, SPARE[n], (k // 2) * P + z * DK:(k // 2) * P + (z + 1) * DK],
                                                 ACT.Copy, scale=pri_bc[:, rel * H + 2 * a + z:rel * H + 2 * a + z + 1]).then_inc(att_moved, 1)
                    for d in range(NB):
                        act.wait_ge(cT_done, d + 1)
                        copy(countT[:, d, :], PS[:, SPARE[4 + d], :], cT_moved)
                act.wait_ge(diff_ready, g + 1)
                dst = rows1[:, :, 0:4] if g == 0 else rows3[:, :, D - 4:D]
                nc.scalar.activation(dst, score[:, :, :], ACT.Exp).then_inc(exp_ready, 1)
                if g == 0:
                    source_hotf(0, True)
                    for i in turns(act, 1, TILES // UN):
                        source_hotf(i, False)

            def source_hotf(i, first):
                for half in range(2):
                    if not first:
                        act.wait_ge(summed, i * UN + (half * HALF + HALF - UN))
                    nc.scalar.activation(hotf[:, half * HALF:(half + 1) * HALF, :], hot_src[:, bass.ds(i * UN + half * HALF, HALF), :],
                                         ACT.Copy, bias=1.0).then_inc(hotf_ready, 1)

            deviations(1)
            move_xT(1, (4, 5))
            for b in range(NB):
                act.wait_ge(feat_done, b + 1)
                copy(feat1[:, b, :], PS[:, b, 0:264], feat_moved)
            source_hotT()
            edge_layer(0)
            act.wait_ge(loc_done, 1)
            copy(loc_rows[:, :], PS[0:TILES, 3, 0:P], loc_moved)
            deviations(2)
            move_xT(2, (0, 1))
            for b in range(NB):
                act.wait_ge(h_moved, b + 1)
                for h in range(H):
                    n = b * H + h
                    if n < H:
                        act.wait_ge(spread2_done, h + 1)
                    if n >= 4:
                        pair_weights_done(act, n - 4)
                    nc.scalar.activation(exp_ring[:, n % 4, 0, :], PS[:, h, :], ACT.Exp, bias=a_neg[:, 0, b, h:h + 1], scale=-1.0)
                    nc.scalar.activation(exp_ring[:, n % 4, 1, :], PS[:, h, :], ACT.Exp, bias=a_neg[:, 1, b, h:h + 1], scale=-0.2).then_inc(pexp_ready, 1)
            for h in range(H):
                act.wait_ge(hpT_done, h + 1)
                copy(hpT[0:DK + 1, h, :], PS[0:DK + 1, 4 + h, :], hpT_moved)
            for k in range(2):
                f = slice(2 * k * D, 2 * (k + 1) * D)
                act.wait_ge(elu_in, k + 1)
                nc.scalar.activation(elu_tmp[:, 1, f], elu_tmp[:, 0, f], ACT.Exp).then_inc(act_step, 1)
                act.wait_ge(act_step, k + 1)
                nc.scalar.activation(elu_tmp[:, 1, f], elu_tmp[:, 1, f], ACT.Exp, bias=minus_one_f).then_inc(elu_exp, 1)
            act.wait_ge(loads["types"], 48)
            nc.scalar.activation(skip_e[:, 1, :], skip_e[:, 0, :], ACT.Exp, scale=-1.0).then_inc(skip_exp, 1)
            deviations(3)
            move_xT(3, (0, 1))
            for n, dst in enumerate((kT[:, 0, :], kT[:, 1, :], vT[:, 0, :], vT[:, 1, :])):
                act.wait_ge(kv_done, n + 1)
                copy(dst, PS[:, (4, 5, 2, 3)[n], :], kv_moved)
            n = 0
            for b in range(NB):
                if b >= 2:
                    act.wait_ge(t3_written[b % 2], 16)
                for a in range(2):
                    for r in range(0, RELS, 4):
                        act.wait_ge(rel_done, 2 * n + 1)
                        copy(stage[:, b % 2, r:r + 4, a * P:(a + 1) * P], PS[:, n % 2, :].rearrange("p (r w) -> p r w", r=4), rel_moved_a)
                        n += 1
            edge_layer(1)
            move_xT(4, (0, 1))
            for b in range(NB):
                act.wait_ge(var_ready, 4 + b)
                nc.scalar.activation(small[:, 64 + b:65 + b], small[:, 60 + b:61 + b], ACT.Sqrt).then_inc(std_ready, 1)

        @block.vector
        def _(dve):
            v = nc.vector
            steps = [0]

            def then(ins):
                steps[0] += 1
                ins.then_inc(dve_step, 1)
                dve.wait_ge(dve_step, steps[0])

            def signal(ins):
                steps[0] += 1
                ins.then_inc(dve_step, 1)
                return steps[0]

            T = group_tmp
            ind = T[:, 0:272].rearrange("p (k j) -> p k j", k=NB)
            scan = T[:, 272:544].rearrange("p (k j) -> p k j", k=NB)
            place = T[:, 544:816].rearrange("p (k j) -> p k j", k=NB)
            loc_i, blk_i, pos_i, low_i = [T[:, 816 + n * EC:816 + (n + 1) * EC].bitcast(i32) for n in range(4)]
            pad_i, pad_j = T[:, 1088:1092].bitcast(i32), T[:, 1092:1096].bitcast(i32)
            pad_f, start, base = T[:, 1096:1100], T[:, 1100:1104], T[:, 1104:1108]

            def group_totals(g):
                key = edges_i[:, g, :]
                v.tensor_scalar(loc_i, key, P - 1, None, ALU.bitwise_and)
                v.memset(payload[g][:, :, 3], 0.0)
                then(v.tensor_scalar(blk_i, key, 7, None, ALU.arith_shift_right))
                v.tensor_copy(payload[g][:, :, 0], loc_i)
                if g == 0:
                    v.tensor_copy(payload[g][:, :, 1].bitcast(i32), edges_i[:, 1, :])
                else:
                    v.scalar_tensor_tensor(payload[g][:, :, 1].bitcast(i32), edges_i[:, 2, :], float(N), edges_i[:, 0, :], ALU.mult, ALU.add)
                v.tensor_copy(payload[g][:, :, 2], edge_w)
                for k in range(NB):
                    ins = v.tensor_scalar(ind[:, k, :], blk_i, float(k), None, ALU.is_equal)
                then(ins)
                for k in range(NB):
                    ins = v.tensor_tensor_scan(scan[:, k, :], ones_f[:, 0:EC], ind[:, k, :], 0.0, ALU.mult, ALU.add)
                then(ins)
                v.tensor_copy(small[:, 0:2].bitcast(bf16), scan[:, :, EC - 1]).then_inc(totals_ready, 1)

            def group_addresses(g, bank):
                dve.wait_ge(prefix_done, g + 1)
                then(v.tensor_scalar(pad_i, PS[:, bank, 4:8], float(P - 1), None, ALU.add))
                then(v.tensor_scalar(pad_j, pad_i, -P, None, ALU.bitwise_and))
                then(v.tensor_copy(pad_f, pad_j))
                then(v.memset(start[:, 0:1], 0.0))
                for k in range(1, NB):
                    then(v.tensor_tensor(start[:, k:k + 1], start[:, k - 1:k], pad_f[:, k - 1:k], ALU.add))
                then(v.scalar_tensor_tensor(base, PS[:, bank, 0:4], -1.0, start, ALU.add, ALU.add))
                for k in range(NB):
                    ins = v.scalar_tensor_tensor(place[:, k, :], scan[:, k, :], base[:, k:k + 1], ind[:, k, :], ALU.add, ALU.mult)
                then(ins)
                then(v.tensor_tensor(place[:, 0:2, :], place[:, 0:2, :], place[:, 2:4, :], ALU.add))
                then(v.tensor_tensor(pos_i, place[:, 0, :], place[:, 1, :], ALU.add))
                then(v.tensor_scalar(low_i, pos_i, P - 1, None, ALU.bitwise_and))
                then(v.tensor_scalar(blk_i, pos_i, 7, None, ALU.arith_shift_right))
                v.scalar_tensor_tensor(address[g][:, :], low_i, float(TILES), blk_i, ALU.mult, ALU.add).then_inc(address_ready, 1)
                then(v.tensor_scalar(block_f, tile_at[:, :], start[:, 1:2], None, ALU.is_ge))
                then(v.scalar_tensor_tensor(block_f, tile_at[:, :], start[:, 2:3], block_f, ALU.is_ge, ALU.add))
                then(v.scalar_tensor_tensor(block_f, tile_at[:, :], start[:, 3:4], block_f, ALU.is_ge, ALU.add))
                then(v.tensor_copy(block_of[g][:, :], block_f))

            dve.wait_ge(loads["edges"], 64)
            dve.wait_ge(fixed, 10)
            group_totals(0)
            then(v.tensor_copy(ends_f[:, :, :], edges_i[:, 0:2, :]))

            def hot_turn(i, first, n=UN):
                for u in range(n):
                    if not first:
                        dve.wait_ge(hots_used, i * UN + (u - (UN - 1)))
                    for k in range(2):
                        ins = v.tensor_scalar(hot_ring[:, u, k, :], iota16[:, :], ends_f[:, k, bass.ds(i * UN + u, 1)], None, ALU.is_equal)
                    ins.then_inc(hots_ready, 1)

            hot_turn(0, True)
            group_addresses(0, 4)
            for i in turns(dve, 1, 6):
                hot_turn(i, False)
            group_totals(1)
            for i in turns(dve, 6, EC // UN):
                hot_turn(i, False)
            hot_turn(EC // UN, False, EC % UN)
            dve.wait_ge(loads["types"], 48)
            for t in range(TYPES):
                v.tensor_scalar(mask[:, t, :], type_row, float(t), None, ALU.is_equal)

            for b in range(NB):
                dve.wait_ge(count_moved, b + 1)
                v.tensor_scalar(adj[:, b, :], count[:, b, :], 1.0, None, ALU.min).then_inc(adj_ready, 1)

            mv = small[:, 40:48].rearrange("p (b k) -> p b k", k=2)
            stats = small[:, 8:32].rearrange("p (b k) -> p b k", k=6)

            def layernorm(k):
                for b in range(NB):
                    ins = v.bn_stats(stats[:, b, :], x[:, b, :])
                then(ins)
                for b in range(NB):
                    ins = v.bn_aggr(mv[:, b, :], stats[:, b, :])
                then(ins)
                v.tensor_scalar(small[:, 60:64], mv[:, :, 1], EPS, None, ALU.add).then_inc(var_ready, 1)
                dve.wait_ge(std_ready, k)
                then(v.reciprocal(small[:, 68:72], small[:, 64:68]))
                for b in range(NB):
                    v.tensor_scalar(x[:, b, :], x[:, b, :], mv[:, b, 0:1], small[:, 68 + b:69 + b], ALU.subtract, ALU.mult).then_inc(x_ready, 1)

            group_addresses(1, 3)
            dve.wait_ge(loads["w1"], 16 * 5)
            dve.wait_ge(loads["w2"], 16 * 3)
            a2 = abc[:, 2:4, :].rearrange("p k f -> p (k f)").rearrange("p (h z f) -> p z h f", h=H, z=2)
            tmp3 = wa_tmp.rearrange("p (h f) -> p h f", h=H)
            vectors = 0
            for c in range(KC):
                w1h = w1x[:, c, 4:4 + D].rearrange("p (h f) -> p h f", h=H)
                w2h = w2x[:, c, 0:D].rearrange("p (h f) -> p h f", h=H)
                for wh, vec, dst in ((w1h, abc[:, 0, :].rearrange("p (h f) -> p h f", h=H), w1x[:, c, 0:4]),
                                     (w1h, abc[:, 1, :].rearrange("p (h f) -> p h f", h=H), w1x[:, c, 260:264]),
                                     (w2h, a2[:, 1, :, :], w2x[:, c, 256:260]),
                                     (w2h, a2[:, 0, :, :], w2x[:, c, 260:264])):
                    then(v.tensor_tensor(tmp3, wh, vec, ALU.mult))
                    v.tensor_reduce(dst, tmp3, X, ALU.add).then_inc(wx_ready, 1)
                    vectors += 1
                    dve.wait_ge(wx_ready, vectors)
            dve.wait_ge(bx_done, 1)
            v.tensor_tensor(xb0.rearrange("p b f -> p (b f)"), x[:, :, :].rearrange("p b f -> p (b f)"),
                            PS[:, 6:8, :].rearrange("p b f -> p (b f)"), ALU.add)
            dve.wait_ge(l0_done, 1)
            then(v.tensor_scalar(small[:, 32:36], PS[:, 2, 0:4], 1.0, None, ALU.max))
            then(v.reciprocal(small[:, 36:40], small[:, 32:36]))
            for b in range(NB):
                dve.wait_ge(l0_done, b // 2 + 1)
                ins = v.scalar_tensor_tensor(x[:, b, :], PS[:, b // 2, (b % 2) * D:(b % 2 + 1) * D], small[:, 36 + b:37 + b], xb0[:, b, :], ALU.mult, ALU.add)
            then(ins)
            layernorm(1)

            def split(dst, src, rest):
                then(v.tensor_copy(dst[0], src))
                then(v.tensor_tensor(rest, src, dst[0], ALU.subtract))
                then(v.tensor_copy(dst[1], rest))
                then(v.tensor_tensor(rest, rest, dst[1], ALU.subtract))
                return v.tensor_copy(dst[2], rest)

            dve.wait_ge(slots_loaded[0], 16)

            def source_hots(i):
                for u in range(UN):
                    ins = v.tensor_scalar(hot_src[:, bass.ds(i * UN + u, 1), :].rearrange("p o n -> p (o n)"), iota16[:, 0:P],
                                          slots[0][:, bass.ds(i * UN + u, 1), 0], 1.0, ALU.is_equal, ALU.subtract)
                ins.then_inc(hot_src_ready, 1)

            for i in turns(dve, 0, TILES // UN):
                source_hots(i)

            def by_tile(f, h):
                return f.unsqueeze(2).broadcast_to([P, TILES, H]) if h is None else h.unsqueeze(1).broadcast_to([P, TILES, H])

            for b in range(NB):
                v.tensor_scalar(others[:, b, :], block_of[0][:, :], float(b), None, ALU.is_equal).then_inc(dve_step, 1)
                steps[0] += 1
            dve.wait_ge(dve_step, steps[0])
            dve.wait_ge(feat_moved, NB)
            own_f = comb[:, :, :].rearrange("p h t -> p (h t)").rearrange("p (t h) -> p t h", h=H)
            then(v.tensor_tensor(own_f, by_tile(others[:, 0, :], None), by_tile(None, feat1[:, 0, 260:264]), ALU.mult))
            for b in range(1, NB):
                then(v.tensor_tensor(tmax[:, :, :], by_tile(others[:, b, :], None), by_tile(None, feat1[:, b, 260:264]), ALU.mult))
                then(v.tensor_tensor(own_f, own_f, tmax[:, :, :], ALU.add))
            split([self3[:, k, :, :] for k in range(3)], own_f, tmax[:, :, :]).then_inc(self_split, 1)

            dve.wait_ge(loads["rel"], 16 * 9)
            v.tensor_scalar(pri_bc, pri_bc, DK ** -0.5, None, ALU.mult).then_inc(priors_ready, 1)

            def source_scores():
                for s in range(HALVES + 1):
                    if s < HALVES:
                        t0, half = s * HALF, s % 2
                        for u in range(HALF):
                            dve.wait_ge(gathered[0][u], 16 * (s + 1))
                        dve.wait_ge(near_done, s + 1)
                        z = zt[:, 0, :].rearrange("p (t h) -> p t h", t=HALF)
                        y = zt[:, 1, :].rearrange("p (t h) -> p t h", t=HALF)
                        own = PS[:, 2 + half, 0:HALF * H].rearrange("p (t h) -> p t h", t=HALF)
                        v.tensor_tensor(z, rows1[:, t0:t0 + HALF, 0:4], own, ALU.add).then_inc(near_used, 1)
                        dve.wait_ge(near_used, s + 1)
                        then(v.scalar_tensor_tensor(y, z, 0.2, z, ALU.mult, ALU.max))
                        weight = slots[0][:, t0:t0 + HALF, 2:3].broadcast_to([P, HALF, H])
                        v.tensor_tensor(score_b[:, half * HALF:(half + 1) * HALF, :], y, weight, ALU.mult).then_inc(score_ready, 1)
                        v.tensor_tensor(score[:, t0:t0 + HALF, :], y, weight, ALU.mult)
                    m = s - 1
                    if m >= 0:
                        dve.wait_ge(wide_ready, 2 * (m + 1))
                        v.tensor_tensor(narrow, wide[:, :, :, 0:P // 2].rearrange("p t h e -> p (t h) e"),
                                        wide[:, :, :, P // 2:P].rearrange("p t h e -> p (t h) e"), ALU.max).then_inc(wide_used, 1)
                        dve.wait_ge(wide_used, m + 1)
                        then(v.tensor_tensor(narrow[:, :, 0:P // 4], narrow[:, :, 0:P // 4], narrow[:, :, P // 4:P // 2], ALU.max))
                        then(v.tensor_reduce(tmax[:, m * HALF:(m + 1) * HALF, :].rearrange("p t h -> p (t h)"), narrow[:, :, 0:P // 4], X, ALU.max))

            def target_scores():
                seen = {}

                def mark(name, ins):
                    steps[0] += 1
                    ins.then_inc(dve_step, 1)
                    seen[name] = steps[0]

                def after(name):
                    if name in seen:
                        dve.wait_ge(dve_step, seen[name])

                def product(s, pair):
                    t = s * HALF + 2 * pair
                    dve.wait_ge(near_done, HALVES + 2 * s + pair + 1)
                    after(("read", pair))
                    own = PS[:, 2 + (s % 2) * 2 + pair, :].rearrange("p (t f) -> p t f", t=2)
                    v.tensor_tensor(products[pair], rows3[:, t:t + 2, 0:D], own, ALU.mult).then_inc(near_used, 1)

                def head_sums(s, pair):
                    t = s * HALF + 2 * pair
                    dve.wait_ge(near_used, HALVES + 2 * s + pair + 1)
                    mark(("read", pair), v.tensor_reduce(score[:, t:t + 2, :].rearrange("p t h -> p (t h)"),
                                                         products[pair].rearrange("p t (h w) -> p (t h) w", h=H), X, ALU.add))

                for s in range(HALVES + 2):
                    m = s - 2
                    if s < HALVES:
                        for u in range(HALF):
                            dve.wait_ge(gathered[1][u], 16 * (s + 1))
                        product(s, 0)
                    if m >= 0:
                        dve.wait_ge(wide_ready, 2 * (HALVES + m + 1))
                        after("maximum")
                        v.tensor_tensor(narrow3, wide[:, :, :, 0:P // 2].rearrange("p t h e -> p (t h) e"),
                                        wide[:, :, :, P // 2:P].rearrange("p t h e -> p (t h) e"), ALU.max).then_inc(wide_used, 1)
                    if s < HALVES:
                        product(s, 1)
                    if m >= 0:
                        dve.wait_ge(wide_used, HALVES + m + 1)
                        mark("narrow", v.tensor_tensor(narrow3[:, :, 0:P // 4], narrow3[:, :, 0:P // 4], narrow3[:, :, P // 4:P // 2], ALU.max))
                    if s < HALVES:
                        head_sums(s, 0)
                        head_sums(s, 1)
                    if m >= 0:
                        after("narrow")
                        mark("maximum", v.tensor_reduce(tmax[:, m * HALF:(m + 1) * HALF, :].rearrange("p t h -> p (t h)"), narrow3[:, :, 0:P // 4], X, ALU.max))
                    if s < HALVES:
                        after(("read", 1))
                        v.tensor_copy(score_b[:, (s % 2) * HALF:(s % 2 + 1) * HALF, :], score[:, s * HALF:(s + 1) * HALF, :]).then_inc(score_ready, 1)
                after("maximum")

            def edge_layer(g):
                bi = g * TILES // UN

                for b in range(NB):
                    ins = v.tensor_scalar(others[:, b, :], block_of[g][:, :], float(b), -BIG, ALU.not_equal, ALU.mult)
                then(ins)
                source_scores() if g == 0 else target_scores()

                by_head = tmax[:, :, :].rearrange("p t h -> p h t")
                two = [comb[:, :, :], prod.rearrange("p k f -> p (k f)")[:, 0:H * TILES].rearrange("p (h t) -> p h t", h=H)]

                def in_block(b):
                    return signal(v.tensor_tensor(two[b % 2], by_head, others[:, b, :].unsqueeze(1).broadcast_to([P, H, TILES]), ALU.add))

                masked = [in_block(0), in_block(1)]
                for b in range(NB):
                    dve.wait_ge(dve_step, masked[b])
                    reduced = signal(v.tensor_reduce(node_max[:, b, :], two[b % 2], X, ALU.max))
                    if b + 2 < NB:
                        dve.wait_ge(dve_step, reduced)
                        masked.append(in_block(b + 2))
                dve.wait_ge(dve_step, reduced)
                own_max = comb[:, :, :].rearrange("p h t -> p (h t)").rearrange("p (t h) -> p t h", h=H)
                before_b = [0] * H
                for b in range(NB):
                    for h in range(H):
                        if b == 0:
                            ins = v.tensor_scalar(own_max[:, :, h], others[:, b, :], node_max[:, b, h:h + 1], None, ALU.add)
                        else:
                            dve.wait_ge(dve_step, before_b[h])
                            ins = v.scalar_tensor_tensor(tile_max[:, :, h] if b == NB - 1 else own_max[:, :, h], others[:, b, :],
                                                         node_max[:, b, h:h + 1], own_max[:, :, h], ALU.add, ALU.max)
                        if b < NB - 1:
                            before_b[h] = signal(ins)
                ins.then_inc(max_ready, 1)
                dve.wait_ge(maxe_done, g + 1)
                v.tensor_tensor(score[:, :, :], score[:, :, :], PS[:, 0, 0:TILES * H].rearrange("p (t h) -> p t h", h=H), ALU.subtract)\
                    .then_inc(diff_ready, 1)
                dve.wait_ge(exp_ready, g + 1)

                def messages(i, half, first=False):
                    t0 = i * UN + half * HALF
                    if g == 1:
                        for u in range(half * HALF + 2, (half + 1) * HALF):
                            if not first:
                                dve.wait_ge(summed, i * UN + (u + 1 - UN + TILES))
                            v.tensor_scalar(hotf[:, u, :], iota16[:, 0:P], slots[1][:, bass.ds(i * UN + u, 1), 0], None, ALU.is_equal)
                    if g == 0:
                        feats, ex = rows1[:, bass.ds(t0, HALF), 4:W1], rows1[:, bass.ds(t0, HALF), 0:4]
                    else:
                        feats, ex = rows3[:, bass.ds(t0, HALF), D:W3], rows3[:, bass.ds(t0, HALF), D - 4:D]
                    feats = feats.rearrange("p t (h f) -> p t h f", h=H)
                    v.tensor_tensor(feats, feats, ex.unsqueeze(3).broadcast_to([P, HALF, H, DK]), ALU.mult).then_inc(message_ready, 1)

                for half in range(2):
                    messages(0, half, True)
                for i in turns(dve, 1, TILES // UN):
                    for half in range(2):
                        messages(i, half)
                dve.wait_ge(sums_done, g + 1)

            rden = small[:, 88:104].rearrange("p (b h) -> p b h", b=NB)

            def denominators(col, bank):
                then(v.tensor_scalar(rden, PS[:, bank:bank + NB, col[0]:col[0] + col[1] * (H - 1) + 1:col[1]], 1e-30, None, ALU.max))
                then(v.reciprocal(rden, rden))

            edge_layer(0)
            denominators((0, 1), 4)
            o1 = part(0, 1024).rearrange("p (b f) -> p b f", b=NB)
            for b in range(NB):
                ins = v.tensor_tensor(o1[:, b, :].rearrange("p (h f) -> p h f", h=H), PS[:, 4 + b, 4:W1].rearrange("p (h f) -> p h f", h=H),
                                      rden[:, b, :].unsqueeze(2).broadcast_to([P, H, DK]), ALU.mult)
            then(ins)
            then(v.tensor_tensor(o1, o1, bias1[:, :].unsqueeze(1).broadcast_to([P, NB, D]), ALU.add))
            then(v.scalar_tensor_tensor(x[:, :, :], o1, 0.0, x[:, :, :], ALU.max, ALU.add))
            layernorm(2)

            v.memset(hx[:, :, :, 64], 1.0)
            def move_h(b):
                dve.wait_ge(h_done, b + 1)
                then(v.tensor_scalar(h_neg[:, 0:260], PS[:, 4 + b, 0:260], 0.0, None, ALU.min))
                v.scalar_tensor_tensor(a_dst[:, b, :], PS[:, 4 + b, D:260], 0.0, h_neg[:, D:260], ALU.max, ALU.add)
                then(v.scalar_tensor_tensor(hx[:, b, :, 0:64], PS[:, 4 + b, 0:D].rearrange("p (h f) -> p h f", h=H), 0.0,
                                            h_neg[:, 0:D].rearrange("p (h f) -> p h f", h=H), ALU.max, ALU.add))
                v.tensor_scalar(a_neg[:, 0, b, :], a_dst[:, b, :], -1.0, None, ALU.mult)
                v.tensor_scalar(a_neg[:, 1, b, :], a_dst[:, b, :], -0.2, None, ALU.mult).then_inc(h_moved, 1)

            def pair(n):
                dve.wait_ge(pexp_ready, n + 1)
                ins = v.scalar_tensor_tensor(exp_ring[:, n % 4, 0, :], exp_ring[:, n % 4, 0, :], 0.0, exp_ring[:, n % 4, 1, :], ALU.max, ALU.min)
                if n % 2:
                    ins.then_inc(pmin_ready, 1)
                else:
                    then(ins)
                    v.tensor_tensor(pair_w[:, n // H, n % H, :], exp_ring[:, n % 4, 0, :], countT[:, n // H, :], ALU.mult).then_inc(pw_ready, 1)

            move_h(0)
            move_h(1)
            pair(0)
            move_h(2)
            pair(1)
            move_h(3)
            for n in range(2, NB * H):
                pair(n)
            dve.wait_ge(hp_done, 1)
            denominators((64, 65), 0)
            hp = part(0, 1024).rearrange("p (b h f) -> p b h f", b=NB, h=H)
            halves = [slice(0, 2 * D), slice(2 * D, 4 * D)]
            hp_flat = part(0, 1024)
            for k in range(2):
                for b in range(2 * k, 2 * k + 2):
                    ins = v.tensor_tensor(hp[:, b, :, :], PS[:, b, 0:260].rearrange("p (h w) -> p h w", h=H)[:, :, 0:64],
                                          rden[:, b, :].unsqueeze(2).broadcast_to([P, H, DK]), ALU.mult)
                then(ins)
                v.tensor_scalar(elu_tmp[:, 0, halves[k]], hp_flat[:, halves[k]], 0.0, None, ALU.min).then_inc(elu_in, 1)
            xf = x[:, :, :].rearrange("p b f -> p (b f)")
            positive = [signal(v.scalar_tensor_tensor(xf[:, f], hp_flat[:, f], 0.0, xf[:, f], ALU.max, ALU.add)) for f in halves]
            for k, f in enumerate(halves):
                dve.wait_ge(dve_step, positive[k])
                dve.wait_ge(elu_exp, k + 1)
                ins = v.scalar_tensor_tensor(xf[:, f], elu_tmp[:, 1, f], 1.0, xf[:, f], ALU.subtract, ALU.add)
            then(ins)
            layernorm(3)

            dve.wait_ge(xT_moved, 6)
            for t in range(TYPES):
                v.tensor_tensor(xmT[:, t, :, :], xT[:, :, :], mask[:, t, :].unsqueeze(1).broadcast_to([P, KC, N]), ALU.mult).then_inc(xm_ready, 1)
            dve.wait_ge(loc_spread, 16)
            dve.wait_ge(index_made, 1)
            hotT_flat = hotT[:, :, :].rearrange("p t n -> p (t n)")
            v.tensor_scalar(hotT_flat, hotT_flat, partition, None, ALU.is_equal).then_inc(hotT_ready, 1)
            dve.wait_ge(skip_exp, 1)
            then(v.tensor_scalar(skip_e[:, 1, :], skip_e[:, 1, :], 1.0, None, ALU.add))
            then(v.reciprocal(skip_e[:, 2, :], skip_e[:, 1, :]))
            for t in range(TYPES):
                ins = v.tensor_scalar(type_w[:, :, t], types_i, float(t), None, ALU.is_equal)
            then(ins)
            v.tensor_tensor(type_w, type_w, skip_e[:, 2, :].unsqueeze(1).broadcast_to([P, NB, TYPES]), ALU.mult)
            n = 0
            for b in range(NB):
                if b >= 2:
                    dve.wait_ge(t3_written[b % 2], 16)
                for a in range(2):
                    for r in range(0, RELS, 4):
                        dve.wait_ge(rel_done, 2 * n + 2)
                        v.tensor_copy(stage[:, b % 2, r:r + 4, D + a * P:D + (a + 1) * P], PS[:, 4 + n % 2, :].rearrange("p (r w) -> p r w", r=4))\
                            .then_inc(rel_moved_v, 1)
                        n += 1
            for k in range(2):
                dve.wait_ge(q_done, k + 1)
                half_q, half_r = q_f[:, k * BANK:(k + 1) * BANK], q_r[:, k * BANK:(k + 1) * BANK]
                then(v.tensor_copy(half_q, PS[:, 6 + k, :]))
                split([parts3[:, m, 2 * k:2 * k + 2, :].rearrange("p b f -> p (b f)") for m in range(3)], half_q, half_r).then_inc(q_split, 1)
            edge_layer(1)
            denominators((0, 1), 4)
            for b in range(NB):
                ins = v.tensor_tensor(agg[:, b, :].rearrange("p (h f) -> p h f", h=H), PS[:, 4 + b, 4:W1].rearrange("p (h f) -> p h f", h=H),
                                      rden[:, b, :].unsqueeze(2).broadcast_to([P, H, DK]), ALU.mult)
            ins.then_inc(agg_ready, 1)
            added = 0
            for b in range(NB + 1):
                def own_type(t, after):
                    if b == NB:
                        return after
                    if t % 2 == 0:
                        dve.wait_ge(o_done, 2 * b + t // 2 + 1)
                    if t > 0:
                        dve.wait_ge(dve_step, after)
                    return signal(v.scalar_tensor_tensor(x[:, b, :], PS[:, 2 * b + t // 2, (t % 2) * D:(t % 2 + 1) * D], type_w[:, b, t:t + 1],
                                                         x[:, b, :], ALU.mult, ALU.add))

                n = b - 1
                now = own_type(0, 0)
                if n >= 0:
                    dve.wait_ge(dve_step, added)
                    step_n = signal(v.bn_stats(stats[:, n, :], x[:, n, :]))
                now = own_type(1, now)
                if n >= 0:
                    dve.wait_ge(dve_step, step_n)
                    then(v.bn_aggr(mv[:, n, :], stats[:, n, :]))
                    v.tensor_scalar(small[:, 60 + n:61 + n], mv[:, n, 1:2], EPS, None, ALU.add).then_inc(var_ready, 1)
                now = own_type(2, now)
                if n >= 0:
                    dve.wait_ge(std_ready, 4 + n)
                    step_n = signal(v.reciprocal(small[:, 68 + n:69 + n], small[:, 64 + n:65 + n]))
                added = own_type(3, now)
                if n >= 0:
                    dve.wait_ge(dve_step, step_n)
                    v.tensor_scalar(x[:, n, :], x[:, n, :], mv[:, n, 0:1], small[:, 68 + n:69 + n], ALU.subtract, ALU.mult).then_inc(x_ready, 1)


_INS = ['x', 'src', 'dst', 'edge_type_8', 'edge_weight', 'node_type_4', 'L0_gnn_W', 'L0_gnn_B', 'L1_gnn_W', 'L1_gnn_a_self',
        'L1_gnn_a_neigh', 'L1_gnn_bias', 'L2_gnn_W', 'L2_gnn_a', 'L3_gnn_k_linears', 'L3_gnn_q_linears', 'L3_gnn_v_linears',
        'L3_gnn_a_linears', 'L3_gnn_relation_att', 'L3_gnn_relation_msg', 'L3_gnn_relation_pri', 'L3_gnn_skip']


def kernel(**inputs):
    import numpy as _np
    import concourse.bacc as _bacc
    from concourse import mybir as _mybir
    from concourse.bass_utils import run_bass_kernel_spmd as _run

    nc = _bacc.Bacc("TRN2", target_bir_lowering=False, num_devices=1)
    arrays, args = {}, []
    for name in _INS:
        a = _np.ascontiguousarray(inputs[name])
        arrays[f"in_{name}_dram"] = a
        args.append(nc.dram_tensor(f"in_{name}_dram", a.shape, _mybir.dt.from_np(a.dtype), kind="ExternalInput").ap())
    args.append(nc.dram_tensor("out_0_dram", (N, D), _mybir.dt.float32, kind="ExternalOutput").ap())
    gnn_kernel(nc, *args)
    r = _run(nc, [arrays], core_ids=[0])
    return r.results[0]["out_0_dram"]
```
